# Optimizing a Trainium2 kernel written in Bass

```python
import numpy as np
import jax
import jax.numpy as jnp

def _softmax(x, axis=-1):
    return jax.nn.softmax(x, axis=axis)

def _gelu(x):
    return jax.nn.gelu(x, approximate=True)

def _silu(x):
    return jax.nn.silu(x)

def _sigmoid(x):
    return jax.nn.sigmoid(x)

def _layernorm(x, axis=-1, eps=1e-05):
    m = jnp.mean(x, axis=axis, keepdims=True)
    v = jnp.var(x, axis=axis, keepdims=True)
    return (x - m) / jnp.sqrt(v + eps)

def _scatter_add(tgt, idx, src, axis=0):
    return tgt.at[idx].add(src)

def _segment_sum(src, seg, n):
    return jax.ops.segment_sum(src, seg, n)
kernel_name = 'mk_hybrid_d2_jaxref_r8_86ac23'

def setup_inputs(seed: int=0):
    np.random.seed(seed)
    _w = jnp.asarray

    def _L0_attn_a_setup():
        import jax, jax.numpy as jnp
        import numpy as np
        import math
        B, T, D = (4, 512, 128)
        H, DK, DV, C = (8, 128, 128, 64)

        def _rms_norm(x, eps=1e-06):
            return x * jax.lax.rsqrt(jnp.mean(x * x, axis=-1, keepdims=True) + eps)
        key = jax.random.key(seed)
        ks = jax.random.split(key, 7)
        s = 0.02
        return {'x': jax.random.normal(ks[0], (B, T, D), jnp.float32), 'Wq': jax.random.normal(ks[1], (H * DK, D), jnp.float32) * s, 'Wk': jax.random.normal(ks[2], (H * DK, D), jnp.float32) * s, 'Wv': jax.random.normal(ks[3], (H * DV, D), jnp.float32) * s, 'Wg': jax.random.normal(ks[4], (H, D), jnp.float32) * s, 'bg': jnp.full((H,), 3.0, jnp.float32), 'Wo': jax.random.normal(ks[5], (D, H * DV), jnp.float32) * s, 'qk_gain': jnp.asarray(4.0, jnp.float32)}
    _L0_attn_a_in = _L0_attn_a_setup()

    def _L0_attn_b_setup():
        import jax, jax.numpy as jnp
        import numpy as np
        D = 128
        H = 16
        KVH = 4
        HD = D // H
        LAT = 32
        WIN = 32
        B, S = (1, 256)
        BASE_G, BASE_L = (1000000.0, 10000.0)
        EPS = 1e-06

        def rmsnorm(x, w):
            return x * jax.lax.rsqrt(jnp.mean(x * x, axis=-1, keepdims=True) + EPS) * w

        def qk_norm(x):
            return x * jax.lax.rsqrt(jnp.mean(x * x, axis=-1, keepdims=True) + EPS)

        def rope(x, base):
            s, hd = (x.shape[-2], x.shape[-1])
            inv_freq = 1.0 / base ** (jnp.arange(0, hd, 2, dtype=jnp.float32) / hd)
            freqs = jnp.arange(s, dtype=jnp.float32)[:, None] * inv_freq[None, :]
            cos, sin = (jnp.cos(freqs), jnp.sin(freqs))
            xe, xo = (x[..., ::2], x[..., 1::2])
            out = jnp.stack([xe * cos - xo * sin, xe * sin + xo * cos], axis=-1)
            return out.reshape(x.shape)

        def split_heads(x, n_heads):
            b, s, _ = x.shape
            return x.reshape(b, s, n_heads, HD).transpose(0, 2, 1, 3)

        def repeat_kv(x):
            return jnp.repeat(x, H // KVH, axis=1)

        def sdpa(q, k, v, mask):
            scores = jnp.einsum('bhqd,bhkd->bhqk', q, k) / np.sqrt(HD).astype(np.float32)
            scores = jnp.where(mask, scores, jnp.float32(-1e+30))
            probs = jax.nn.softmax(scores, axis=-1)
            return jnp.einsum('bhqk,bhkd->bhqd', probs, v)

        def merge_heads(x):
            b, h, s, hd = x.shape
            return x.transpose(0, 2, 1, 3).reshape(b, s, h * hd)

        def global_latent_attn(x, wq, w_kv_down, w_k_up, w_v_up, wo):
            q = split_heads(x @ wq, H)
            latent = x @ w_kv_down
            k = split_heads(latent @ w_k_up, KVH)
            v = split_heads(latent @ w_v_up, KVH)
            q, k = (rope(q, BASE_G), rope(k, BASE_G))
            q, k = (qk_norm(q), qk_norm(k))
            k, v = (repeat_kv(k), repeat_kv(v))
            i = jnp.arange(x.shape[1])
            causal = i[:, None] >= i[None, :]
            return merge_heads(sdpa(q, k, v, causal)) @ wo

        def local_gqa_attn(x, wq, wk, wv, wo):
            q = split_heads(x @ wq, H)
            k = split_heads(x @ wk, KVH)
            v = split_heads(x @ wv, KVH)
            q, k = (rope(q, BASE_L), rope(k, BASE_L))
            q, k = (qk_norm(q), qk_norm(k))
            k, v = (repeat_kv(k), repeat_kv(v))
            i = jnp.arange(x.shape[1])
            diff = i[:, None] - i[None, :]
            mask = (diff >= 0) & (diff < WIN)
            return merge_heads(sdpa(q, k, v, mask)) @ wo
        key = jax.random.key(seed)
        ks = jax.random.split(key, 12)
        std = 0.02
        return {'hidden': jax.random.normal(ks[0], (B, S, D), dtype=jnp.float32), 'norm1_w': jnp.ones((D,), jnp.float32), 'norm2_w': jnp.ones((D,), jnp.float32), 'g_wq': jax.random.normal(ks[1], (D, H * HD), jnp.float32) * std, 'g_kv_down': jax.random.normal(ks[2], (D, LAT), jnp.float32) * std, 'g_k_up': jax.random.normal(ks[3], (LAT, KVH * HD), jnp.float32) * std, 'g_v_up': jax.random.normal(ks[4], (LAT, KVH * HD), jnp.float32) * std, 'g_wo': jax.random.normal(ks[5], (D, D), jnp.float32) * std, 'l_wq': jax.random.normal(ks[6], (D, H * HD), jnp.float32) * std, 'l_wk': jax.random.normal(ks[7], (D, KVH * HD), jnp.float32) * std, 'l_wv': jax.random.normal(ks[8], (D, KVH * HD), jnp.float32) * std, 'l_wo': jax.random.normal(ks[9], (D, D), jnp.float32) * std}
    _L0_attn_b_in = _L0_attn_b_setup()

    def _L0_ffn_setup():
        import jax, jax.numpy as jnp
        import numpy as np
        DIM = 128
        DEPTH = 2
        HEADS = 8
        DIM_HEAD = 64
        WINDOW = 64
        INNER = HEADS * DIM_HEAD
        HID = int(DIM * 4 * 2 / 3)
        B, N = (2, 1024)
        QK_SCALE = 8.0

        def shift_token(t):
            t1, t2 = jnp.split(t, 2, axis=-1)
            t2 = jnp.pad(t2, ((0, 0), (1, 0), (0, 0)))[:, :-1]
            return jnp.concatenate([t1, t2], axis=-1)

        def l2norm(t):
            return t / jnp.clip(jnp.linalg.norm(t, axis=-1, keepdims=True), 1e-12)

        def rotate_half(x):
            x1, x2 = jnp.split(x, 2, axis=-1)
            return jnp.concatenate([-x2, x1], axis=-1)

        def rotary_xpos(q, k):
            n = q.shape[-2]
            half_idx = jnp.arange(0, DIM_HEAD, 2, dtype=jnp.float32)
            inv_freq = 1.0 / 10000.0 ** (half_idx / DIM_HEAD)
            t = jnp.arange(n, dtype=jnp.float32)
            freqs = t[:, None] * inv_freq[None, :]
            freqs = jnp.concatenate([freqs, freqs], axis=-1)
            base = (half_idx + 0.4 * DIM_HEAD) / (1.4 * DIM_HEAD)
            power = (t - n // 2) / float(WINDOW // 2)
            scale = base[None, :] ** power[:, None]
            scale = jnp.concatenate([scale, scale], axis=-1)
            cos, sin = (jnp.cos(freqs), jnp.sin(freqs))
            q = q * cos * scale + rotate_half(q) * sin * scale
            k = k * cos / scale + rotate_half(k) * sin / scale
            return (q, k)

        def local_attention(q, k, v):
            b, h, n, d = q.shape
            w = n // WINDOW
            bq = q.reshape(b, h, w, WINDOW, d) * QK_SCALE
            bk = k.reshape(b, h, w, WINDOW, d)
            bv = v.reshape(b, h, w, WINDOW, d)

            def look_around(t):
                p = jnp.pad(t, ((0, 0), (0, 0), (1, 0), (0, 0), (0, 0)))
                return jnp.concatenate([p[:, :, :w], p[:, :, 1:]], axis=3)
            bk, bv = (look_around(bk), look_around(bv))
            bt = jnp.arange(n).reshape(w, WINDOW)
            btp = jnp.pad(bt, ((1, 0), (0, 0)), constant_values=-1)
            btk = jnp.concatenate([btp[:w], btp[1:]], axis=1)
            sim = jnp.einsum('bhwid,bhwjd->bhwij', bq, bk)
            i = bt[:, :, None]
            j = btk[:, None, :]
            mask = (i < j) | (i > j + WINDOW) | (j == -1)
            sim = jnp.where(mask, -jnp.finfo(sim.dtype).max, sim)
            attn = jax.nn.softmax(sim, axis=-1)
            out = jnp.einsum('bhwij,bhwjd->bhwid', attn, bv)
            return out.reshape(b, h, n, d)

        def _layer(x, wqkv, qs, ksc, wo, lg, lb, w1, b1, w2, b2):
            b, n, _ = x.shape
            h = shift_token(x)
            qkv = h @ wqkv
            q, k, v = jnp.split(qkv, 3, axis=-1)
            to_heads = lambda t: t.reshape(b, n, HEADS, DIM_HEAD).transpose(0, 2, 1, 3)
            q, k, v = (to_heads(q), to_heads(k), to_heads(v))
            q = l2norm(q) * qs
            k = l2norm(k) * ksc
            q, k = rotary_xpos(q, k)
            o = local_attention(q, k, v)
            o = o.transpose(0, 2, 1, 3).reshape(b, n, INNER)
            x = x + o @ wo
            h = shift_token(x)
            mu = h.mean(-1, keepdims=True)
            var = h.var(-1, keepdims=True)
            h = (h - mu) / jnp.sqrt(var + 1e-05) * lg + lb
            h = h @ w1 + b1
            a, g = jnp.split(h, 2, axis=-1)
            h = a * jax.nn.gelu(g, approximate=False)
            x = x + h @ w2 + b2
            return x
        key = jax.random.key(seed)
        ks = jax.random.split(key, 6)
        return {'x': jax.random.normal(ks[0], (B, N, DIM), jnp.float32), 'wqkv': jax.random.normal(ks[1], (DEPTH, DIM, 3 * INNER), jnp.float32) * 0.02, 'q_scale': jnp.ones((DEPTH, DIM_HEAD), jnp.float32), 'k_scale': jnp.ones((DEPTH, DIM_HEAD), jnp.float32), 'wo': jax.random.normal(ks[2], (DEPTH, INNER, DIM), jnp.float32) * 0.02, 'ln_g': jnp.ones((DEPTH, DIM), jnp.float32), 'ln_b': jnp.zeros((DEPTH, DIM), jnp.float32), 'w1': jax.random.normal(ks[3], (DEPTH, DIM, 2 * HID), jnp.float32) * 0.02, 'b1': jnp.zeros((DEPTH, 2 * HID), jnp.float32), 'w2': jax.random.normal(ks[4], (DEPTH, HID, DIM), jnp.float32) * 0.02, 'b2': jnp.zeros((DEPTH, DIM), jnp.float32)}
    _L0_ffn_in = _L0_ffn_setup()

    def _L1_attn_a_setup():
        import jax, jax.numpy as jnp
        import numpy as np
        import math
        B, S, DM, H = (4, 512, 128, 16)
        HD = DM // H
        key = jax.random.key(seed)
        ks = jax.random.split(key, 5)

        def xavier(k, shape):
            bound = math.sqrt(6.0 / (shape[0] + shape[1]))
            return jax.random.uniform(k, shape, jnp.float32, -bound, bound)
        return {'x': jax.random.normal(ks[0], (B, S, DM), jnp.float32), 'Wq': xavier(ks[1], (DM, DM)), 'Wk': xavier(ks[2], (DM, DM)), 'Wv': xavier(ks[3], (DM, DM)), 'Wfc': xavier(ks[4], (DM, DM))}
    _L1_attn_a_in = _L1_attn_a_setup()

    def _L1_attn_b_setup():
        import jax, jax.numpy as jnp
        import numpy as np
        DIM = 128
        DIM_HEAD = 64
        HEADS = DIM // DIM_HEAD
        B, N = (2, 256)
        LN_EPS = 1e-05
        RMS_EPS = 1e-08

        def _rmsnorm(x, gamma):
            d = x.shape[-1]
            norm = jnp.linalg.norm(x, axis=-1, keepdims=True) * d ** (-0.5)
            return x / jnp.maximum(norm, RMS_EPS) * gamma

        def _layernorm(x, gamma, beta):
            mu = jnp.mean(x, axis=-1, keepdims=True)
            var = jnp.var(x, axis=-1, keepdims=True)
            return (x - mu) * jax.lax.rsqrt(var + LN_EPS) * gamma + beta
        key = jax.random.key(seed)
        ks = jax.random.split(key, 8)
        s = DIM ** (-0.5)
        return {'x': jax.random.normal(ks[0], (B, N, DIM), dtype=jnp.float32), 'ln_gamma': jnp.ones((DIM,), jnp.float32), 'ln_beta': jnp.zeros((DIM,), jnp.float32), 'q_gamma': jnp.ones((DIM_HEAD,), jnp.float32), 'k_gamma': jnp.ones((DIM_HEAD,), jnp.float32), 'w_q': jax.random.normal(ks[1], (DIM, DIM), jnp.float32) * s, 'w_k': jax.random.normal(ks[2], (DIM, DIM), jnp.float32) * s, 'w_v': jax.random.normal(ks[3], (DIM, DIM), jnp.float32) * s, 'w_o': jax.random.normal(ks[4], (DIM, DIM), jnp.float32) * s, 'b_o': jnp.zeros((DIM,), jnp.float32)}
    _L1_attn_b_in = _L1_attn_b_setup()

    def _L1_ffn_setup():
        import jax, jax.numpy as jnp
        import numpy as np
        B, S, D, E = (2, 512, 128, 8)
        key = jax.random.key(seed)
        ks = jax.random.split(key, 7)
        s = 1.0 / np.sqrt(D)
        return {'x': jax.random.normal(ks[0], (B, S, D), jnp.float32), 'Ws': jax.random.normal(ks[1], (E, D), jnp.float32) * s, 'bs': jax.random.normal(ks[2], (E,), jnp.float32) * s, 'W1': jax.random.normal(ks[3], (E, D, D), jnp.float32) * s, 'b1': jax.random.normal(ks[4], (E, D), jnp.float32) * s, 'W2': jax.random.normal(ks[5], (E, D, D), jnp.float32) * s, 'b2': jax.random.normal(ks[6], (E, D), jnp.float32) * s}
    _L1_ffn_in = _L1_ffn_setup()
    _d = {'L0_attn_a_x': _L0_attn_a_in['x'], 'L0_attn_a_Wq': _L0_attn_a_in['Wq'], 'L0_attn_a_Wk': _L0_attn_a_in['Wk'], 'L0_attn_a_Wv': _L0_attn_a_in['Wv'], 'L0_attn_a_Wg': _L0_attn_a_in['Wg'], 'L0_attn_a_bg': _L0_attn_a_in['bg'], 'L0_attn_a_Wo': _L0_attn_a_in['Wo'], 'L0_attn_a_qk_gain': _L0_attn_a_in['qk_gain'], 'L0_attn_b_norm1_w': _L0_attn_b_in['norm1_w'], 'L0_attn_b_norm2_w': _L0_attn_b_in['norm2_w'], 'L0_attn_b_g_wq': _L0_attn_b_in['g_wq'], 'L0_attn_b_g_kv_down': _L0_attn_b_in['g_kv_down'], 'L0_attn_b_g_k_up': _L0_attn_b_in['g_k_up'], 'L0_attn_b_g_v_up': _L0_attn_b_in['g_v_up'], 'L0_attn_b_g_wo': _L0_attn_b_in['g_wo'], 'L0_attn_b_l_wq': _L0_attn_b_in['l_wq'], 'L0_attn_b_l_wk': _L0_attn_b_in['l_wk'], 'L0_attn_b_l_wv': _L0_attn_b_in['l_wv'], 'L0_attn_b_l_wo': _L0_attn_b_in['l_wo'], 'L0_ffn_wqkv': _L0_ffn_in['wqkv'], 'L0_ffn_q_scale': _L0_ffn_in['q_scale'], 'L0_ffn_k_scale': _L0_ffn_in['k_scale'], 'L0_ffn_wo': _L0_ffn_in['wo'], 'L0_ffn_ln_g': _L0_ffn_in['ln_g'], 'L0_ffn_ln_b': _L0_ffn_in['ln_b'], 'L0_ffn_w1': _L0_ffn_in['w1'], 'L0_ffn_b1': _L0_ffn_in['b1'], 'L0_ffn_w2': _L0_ffn_in['w2'], 'L0_ffn_b2': _L0_ffn_in['b2'], 'L1_attn_a_Wq': _L1_attn_a_in['Wq'], 'L1_attn_a_Wk': _L1_attn_a_in['Wk'], 'L1_attn_a_Wv': _L1_attn_a_in['Wv'], 'L1_attn_a_Wfc': _L1_attn_a_in['Wfc'], 'L1_attn_b_ln_gamma': _L1_attn_b_in['ln_gamma'], 'L1_attn_b_ln_beta': _L1_attn_b_in['ln_beta'], 'L1_attn_b_q_gamma': _L1_attn_b_in['q_gamma'], 'L1_attn_b_k_gamma': _L1_attn_b_in['k_gamma'], 'L1_attn_b_w_q': _L1_attn_b_in['w_q'], 'L1_attn_b_w_k': _L1_attn_b_in['w_k'], 'L1_attn_b_w_v': _L1_attn_b_in['w_v'], 'L1_attn_b_w_o': _L1_attn_b_in['w_o'], 'L1_attn_b_b_o': _L1_attn_b_in['b_o'], 'L1_ffn_Ws': _L1_ffn_in['Ws'], 'L1_ffn_bs': _L1_ffn_in['bs'], 'L1_ffn_W1': _L1_ffn_in['W1'], 'L1_ffn_b1': _L1_ffn_in['b1'], 'L1_ffn_W2': _L1_ffn_in['W2'], 'L1_ffn_b2': _L1_ffn_in['b2']}
    _x0 = _d['L0_attn_a_x']
    _d['L0_attn_a_x'] = jax.random.normal(jax.random.fold_in(jax.random.key(seed), 1), (4, 512, 128), dtype=_x0.dtype)
    del _x0
    return _d

def reference(L0_attn_a_x, L0_attn_a_Wq, L0_attn_a_Wk, L0_attn_a_Wv, L0_attn_a_Wg, L0_attn_a_bg, L0_attn_a_Wo, L0_attn_a_qk_gain, L0_attn_b_norm1_w, L0_attn_b_norm2_w, L0_attn_b_g_wq, L0_attn_b_g_kv_down, L0_attn_b_g_k_up, L0_attn_b_g_v_up, L0_attn_b_g_wo, L0_attn_b_l_wq, L0_attn_b_l_wk, L0_attn_b_l_wv, L0_attn_b_l_wo, L0_ffn_wqkv, L0_ffn_q_scale, L0_ffn_k_scale, L0_ffn_wo, L0_ffn_ln_g, L0_ffn_ln_b, L0_ffn_w1, L0_ffn_b1, L0_ffn_w2, L0_ffn_b2, L1_attn_a_Wq, L1_attn_a_Wk, L1_attn_a_Wv, L1_attn_a_Wfc, L1_attn_b_ln_gamma, L1_attn_b_ln_beta, L1_attn_b_q_gamma, L1_attn_b_k_gamma, L1_attn_b_w_q, L1_attn_b_w_k, L1_attn_b_w_v, L1_attn_b_w_o, L1_attn_b_b_o, L1_ffn_Ws, L1_ffn_bs, L1_ffn_W1, L1_ffn_b1, L1_ffn_W2, L1_ffn_b2):

    def _L0_attn_a_ref(x, Wq, Wk, Wv, Wg, bg, Wo, qk_gain):
        import jax, jax.numpy as jnp
        import numpy as np
        import math
        B, T, D = (4, 512, 128)
        H, DK, DV, C = (8, 128, 128, 64)

        def _rms_norm(x, eps=1e-06):
            return x * jax.lax.rsqrt(jnp.mean(x * x, axis=-1, keepdims=True) + eps)
        Bs, Ts, Ds = x.shape
        pad = (C - Ts % C) % C
        if pad:
            x = jnp.pad(x, ((0, 0), (0, pad), (0, 0)))
        Tp = x.shape[1]
        n = Tp // C
        q = (x @ Wq.T).reshape(Bs, Tp, H, DK).transpose(0, 2, 1, 3)
        k = (x @ Wk.T).reshape(Bs, Tp, H, DK).transpose(0, 2, 1, 3)
        v = (x @ Wv.T).reshape(Bs, Tp, H, DV).transpose(0, 2, 1, 3)
        g = jax.nn.sigmoid(x @ Wg.T + bg).transpose(0, 2, 1)
        q = _rms_norm(q) * qk_gain
        k = _rms_norm(k)
        q = q.reshape(Bs, H, n, C, DK)
        k = k.reshape(Bs, H, n, C, DK)
        v = v.reshape(Bs, H, n, C, DV)
        g = g.reshape(Bs, H, n, C)
        mask = jnp.tril(jnp.ones((C, C), bool))
        scores = jnp.einsum('bhntd,bhnsd->bhnts', q, k) / math.sqrt(DK)
        scores = jnp.where(mask, scores, -jnp.inf)
        attn = jax.nn.softmax(scores, axis=-1)
        y_in = jnp.einsum('bhnts,bhnsd->bhntd', attn, v)
        kv = jnp.einsum('bhntd,bhnte->bhnde', k, v)
        gamma = jnp.exp(jnp.sum(jnp.log(g), axis=-1))
        qs = jnp.moveaxis(q, 2, 0)
        kvs = jnp.moveaxis(kv, 2, 0)
        gs = jnp.moveaxis(gamma, 2, 0)

        def step(state, inp):
            qn, kvn, gn = inp
            yc = jnp.einsum('bhtd,bhde->bhte', qn, state)
            new_state = state * gn[:, :, None, None] + kvn
            return (new_state, yc)
        state0 = jnp.zeros((Bs, H, DK, DV), x.dtype)
        _, ycs = jax.lax.scan(step, state0, (qs, kvs, gs))
        y_cross = jnp.moveaxis(ycs, 0, 2)
        y = (y_in + y_cross).reshape(Bs, H, Tp, DV).transpose(0, 2, 1, 3).reshape(Bs, Tp, H * DV)
        y = y @ Wo.T
        if pad:
            y = y[:, :Ts, :]
        return y

    def _L0_attn_b_ref(hidden, norm1_w, norm2_w, g_wq, g_kv_down, g_k_up, g_v_up, g_wo, l_wq, l_wk, l_wv, l_wo):
        import jax, jax.numpy as jnp
        import numpy as np
        D = 128
        H = 16
        KVH = 4
        HD = D // H
        LAT = 32
        WIN = 32
        B, S = (1, 256)
        BASE_G, BASE_L = (1000000.0, 10000.0)
        EPS = 1e-06

        def rmsnorm(x, w):
            return x * jax.lax.rsqrt(jnp.mean(x * x, axis=-1, keepdims=True) + EPS) * w

        def qk_norm(x):
            return x * jax.lax.rsqrt(jnp.mean(x * x, axis=-1, keepdims=True) + EPS)

        def rope(x, base):
            s, hd = (x.shape[-2], x.shape[-1])
            inv_freq = 1.0 / base ** (jnp.arange(0, hd, 2, dtype=jnp.float32) / hd)
            freqs = jnp.arange(s, dtype=jnp.float32)[:, None] * inv_freq[None, :]
            cos, sin = (jnp.cos(freqs), jnp.sin(freqs))
            xe, xo = (x[..., ::2], x[..., 1::2])
            out = jnp.stack([xe * cos - xo * sin, xe * sin + xo * cos], axis=-1)
            return out.reshape(x.shape)

        def split_heads(x, n_heads):
            b, s, _ = x.shape
            return x.reshape(b, s, n_heads, HD).transpose(0, 2, 1, 3)

        def repeat_kv(x):
            return jnp.repeat(x, H // KVH, axis=1)

        def sdpa(q, k, v, mask):
            scores = jnp.einsum('bhqd,bhkd->bhqk', q, k) / np.sqrt(HD).astype(np.float32)
            scores = jnp.where(mask, scores, jnp.float32(-1e+30))
            probs = jax.nn.softmax(scores, axis=-1)
            return jnp.einsum('bhqk,bhkd->bhqd', probs, v)

        def merge_heads(x):
            b, h, s, hd = x.shape
            return x.transpose(0, 2, 1, 3).reshape(b, s, h * hd)

        def global_latent_attn(x, wq, w_kv_down, w_k_up, w_v_up, wo):
            q = split_heads(x @ wq, H)
            latent = x @ w_kv_down
            k = split_heads(latent @ w_k_up, KVH)
            v = split_heads(latent @ w_v_up, KVH)
            q, k = (rope(q, BASE_G), rope(k, BASE_G))
            q, k = (qk_norm(q), qk_norm(k))
            k, v = (repeat_kv(k), repeat_kv(v))
            i = jnp.arange(x.shape[1])
            causal = i[:, None] >= i[None, :]
            return merge_heads(sdpa(q, k, v, causal)) @ wo

        def local_gqa_attn(x, wq, wk, wv, wo):
            q = split_heads(x @ wq, H)
            k = split_heads(x @ wk, KVH)
            v = split_heads(x @ wv, KVH)
            q, k = (rope(q, BASE_L), rope(k, BASE_L))
            q, k = (qk_norm(q), qk_norm(k))
            k, v = (repeat_kv(k), repeat_kv(v))
            i = jnp.arange(x.shape[1])
            diff = i[:, None] - i[None, :]
            mask = (diff >= 0) & (diff < WIN)
            return merge_heads(sdpa(q, k, v, mask)) @ wo
        x = hidden
        x = x + global_latent_attn(rmsnorm(x, norm1_w), g_wq, g_kv_down, g_k_up, g_v_up, g_wo)
        x = x + local_gqa_attn(rmsnorm(x, norm2_w), l_wq, l_wk, l_wv, l_wo)
        return x

    def _L0_ffn_ref(x, wqkv, q_scale, k_scale, wo, ln_g, ln_b, w1, b1, w2, b2):
        import jax, jax.numpy as jnp
        import numpy as np
        DIM = 128
        DEPTH = 2
        HEADS = 8
        DIM_HEAD = 64
        WINDOW = 64
        INNER = HEADS * DIM_HEAD
        HID = int(DIM * 4 * 2 / 3)
        B, N = (2, 1024)
        QK_SCALE = 8.0

        def shift_token(t):
            t1, t2 = jnp.split(t, 2, axis=-1)
            t2 = jnp.pad(t2, ((0, 0), (1, 0), (0, 0)))[:, :-1]
            return jnp.concatenate([t1, t2], axis=-1)

        def l2norm(t):
            return t / jnp.clip(jnp.linalg.norm(t, axis=-1, keepdims=True), 1e-12)

        def rotate_half(x):
            x1, x2 = jnp.split(x, 2, axis=-1)
            return jnp.concatenate([-x2, x1], axis=-1)

        def rotary_xpos(q, k):
            n = q.shape[-2]
            half_idx = jnp.arange(0, DIM_HEAD, 2, dtype=jnp.float32)
            inv_freq = 1.0 / 10000.0 ** (half_idx / DIM_HEAD)
            t = jnp.arange(n, dtype=jnp.float32)
            freqs = t[:, None] * inv_freq[None, :]
            freqs = jnp.concatenate([freqs, freqs], axis=-1)
            base = (half_idx + 0.4 * DIM_HEAD) / (1.4 * DIM_HEAD)
            power = (t - n // 2) / float(WINDOW // 2)
            scale = base[None, :] ** power[:, None]
            scale = jnp.concatenate([scale, scale], axis=-1)
            cos, sin = (jnp.cos(freqs), jnp.sin(freqs))
            q = q * cos * scale + rotate_half(q) * sin * scale
            k = k * cos / scale + rotate_half(k) * sin / scale
            return (q, k)

        def local_attention(q, k, v):
            b, h, n, d = q.shape
            w = n // WINDOW
            bq = q.reshape(b, h, w, WINDOW, d) * QK_SCALE
            bk = k.reshape(b, h, w, WINDOW, d)
            bv = v.reshape(b, h, w, WINDOW, d)

            def look_around(t):
                p = jnp.pad(t, ((0, 0), (0, 0), (1, 0), (0, 0), (0, 0)))
                return jnp.concatenate([p[:, :, :w], p[:, :, 1:]], axis=3)
            bk, bv = (look_around(bk), look_around(bv))
            bt = jnp.arange(n).reshape(w, WINDOW)
            btp = jnp.pad(bt, ((1, 0), (0, 0)), constant_values=-1)
            btk = jnp.concatenate([btp[:w], btp[1:]], axis=1)
            sim = jnp.einsum('bhwid,bhwjd->bhwij', bq, bk)
            i = bt[:, :, None]
            j = btk[:, None, :]
            mask = (i < j) | (i > j + WINDOW) | (j == -1)
            sim = jnp.where(mask, -jnp.finfo(sim.dtype).max, sim)
            attn = jax.nn.softmax(sim, axis=-1)
            out = jnp.einsum('bhwij,bhwjd->bhwid', attn, bv)
            return out.reshape(b, h, n, d)

        def _layer(x, wqkv, qs, ksc, wo, lg, lb, w1, b1, w2, b2):
            b, n, _ = x.shape
            h = shift_token(x)
            qkv = h @ wqkv
            q, k, v = jnp.split(qkv, 3, axis=-1)
            to_heads = lambda t: t.reshape(b, n, HEADS, DIM_HEAD).transpose(0, 2, 1, 3)
            q, k, v = (to_heads(q), to_heads(k), to_heads(v))
            q = l2norm(q) * qs
            k = l2norm(k) * ksc
            q, k = rotary_xpos(q, k)
            o = local_attention(q, k, v)
            o = o.transpose(0, 2, 1, 3).reshape(b, n, INNER)
            x = x + o @ wo
            h = shift_token(x)
            mu = h.mean(-1, keepdims=True)
            var = h.var(-1, keepdims=True)
            h = (h - mu) / jnp.sqrt(var + 1e-05) * lg + lb
            h = h @ w1 + b1
            a, g = jnp.split(h, 2, axis=-1)
            h = a * jax.nn.gelu(g, approximate=False)
            x = x + h @ w2 + b2
            return x
        for l in range(DEPTH):
            x = _layer(x, wqkv[l], q_scale[l], k_scale[l], wo[l], ln_g[l], ln_b[l], w1[l], b1[l], w2[l], b2[l])
        return x

    def _L1_attn_a_ref(x, Wq, Wk, Wv, Wfc):
        import jax, jax.numpy as jnp
        import numpy as np
        import math
        B, S, DM, H = (4, 512, 128, 16)
        HD = DM // H
        b, s, dm = x.shape
        h, hd = (H, dm // H)
        Q = (x @ Wq.T).reshape(b, s, h, hd)
        K = (x @ Wk.T).reshape(b, s, h, hd)
        V = (x @ Wv.T).reshape(b, s, h, hd)
        scores = jnp.einsum('bshd,bstd->bsht', Q, K) / math.sqrt(hd)
        attn = jax.nn.softmax(scores, axis=-1)
        out = jnp.einsum('bsht,bstd->bshd', attn, V).reshape(b, s, dm)
        return out @ Wfc.T

    def _L1_attn_b_ref(x, ln_gamma, ln_beta, q_gamma, k_gamma, w_q, w_k, w_v, w_o, b_o):
        import jax, jax.numpy as jnp
        import numpy as np
        DIM = 128
        DIM_HEAD = 64
        HEADS = DIM // DIM_HEAD
        B, N = (2, 256)
        LN_EPS = 1e-05
        RMS_EPS = 1e-08

        def _rmsnorm(x, gamma):
            d = x.shape[-1]
            norm = jnp.linalg.norm(x, axis=-1, keepdims=True) * d ** (-0.5)
            return x / jnp.maximum(norm, RMS_EPS) * gamma

        def _layernorm(x, gamma, beta):
            mu = jnp.mean(x, axis=-1, keepdims=True)
            var = jnp.var(x, axis=-1, keepdims=True)
            return (x - mu) * jax.lax.rsqrt(var + LN_EPS) * gamma + beta
        h, dh = (HEADS, DIM_HEAD)
        xn = _layernorm(x, ln_gamma, ln_beta)

        def proj(w):
            y = xn @ w.T
            b, n, _ = y.shape
            return y.reshape(b, n, h, dh).transpose(0, 2, 1, 3)
        q = proj(w_q)
        k = proj(w_k)
        v = proj(w_v)
        qn = _rmsnorm(q, q_gamma) * dh ** (-0.5)
        kn = _rmsnorm(k, k_gamma)
        sim = jnp.einsum('bhid,bhjd->bhij', qn, kn)
        attn = jax.nn.softmax(sim, axis=-1)
        out = jnp.einsum('bhij,bhjd->bhid', attn, v)
        b, _, n, _ = out.shape
        out = out.transpose(0, 2, 1, 3).reshape(b, n, h * dh)
        return out @ w_o.T + b_o

    def _L1_ffn_ref(x, Ws, bs, W1, b1, W2, b2):
        import jax, jax.numpy as jnp
        import numpy as np
        B, S, D, E = (2, 512, 128, 8)
        b, s, d = x.shape
        xf = x.reshape(-1, d)
        logits = xf @ Ws.T + bs
        probs = jax.nn.softmax(logits, axis=-1)
        routes = jnp.argmax(probs, axis=-1)
        pmax = jnp.max(probs, axis=-1)
        xf = xf * pmax[:, None]
        perm = jnp.argsort(routes, stable=True)
        xs = xf[perm]
        rs = routes[perm]
        h = jax.nn.relu(jnp.einsum('td,edf->etf', xs, W1) + b1[:, None, :])
        y = jnp.einsum('etf,efd->etd', h, W2) + b2[:, None, :]
        out = y[rs, jnp.arange(rs.shape[0])]
        return out.reshape(b, s, d)
    x = L0_attn_a_x
    x = x + _L0_attn_a_ref(_layernorm(x, axis=-1), L0_attn_a_Wq, L0_attn_a_Wk, L0_attn_a_Wv, L0_attn_a_Wg, L0_attn_a_bg, L0_attn_a_Wo, L0_attn_a_qk_gain)
    x = x + _L0_ffn_ref(_layernorm(x, axis=-1), L0_ffn_wqkv, L0_ffn_q_scale, L0_ffn_k_scale, L0_ffn_wo, L0_ffn_ln_g, L0_ffn_ln_b, L0_ffn_w1, L0_ffn_b1, L0_ffn_w2, L0_ffn_b2)
    x = x + _L0_attn_b_ref(_layernorm(x, axis=-1), L0_attn_b_norm1_w, L0_attn_b_norm2_w, L0_attn_b_g_wq, L0_attn_b_g_kv_down, L0_attn_b_g_k_up, L0_attn_b_g_v_up, L0_attn_b_g_wo, L0_attn_b_l_wq, L0_attn_b_l_wk, L0_attn_b_l_wv, L0_attn_b_l_wo)
    x = x + _L0_ffn_ref(_layernorm(x, axis=-1), L0_ffn_wqkv, L0_ffn_q_scale, L0_ffn_k_scale, L0_ffn_wo, L0_ffn_ln_g, L0_ffn_ln_b, L0_ffn_w1, L0_ffn_b1, L0_ffn_w2, L0_ffn_b2)
    x = x + _L1_attn_a_ref(_layernorm(x, axis=-1), L1_attn_a_Wq, L1_attn_a_Wk, L1_attn_a_Wv, L1_attn_a_Wfc)
    x = x + _L1_ffn_ref(_layernorm(x, axis=-1), L1_ffn_Ws, L1_ffn_bs, L1_ffn_W1, L1_ffn_b1, L1_ffn_W2, L1_ffn_b2)
    x = x + _L1_attn_b_ref(_layernorm(x, axis=-1), L1_attn_b_ln_gamma, L1_attn_b_ln_beta, L1_attn_b_q_gamma, L1_attn_b_k_gamma, L1_attn_b_w_q, L1_attn_b_w_k, L1_attn_b_w_v, L1_attn_b_w_o, L1_attn_b_b_o)
    x = x + _L1_ffn_ref(_layernorm(x, axis=-1), L1_ffn_Ws, L1_ffn_bs, L1_ffn_W1, L1_ffn_b1, L1_ffn_W2, L1_ffn_b2)
    return x

_drawn_inputs = setup_inputs


def setup_inputs(seed=0):
    import zlib

    import numpy as np

    out = dict(_drawn_inputs(seed))
    spreads = {'L0_attn_a_bg': (3.0, 0.2),
     'L0_attn_b_norm1_w': (1.0, 0.6),
     'L0_attn_b_norm2_w': (1.0, 0.6),
     'L0_ffn_q_scale': (1.0, 0.6),
     'L0_ffn_k_scale': (1.0, 0.6),
     'L0_ffn_ln_g': (1.0, 0.6),
     'L0_ffn_ln_b': (0.0, 0.8),
     'L0_ffn_b1': (0.0, 0.8),
     'L0_ffn_b2': (0.0, 0.8),
     'L1_attn_b_ln_gamma': (1.0, 0.6),
     'L1_attn_b_ln_beta': (0.0, 0.8),
     'L1_attn_b_q_gamma': (1.0, 0.6),
     'L1_attn_b_k_gamma': (1.0, 0.6),
     'L1_attn_b_b_o': (0.0, 0.8)}
    factors = {'L0_attn_a_Wg': 8.0,
     'L0_attn_b_g_wq': 8.0,
     'L0_attn_b_g_kv_down': 8.0,
     'L0_attn_b_g_k_up': 8.0,
     'L0_attn_b_g_v_up': 8.0,
     'L0_attn_b_g_wo': 8.0,
     'L0_attn_b_l_wq': 8.0,
     'L0_attn_b_l_wk': 8.0,
     'L0_attn_b_l_wv': 8.0,
     'L0_attn_b_l_wo': 8.0,
     'L0_ffn_wqkv': 8.0,
     'L0_ffn_wo': 8.0,
     'L0_ffn_w1': 8.0,
     'L0_ffn_w2': 8.0,
     'L1_attn_a_Wq': 8.0,
     'L1_attn_a_Wk': 8.0,
     'L1_attn_a_Wv': 7.698,
     'L1_attn_a_Wfc': 7.795,
     'L1_attn_b_w_q': 8.0,
     'L1_attn_b_w_k': 8.0,
     'L1_attn_b_w_v': 8.0,
     'L1_attn_b_w_o': 8.0,
     'L1_ffn_Ws': 8.0,
     'L1_ffn_bs': 8.0,
     'L1_ffn_W1': 8.0,
     'L1_ffn_b1': 8.0,
     'L1_ffn_W2': 7.558,
     'L1_ffn_b2': 8.0}
    for name, (base, spread) in spreads.items():
        noise = np.random.default_rng([zlib.crc32(name.encode()), seed]).standard_normal(out[name].shape)
        drawn = base * np.exp(spread * noise) if base else spread * noise
        out[name] = jnp.asarray(drawn.astype(out[name].dtype))
    for name, factor in factors.items():
        out[name] = (out[name] * factor).astype(out[name].dtype)
    return out
```

```python
from contextlib import ExitStack

import numpy as np

import concourse.bass as bass
from concourse import mybir

STAGES = 8

ALU = mybir.AluOpType
ACT = mybir.ActivationFunctionType
F32 = mybir.dt.float32
U32 = mybir.dt.uint32
AX = mybir.AxisListType.X

P = 128
NB = 4
S = 512
NT = S // P
D = 128
HA, CH = 8, 64
NCH = S // CH
HF, DF = 8, 64
WIN = 64
KW = P + WIN
HID = 341
HID_C = [128, 128, HID - 256]
NG, NR, HD = 4, 4, 8
HB = NG * NR
LW = 32
E = 8
TT = NB * NT
EPS6, EPS5 = 1e-6, 1e-5
NEG = -1e30


def constants():
    f = np.float32
    p = np.arange(P)
    t = {}
    t["ident"] = np.eye(P)
    same = (p[:, None] // CH) == (p[None, :] // CH)
    t["mask_a"] = np.where(same & (p[None, :] <= p[:, None]), 0.0, NEG)
    c = np.arange(KW)
    t["mask_f"] = np.where((c[None, :] >= p[:, None]) & (c[None, :] - WIN <= p[:, None]), 0.0, -1e25)
    t["causal"] = (p[None, :] >= p[:, None]) * 1.0
    q = np.arange(P + LW)
    t["local"] = ((q[None, :] >= p[:, None]) & (q[None, :] < p[:, None] + LW)) * 1.0
    t["shift"] = np.eye(P, k=1)
    t["carry"] = np.zeros((P, P))
    t["carry"][P - 1, 0] = 1.0
    t["half0"] = np.repeat((p < CH)[:, None], P, 1) * 1.0
    t["half1"] = np.repeat((p >= CH)[:, None], P, 1) * 1.0
    t["rows"] = ((p[:, None] % 32) // HD == np.arange(NR)[None, :]) * 1.0
    t["neghalf"] = np.full((P, 80), -0.5)
    t["ones"] = np.ones((P, P))
    t["before"] = (p[:, None] < p[None, :]) * 1.0
    t["iota8"] = np.repeat((np.arange(E) - E)[None, :], P, 0) * 1.0
    half = np.arange(0, DF, 2, dtype=f)
    inv = (f(1) / np.power(10000.0, half.astype(np.float64) / DF).astype(f)).astype(f)
    pos = np.arange(S, dtype=f)
    fr = (pos[:, None] * inv[None, :]).astype(f).astype(np.float64)
    base = ((half + f(0.4 * DF)) / f(1.4 * DF)).astype(f).astype(np.float64)
    power = ((pos - S // 2) / f(WIN // 2)).astype(np.float64)
    sc = base[None, :] ** power[:, None]
    cos, sin = np.cos(fr), np.sin(fr)
    both = lambda a: np.concatenate([a, a], 1)
    sign = lambda a: np.concatenate([a, -a], 1)
    tile = lambda a: a.reshape(NT, P, -1).transpose(1, 0, 2).reshape(P, -1)
    t["cos_q"], t["sin_q"] = tile(both(cos * sc * 8.0)), tile(sign(sin * sc * 8.0))
    t["cos_k"], t["sin_k"] = tile(both(cos / sc)), tile(sign(sin / sc))
    for name, b in (("g", 1e6), ("l", 1e4)):
        iv = (f(1) / np.power(f(b), np.arange(0, HD, 2, dtype=f) / f(HD))).astype(f)
        fq = (pos[:, None] * iv[None, :]).astype(f).astype(np.float64)
        t["cos_" + name], t["sin_" + name] = tile(np.cos(fq)), tile(np.sin(fq))
    return {k: np.ascontiguousarray(v, dtype=f) for k, v in t.items()}


def places(blocks):
    at, out = 0, {}
    for name, w in blocks:
        out[name] = (at, w)
        at += w
    return out, at


WEIGHTS = [("a_qkv", 3072), ("a_wo", 1024), ("a_wg", 8),
           ("f_wqkv", 3072), ("f_wo", 1024), ("f_w1", 2 * 2 * HID), ("f_w2", 2 * 3 * 128),
           ("f_cols", 2 * 8),
           ("b_norm", 2), ("b_gq", 128), ("b_lq", 128), ("b_down", 32), ("b_up", 64), ("b_lkv", 64),
           ("b_gwo", 128), ("b_lwo", 128),
           ("c_qkv", 384), ("c_fc", 128),
           ("d_qkv", 384), ("d_wo", 128), ("d_cols", 4),
           ("e_ws", 8), ("e_w1", 1024), ("e_w2", 1024), ("e_b1", 8), ("e_b2", 128)]
ROWS = [("bg", HA), ("gain", 1), ("qs", 2 * DF), ("ks", 2 * DF), ("b2", 2 * D), ("bo", D), ("bs", E)]


def program(nc, x_in, w_in, c_in, r_in, out, scratch, c_at):
    w_at, w_cols = places(WEIGHTS)
    r_at, r_cols = places(ROWS)
    c_cols = sum(w for _, w in c_at.values())
    with ExitStack() as ctx:
        def sb(name, shape, dt=F32):
            return ctx.enter_context(nc.sbuf_tensor(name, shape, dt))

        Wt, Ct, Rt = sb("weights", [P, w_cols]), sb("consts", [P, c_cols]), sb("rows", [P, r_cols])

        def W(name, a=0, b=None):
            at, w = w_at[name]
            return Wt[:, at + a:at + (w if b is None else b)]

        def C(name, a=0, b=None):
            at, w = c_at[name]
            return Ct[:, at + a:at + (w if b is None else b)]

        def R(name, a=0, b=None):
            at, w = r_at[name]
            return Rt[:, at + a:at + (w if b is None else b)]

        ident = C("ident")
        ps = ctx.enter_context(nc.psum_tensor("ps", [P, 8, 512], F32))

        X = sb("X", [P, TT, D])
        XB = sb("XB", [P, NT, D])
        Y = sb("Y", [P, NT, D])
        stats = sb("stats", [P, TT, 6])
        mv = sb("mv", [P, TT, 2])
        rstd = sb("rstd", [P, 80])
        xT = sb("xT", [P, S])
        tabs = sb("tabs", [P, 2, 4, NT * DF])
        arena = sb("arena", [P, 24576])
        taken = [0]

        def carve(n):
            at = taken[0]
            taken[0] += n
            assert taken[0] <= 24576, taken
            return arena[:, at:at + n]

        a_kn = carve(4096).rearrange("p (j h d) -> p j h d", j=NT, h=HA)
        a_v = carve(4096).rearrange("p (j n) -> p j n", j=NT)
        a_qT = carve(4096).rearrange("p (h t) -> p h t", h=HA)
        a_kT = carve(4096).rearrange("p (h t) -> p h t", h=HA)
        a_union = taken[0]
        a_sqr = carve(2048)
        a_qn = carve(1024).rearrange("p (h d) -> p h d", h=HA)
        taken[0] = a_union
        a_st = carve(2048).rearrange("p (z n d) -> p z n d", z=2, n=NCH)
        a_yT = carve(4096).rearrange("p (h t) -> p h t", h=HA)
        a_sc = sb("a_sc", [P, 2, NT, P])
        a_p = sb("a_p", [P, 2, NT, P])
        a_pT = sb("a_pT", [P, NT, P])
        a_gate = sb("a_gate", [P, 32])
        a_gam = sb("a_gam", [P, 2, NT, HA])
        small = sb("small", [P, 6, 16])
        mxa, nma, rsa, ria = small[:, 0, :], small[:, 1, :], small[:, 2, :], small[:, 3, :]
        taken[0] = 0
        f_v = carve(2048).rearrange("p (j n) -> p j n", j=NT)
        f_sqr = carve(1024)
        f_t1, f_t2, f_t3, f_t4 = carve(512), carve(512), carve(512), carve(512)
        f_qr, f_kr = carve(512), carve(512)
        f_qT = carve(512).rearrange("p (c t) -> p c t", c=4)
        f_kT = carve(2048).rearrange("p (c t) -> p c t", c=4)
        f_sc = carve(8 * KW).rearrange("p (h s) -> p h s", h=HF)
        f_p = carve(8 * 256).rearrange("p (h s) -> p h s", h=HF)
        f_pT = carve(8 * 256).rearrange("p (h s t) -> p h s t", h=HF, s=2)
        f_os = carve(512)
        f_oT = carve(512).rearrange("p (c t) -> p c t", c=4)
        f_h = carve(512).rearrange("p (j d) -> p j d", j=NT)
        f_hnT = carve(512)
        f_gb = carve(3 * 512).rearrange("p (c t) -> p c t", c=3)
        f_hm = carve(3 * 512).rearrange("p (c t) -> p c t", c=3)
        f_hT = sb("f_hT", [P, S])
        f_rn, f_mx, f_nm, f_rs, f_ri = small[:, 0, :], small[:, 1, :], small[:, 2, :], small[:, 3, :], small[:, 4, :]
        taken[0] = 0
        b_sq = carve(4 * 160)
        b_qk = carve(4 * 160).rearrange("p (j h d) -> p j h d", j=NT, h=20)
        b_qr = carve(4 * 160).rearrange("p (j h d) -> p j h d", j=NT, h=20)
        b_t = [carve(4 * 80).rearrange("p (j h d) -> p j h d", j=NT, h=20) for _ in range(4)]
        b_kr = carve(512).rearrange("p (j g r d) -> p j g r d", j=NT, g=NG, r=NR)
        b_latT = carve(512)
        b_qT = carve(512)
        b_kT = carve(2048).rearrange("p (r t) -> p r t", r=NR)
        b_os = carve(512).rearrange("p (j h d) -> p j h d", j=NT, h=HB)
        b_oT = carve(512)
        b_hn = carve(512).rearrange("p (j d) -> p j d", j=NT)
        b_p = carve(2 * 2 * 1280).rearrange("p (z h t) -> p z h t", z=2, h=2)
        b_vx = sb("b_vx", [P, NT, NG, HD + 1])
        b_ri = sb("b_ri", [P, NT, HB])
        taken[0] = 0
        c_qkv = carve(NT * 384).rearrange("p (j n) -> p j n", j=NT)
        c_prod = carve(2048)
        c_mix = carve(2 * 2048).rearrange("p (z n) -> p z n", z=2)
        c_sc = carve(2 * 256).rearrange("p (z h t) -> p z h t", z=2, h=HB)
        c_e = carve(2 * 256).rearrange("p (z h t) -> p z h t", z=2, h=HB)
        c_os = carve(512)
        c_oT = carve(512)
        taken[0] = 0
        m_qT = carve(512)
        m_kT = carve(512)
        m_v = carve(512).rearrange("p (j n) -> p j n", j=NT)
        m_p = carve(2048).rearrange("p (z h s) -> p z h s", z=2, h=2)
        m_pT = carve(1024).rearrange("p (h j t) -> p h j t", h=2, j=NT)
        m_os = carve(512)
        m_oT = carve(512)
        m_sq = carve(1024)
        m_qk = carve(1024).rearrange("p (j n) -> p j n", j=NT)
        m_rs = sb("m_rs", [P, NT * 2])
        taken[0] = 0
        e_xl = carve(2048).rearrange("p (i d) -> p i d", i=TT)
        e_xT = carve(2048)
        e_acc = carve(2048).rearrange("p (i d) -> p i d", i=TT)
        e_h = carve(1024).rearrange("p (z t) -> p z t", z=2)
        e_back = carve(2048).rearrange("p (i d) -> p i d", i=TT)
        e_ohT = carve(2048)
        e_small = carve(8 * 128).rearrange("p (k i e) -> p k i e", k=8, i=TT)
        e_lg, e_ex, e_pr, e_oh, e_cand, e_tot, e_pre, e_pos = (e_small[:, k] for k in range(8))
        e_m = carve(6 * 16).rearrange("p (k i) -> p k i", k=6)
        e_eo = carve(8)
        e_idx = sb("e_idx", [P, TT], U32)

        names = """ln_out pow_in pow_out dve_step act_step stage_end xb_in xb_out
            a_xT_ps a_xT a_gate_ps a_gate_in a_decay a_gsum a_gamma a_proj a_sq a_vcopy a_norm
            a_tps a_tcopy a_kv a_state a_scores a_max a_exp a_prob a_pT_ps a_pT_in a_y_ps a_yT_in a_o
            f_yT_ps f_hT_in f_proj f_sq f_vcopy f_rope f_q_ps f_q_in f_k_ps f_k_in f_sc_ps f_max
            f_exp f_pT_ps f_pT_a f_pT_b f_o_ps f_o_in f_oT_ps f_oT_in f_attn f_y f_sh f_h_in f_hnT_ps
            f_hnT_in f_up f_gelu f_mid f_down f_fin f_zero
            b_hn_in b_xT_ps b_hT b_lat_ps b_lat_in b_kvq b_qk_in b_rope b_tps b_qT_in b_kT_in b_s
            b_exp b_mask b_pv b_os_in b_oT_ps b_oT_in b_out b_y
            c_xT_ps c_xT c_proj c_qkv_in c_shift c_exp c_wts c_prod c_red c_os_in c_oT_ps c_oT_in c_out
            m_xT_ps m_xT m_proj m_sq m_qk_in m_tps m_kT_in m_qv_in m_s m_max m_exp m_tp m_pT_a m_pT_b m_pv
            m_os_in m_oT_ps m_oT_in m_out""".split()
        sems = {n: ctx.enter_context(nc.semaphore(n)) for n in names}
        s = type("Sems", (), sems)
        batch_go = ctx.enter_context(nc.semaphore("batch_go"))
        batch_done = ctx.enter_context(nc.semaphore("batch_done"))
        batch_seen = ctx.enter_context(nc.semaphore("batch_seen"))
        s_loaded = ctx.enter_context(nc.semaphore("s_loaded"))
        s_tabs = ctx.enter_context(nc.semaphore("s_tabs"))
        s_store = ctx.enter_context(nc.semaphore("s_store"))
        e_names = """e_ln e_xT_ps e_xT_in e_lg_ps e_shift e_expd e_probs e_rank_ps e_idx_in e_xsT_ps
            e_xsT_in e_oT_ps e_oT_in e_b2_ps e_b2_in e_up e_relu e_down e_acc_in e_sent e_back_in e_out""".split()
        es = type("ESems", (), {n: ctx.enter_context(nc.semaphore(n)) for n in e_names})

        block = ctx.enter_context(nc.Block())

        class Count:
            def __init__(self):
                self.n = 0

            def next(self):
                self.n += 1
                return self.n

        def chain(eng, sem, count):
            def after(ins):
                ins.then_inc(sem, 1)
                eng.wait_ge(sem, count.next())
            return after

        def stage_done(eng, k):
            eng.drain().then_inc(s.stage_end, 1)
            eng.wait_ge(s.stage_end, 4 * k)

        in_loop = ["a", "f", "b", "f", "c"][:min(STAGES, 5)]

        @block.tensor
        def _(pe):
            mm, tr = pe.matmul, pe.transpose

            def transposes(bank, src):
                for j in range(NT):
                    last = tr(ps[:, bank, j * P:(j + 1) * P], src(j), ident)
                return last

            def linear_attention(ln):
                pe.wait_ge(s.ln_out, ln)
                transposes(0, lambda j: Y[:, j, :]).then_inc(s.a_xT_ps, 1)
                pe.wait_ge(s.a_xT, 1)
                for j in range(NT):
                    last = mm(ps[:, 7, j * HA:(j + 1) * HA], xT[:, j * P:(j + 1) * P], W("a_wg"),
                              start=True, stop=True)
                last.then_inc(s.a_gate_ps, 1)

                def project(j):
                    if j >= 1:
                        pe.wait_ge(s.a_norm, j)
                        pe.wait_ge(s.a_vcopy, j)
                    for c in range(6):
                        last = mm(ps[:, c, :], xT[:, j * P:(j + 1) * P], W("a_qkv", 512 * c, 512 * c + 512),
                                  start=True, stop=True)
                    last.then_inc(s.a_proj, 1)

                def turn(j):
                    pe.wait_ge(s.a_norm, j + 1)
                    for g in range(4):
                        T = 4 * j + g
                        if T == 1:
                            pe.wait_ge(s.a_gate_in, 1)
                        if T >= 2:
                            pe.wait_ge(s.a_tcopy, T - 1)
                        for i in range(4):
                            h = 4 * (g % 2) + i
                            src = a_qn[:, h, :] if g < 2 else a_kn[:, j, h, :]
                            last = tr(ps[:, 6 + T % 2, i * P:(i + 1) * P], src, ident)
                        last.then_inc(s.a_tps, 1)

                project(0)
                for j in range(NT):
                    if j + 1 < NT:
                        project(j + 1)
                    turn(j)
                pe.wait_ge(s.a_decay, 1)
                for half in range(2):
                    last = mm(ps[:, 0, 32 * half:32 * half + 32], C("half%d" % half), a_gate[:, :],
                              start=True, stop=True)
                last.then_inc(s.a_gsum, 1)
                pe.wait_ge(s.a_gamma, 1)
                pe.wait_ge(s.a_vcopy, NT)
                pe.wait_ge(s.a_tcopy, 4 * NT)

                def outer(h):
                    if h >= 2:
                        pe.wait_ge(s.a_state, h - 1)
                    for n in range(NCH - 1):
                        j, r = n // 2, n % 2
                        last = mm(ps[:, 2 * (h % 2) + r, j * P:(j + 1) * P],
                                  a_kn[64 * r:64 * r + 64, j, h, :],
                                  a_v[64 * r:64 * r + 64, j, h * P:(h + 1) * P], start=True, stop=True)
                    last.then_inc(s.a_kv, 1)

                def scores(h):
                    if h >= 2:
                        pe.wait_ge(s.a_max, h - 1)
                    for j in range(NT):
                        last = mm(ps[:, 4 + h % 2, j * P:(j + 1) * P], a_qT[:, h, j * P:(j + 1) * P],
                                  a_kT[:, h, j * P:(j + 1) * P], start=True, stop=True)
                    last.then_inc(s.a_scores, 1)

                def turn_probs(h):
                    pe.wait_ge(s.a_prob, h + 1)
                    if h >= 1:
                        pe.wait_ge(s.a_pT_in, h)
                    for j in range(NT):
                        last = tr(ps[:, 6, j * P:(j + 1) * P], a_p[:, h % 2, j, :], ident)
                    last.then_inc(s.a_pT_ps, 1)

                def mix(h):
                    pe.wait_ge(s.a_pT_in, h + 1)
                    pe.wait_ge(s.a_state, h + 1)
                    if h >= 1:
                        pe.wait_ge(s.a_yT_in, h)
                    for j in range(NT):
                        mm(ps[:, 7, j * P:(j + 1) * P], a_v[:, j, h * P:(h + 1) * P], a_pT[:, j, :],
                           start=True, stop=True, skip_group_check=True)
                        for n in (2 * j, 2 * j + 1):
                            if n:
                                last = mm(ps[:, 7, n * CH:(n + 1) * CH], a_st[:, h % 2, n, :],
                                          a_qT[:, h, n * CH:(n + 1) * CH], start=False, stop=True,
                                          skip_group_check=True)
                    last.then_inc(s.a_y_ps, 1)

                for i in range(HA + 1):
                    if i < HA:
                        outer(i)
                        scores(i)
                    if i:
                        turn_probs(i - 1)
                        mix(i - 1)
                pe.wait_ge(s.a_yT_in, HA)
                for j in range(NT):
                    for h in range(HA):
                        last = mm(ps[:, 0, j * P:(j + 1) * P], a_yT[:, h, j * P:(j + 1) * P],
                                  W("a_wo", 128 * h, 128 * h + 128), start=h == 0, stop=h == HA - 1)
                last.then_inc(s.a_o, 1)

            def window_layer(k, l, ln):
                u0 = NT * k
                pe.wait_ge(s.ln_out, ln)
                if l:
                    pe.wait_ge(s.f_fin, k)
                transposes(0, lambda j: Y[:, j, :]).then_inc(s.f_yT_ps, 1)
                pe.wait_ge(s.f_hT_in, k + 1)

                def project(j):
                    u = u0 + j
                    if j:
                        pe.wait_ge(s.f_rope, u)
                        pe.wait_ge(s.f_vcopy, u)
                    for c in range(3):
                        last = mm(ps[:, c, :], f_hT[:, j * P:(j + 1) * P],
                                  W("f_wqkv", 1536 * l + 512 * c, 1536 * l + 512 * c + 512), start=True, stop=True)
                    last.then_inc(s.f_proj, 1)

                def turn_qk(j):
                    u = u0 + j
                    pe.wait_ge(s.f_rope, u + 1)
                    if j:
                        pe.wait_ge(s.f_y, u)
                    for c in range(4):
                        last = tr(ps[:, 3, c * P:(c + 1) * P], f_qr[:, c * P:(c + 1) * P], ident)
                    last.then_inc(s.f_q_ps, 1)
                    pe.wait_ge(s.f_q_in, u + 1)
                    for c in range(4):
                        last = tr(ps[:, 3, c * P:(c + 1) * P], f_kr[:, c * P:(c + 1) * P], ident)
                    last.then_inc(s.f_k_ps, 1)

                def scores(j, g):
                    u = u0 + j
                    pe.wait_ge(s.f_k_in, u + 1)
                    if 2 * u + g >= 1:
                        pe.wait_ge(s.f_max, 2 * u + g)
                    lo = 0 if j else WIN
                    for i in range(4):
                        h = 4 * g + i
                        rows = slice(64 * (h % 2), 64 * (h % 2) + 64)
                        at = KW * (i // 2)
                        last = mm(ps[:, 4 + h % 2, at + lo:at + KW], f_qT[rows, h // 2, :],
                                  f_kT[rows, h // 2, j * P - WIN + lo:(j + 1) * P], start=True, stop=True)
                    last.then_inc(s.f_sc_ps, 1)

                def turn_probs(j, g):
                    n = 2 * (u0 + j) + g
                    pe.wait_ge(s.f_zero, k // 2 + 1)
                    pe.wait_ge(s.f_exp, n + 1)
                    if n:
                        pe.wait_ge(s.f_pT_a, n)
                        pe.wait_ge(s.f_pT_b, n)
                    for i in range(4):
                        for side in ((0, 1) if j else (1,)):
                            last = tr(ps[:, 6 + i // 2, 256 * (i % 2) + 128 * side:256 * (i % 2) + 128 * side + 128],
                                      f_p[:, 4 * g + i, 128 * side:128 * side + 128], ident)
                    last.then_inc(s.f_pT_ps, 1)

                def values(j, g):
                    n = 2 * (u0 + j) + g
                    pe.wait_ge(s.f_pT_a, n + 1)
                    pe.wait_ge(s.f_pT_b, n + 1)
                    for i in range(4):
                        h = 4 * g + i
                        o = ps[:, 3, h * DF:(h + 1) * DF]
                        last = mm(o, f_pT[:, h, 1, :], f_v[:, j, h * DF:(h + 1) * DF], start=True, stop=j == 0)
                        if j:
                            last = mm(o, f_pT[:, h, 0, :], f_v[:, j - 1, h * DF:(h + 1) * DF],
                                      start=False, stop=True)
                    last.then_inc(s.f_o_ps, 1)

                def out_rows(j):
                    u = u0 + j
                    pe.wait_ge(s.f_o_in, u + 1)
                    for c in range(4):
                        last = tr(ps[:, 3, c * P:(c + 1) * P], f_os[:, c * P:(c + 1) * P], ident)
                    last.then_inc(s.f_oT_ps, 1)
                    pe.wait_ge(s.f_oT_in, u + 1)
                    for c in range(4):
                        last = mm(ps[:, 3, 0:D], f_oT[:, c, :], W("f_wo", 512 * l + 128 * c, 512 * l + 128 * c + 128),
                                  start=c == 0, stop=c == 3)
                    last.then_inc(s.f_attn, 1)

                project(0)
                for j in range(NT):
                    if j + 1 < NT:
                        project(j + 1)
                    turn_qk(j)
                    scores(j, 0)
                    scores(j, 1)
                    turn_probs(j, 0)
                    values(j, 0)
                    turn_probs(j, 1)
                    values(j, 1)
                    out_rows(j)
                pe.wait_ge(s.f_y, u0 + NT)
                for j in range(NT):
                    last = mm(ps[:, 0, 64 * j:64 * j + 64], C("shift"), Y[:, j, 64:128], start=True, stop=j == 0)
                    if j:
                        last = mm(ps[:, 0, 64 * j:64 * j + 64], C("carry"), Y[:, j - 1, 64:128],
                                  start=False, stop=True)
                last.then_inc(s.f_sh, 1)
                pe.wait_ge(s.ln_out, ln + 1 + l)
                transposes(1, lambda j: f_h[:, j, :]).then_inc(s.f_hnT_ps, 1)
                pe.wait_ge(s.f_hnT_in, k + 1)
                for c, m in enumerate(HID_C):
                    for a in range(2):
                        at = 2 * HID * l + HID * (1 - a) + 128 * c
                        last = mm(ps[0:m, 2 + 2 * c + a, :], W("f_w1", at, at + m), f_hnT, start=True, stop=True)
                    last.then_inc(s.f_up, 1)
                pe.wait_ge(s.f_mid, 3 * (k + 1))
                for j in range(NT):
                    for c, m in enumerate(HID_C):
                        at = 384 * l + 128 * c
                        last = mm(ps[:, 0, j * P:(j + 1) * P], f_hm[0:m, c, j * P:(j + 1) * P],
                                  W("f_w2", at, at + 128)[0:m, :], start=c == 0, stop=c == 2)
                last.then_inc(s.f_down, 1)

            def small_heads(k):
                glob = k == 0
                pe.wait_ge(s.b_hn_in, k + 1)
                transposes(0, lambda j: b_hn[:, j, :]).then_inc(s.b_xT_ps, 1)
                pe.wait_ge(s.b_hT, k + 1)
                if glob:
                    mm(ps[0:32, 1, :], W("b_down"), xT[:, :], start=True, stop=True).then_inc(s.b_lat_ps, 1)
                    pe.wait_ge(s.b_lat_in, 1)
                for j in range(NT):
                    t = slice(j * P, (j + 1) * P)
                    if glob:
                        mm(ps[:, 2, 64 * j:64 * j + 64], b_latT[0:32, t], W("b_up")[0:32, :], start=True, stop=True)
                    else:
                        mm(ps[:, 2, 64 * j:64 * j + 64], xT[:, t], W("b_lkv"), start=True, stop=True)
                    last = mm(ps[:, 3, t], xT[:, t], W("b_gq" if glob else "b_lq"), start=True, stop=True)
                last.then_inc(s.b_kvq, 1)
                pe.wait_ge(s.b_rope, k + 1)
                transposes(4, lambda j: b_qr[:, j, 0:HB, :].rearrange("p h d -> p (h d)"))
                transposes(5, lambda j: b_kr[:, j].rearrange("p g r d -> p (g r d)")).then_inc(s.b_tps, 1)
                pe.wait_ge(s.b_qT_in, k + 1)
                pe.wait_ge(s.b_kT_in, k + 1)

                def scores(u, j):
                    st = 32 * k + 4 * u + j
                    slot = (4 * u + j) % 3
                    if 4 * u + j >= 3:
                        pe.wait_ge(s.b_exp, st - 2)
                    n = small_width(glob, j)
                    r, gp = u // 2, u % 2
                    for hh in range(2):
                        g = 2 * gp + hh
                        rows = slice(32 * g, 32 * g + 32)
                        last = mm(ps[:, 2 * slot + hh, 0:n], b_kT[rows, r, j * P:(j + 1) * P],
                                  b_qT[rows, j * P:j * P + n], start=True, stop=True)
                    last.then_inc(s.b_s, 1)

                def values(u):
                    pe.wait_ge(s.b_mask, 32 * k + 4 * u + 4)
                    r, gp = u // 2, u % 2
                    for i in range(NT):
                        for hh in range(2):
                            g = 2 * gp + hh
                            at = (i % 2) * 144 + (NR * g + r) * 9
                            src = list(range(i + 1)) if glob else [i] + [i - 1] * (i > 0)
                            for n, j in enumerate(src):
                                o = small_at(glob, j) + (i - j) * P
                                m = P if glob or i == j else LW
                                last = mm(ps[0:m, 6 + i // 2, at:at + 9], b_p[:, u % 2, hh, o:o + m],
                                          b_vx[:, j, g, :], start=n == 0, stop=n == len(src) - 1,
                                          skip_group_check=True)
                    last.then_inc(s.b_pv, 1)

                for u in range(9):
                    for j in range(NT):
                        if u < 8:
                            scores(u, j)
                    if u:
                        values(u - 1)
                pe.wait_ge(s.b_os_in, k + 1)
                transposes(0, lambda j: b_os[:, j].rearrange("p h d -> p (h d)")).then_inc(s.b_oT_ps, 1)
                pe.wait_ge(s.b_oT_in, k + 1)
                for j in range(NT):
                    last = mm(ps[:, 1, j * P:(j + 1) * P], b_oT[:, j * P:(j + 1) * P],
                              W("b_gwo" if glob else "b_lwo"), start=True, stop=True)
                last.then_inc(s.b_out, 1)

            def head_attention(ln):
                pe.wait_ge(s.ln_out, ln)
                transposes(0, lambda j: Y[:, j, :]).then_inc(s.c_xT_ps, 1)
                pe.wait_ge(s.c_xT, 1)
                for j in range(NT):
                    last = mm(ps[:, 1 + j, 0:384], xT[:, j * P:(j + 1) * P], W("c_qkv"), start=True, stop=True)
                last.then_inc(s.c_proj, 1)
                pe.wait_ge(s.c_os_in, 1)
                transposes(0, lambda j: c_os[:, j * P:(j + 1) * P]).then_inc(s.c_oT_ps, 1)
                pe.wait_ge(s.c_oT_in, 1)
                for j in range(NT):
                    last = mm(ps[:, 5, j * P:(j + 1) * P], c_oT[:, j * P:(j + 1) * P], W("c_fc"),
                              start=True, stop=True)
                last.then_inc(s.c_out, 1)

            def full_attention(ln):
                pe.wait_ge(s.ln_out, ln)
                transposes(0, lambda j: Y[:, j, :]).then_inc(s.m_xT_ps, 1)
                pe.wait_ge(s.m_xT, 1)
                for j in range(NT):
                    for c in range(3):
                        last = mm(ps[:, 1 + c, j * P:(j + 1) * P], xT[:, j * P:(j + 1) * P],
                                  W("d_qkv", 128 * c, 128 * c + 128), start=True, stop=True)
                last.then_inc(s.m_proj, 1)
                pe.wait_ge(s.m_qk_in, 1)
                transposes(4, lambda j: m_qk[:, j, 0:128])
                transposes(5, lambda j: m_qk[:, j, 128:256]).then_inc(s.m_tps, 1)
                pe.wait_ge(s.m_qv_in, 1)
                pe.wait_ge(s.m_kT_in, 1)
                steps, dv = full_steps(), DF

                def scores(st):
                    if st >= 2:
                        pe.wait_ge(s.m_exp, st - 1)
                    i, hs = steps[st]
                    for hh, (h, rows) in enumerate(hs):
                        last = mm(ps[:, 2 * (st % 2) + hh, :], m_qT[rows, i * P:(i + 1) * P], m_kT[rows, :],
                                  start=True, stop=True)
                    last.then_inc(s.m_s, 1)

                def turn(st):
                    pe.wait_ge(s.m_exp, st + 1)
                    if st:
                        pe.wait_ge(s.m_pT_a, st)
                        pe.wait_ge(s.m_pT_b, st)
                    for hh in range(2):
                        for j in range(NT):
                            last = tr(ps[:, 4 + hh, j * P:(j + 1) * P], m_p[:, st % 2, hh, j * P:(j + 1) * P], ident)
                    last.then_inc(s.m_tp, 1)

                def values(st):
                    pe.wait_ge(s.m_pT_a, st + 1)
                    pe.wait_ge(s.m_pT_b, st + 1)
                    i, hs = steps[st]
                    for hh, (h, _) in enumerate(hs):
                        for j in range(NT):
                            last = mm(ps[:, 6, i * P + h * dv:i * P + (h + 1) * dv], m_pT[:, hh, j, :],
                                      m_v[:, j, h * dv:(h + 1) * dv], start=j == 0, stop=j == NT - 1)
                    last.then_inc(s.m_pv, 1)

                for st in range(len(steps) + 1):
                    if st < len(steps):
                        scores(st)
                    if st:
                        turn(st - 1)
                        values(st - 1)
                pe.wait_ge(s.m_os_in, 1)
                transposes(0, lambda j: m_os[:, j * P:(j + 1) * P]).then_inc(s.m_oT_ps, 1)
                pe.wait_ge(s.m_oT_in, 1)
                for j in range(NT):
                    last = mm(ps[:, 1, j * P:(j + 1) * P], m_oT[:, j * P:(j + 1) * P], W("d_wo"), start=True, stop=True)
                last.then_inc(s.m_out, 1)

            def experts(k):
                def all_turned(src, ps_sem, in_sem, base):
                    for c in range(NB):
                        if c >= 2:
                            pe.wait_ge(in_sem, base + c - 1)
                        transposes(c % 2, lambda j: src[:, NT * c + j, :]).then_inc(ps_sem, 1)

                pe.wait_ge(es.e_ln, k + 1)
                all_turned(e_xl, es.e_xT_ps, es.e_xT_in, NB * k)
                pe.wait_ge(es.e_xT_in, NB * (k + 1))
                for i in range(TT):
                    last = mm(ps[:, 2, E * i:E * i + E], e_xT[:, i * P:(i + 1) * P], W("e_ws"), start=True, stop=True)
                last.then_inc(es.e_lg_ps, 1)
                pe.wait_ge(es.e_probs, k + 1)
                oh = e_oh.rearrange("p i e -> p (i e)")
                mm(ps[:, 3, 0:128], C("before"), oh, start=True, stop=True)
                mm(ps[:, 3, 128:256], C("ones"), oh, start=True, stop=True).then_inc(es.e_rank_ps, 1)
                all_turned(e_xl, es.e_xsT_ps, es.e_xsT_in, NB * k)
                for c in range(NB):
                    for j in range(NT):
                        last = tr(ps[0:E, 4 + c, j * P:(j + 1) * P], e_oh[:, NT * c + j, :], ident)
                last.then_inc(es.e_oT_ps, 1)
                pe.wait_ge(es.e_oT_in, k + 1)
                for c in range(NB):
                    for j in range(NT):
                        i = NT * c + j
                        last = mm(ps[:, 4 + c, j * P:(j + 1) * P], e_ohT[0:E, i * P:(i + 1) * P],
                                  W("e_b2")[0:E, :], start=True, stop=True)
                last.then_inc(es.e_b2_ps, 1)
                pe.wait_ge(es.e_b2_in, k + 1)
                pe.wait_ge(es.e_xsT_in, NB * (k + 1))
                n = E * NB

                def up(q):
                    e, c = q // NB, q % NB
                    if q >= 2:
                        pe.wait_ge(es.e_relu, n * k + q - 1)
                    mm(ps[:, 4 + q % 2, :], W("e_w1", 128 * e, 128 * e + 128), e_xT[:, c * 512:(c + 1) * 512],
                       start=True, stop=True).then_inc(es.e_up, 1)

                def down(q):
                    e = q // NB
                    pe.wait_ge(es.e_relu, n * k + q + 1)
                    if q >= 2:
                        pe.wait_ge(es.e_acc_in, n * k + q - 1)
                    for j in range(NT):
                        last = mm(ps[:, 6 + q % 2, j * P:(j + 1) * P], e_h[:, q % 2, j * P:(j + 1) * P],
                                  W("e_w2", 128 * e, 128 * e + 128), start=True, stop=True)
                    last.then_inc(es.e_down, 1)

                for q in range(n + 1):
                    if q < n:
                        up(q)
                    if q:
                        down(q - 1)

            def stages(which):
                ln = f = 0
                for i, st in enumerate(which):
                    if st == "a":
                        ln += 1
                        linear_attention(ln)
                    elif st == "f":
                        for l in range(2):
                            window_layer(f, l, ln + 1)
                            f += 1
                        ln += 3
                    elif st == "b":
                        small_heads(0)
                        small_heads(1)
                    elif st == "c":
                        ln += 1
                        head_attention(ln)
                    else:
                        ln += 2
                        full_attention(ln)
                    stage_done(pe, i + 1)

            pe.wait_ge(s_loaded, 64)
            with pe.Fori(0, NB) as b:
                pe.wait_ge(batch_go, b + 1)
                pe.sem_inc(batch_seen, 1)
                stages(in_loop)
                pe.drain().then_inc(batch_done, 1)
            if STAGES >= 6:
                pe.wait_ge(batch_go, NB + 1)
                pe.sem_inc(batch_seen, 1)
                experts(0)
            if STAGES >= 7:
                with pe.Fori(0, NB) as b:
                    pe.wait_ge(batch_go, b + NB + 2)
                    pe.sem_inc(batch_seen, 1)
                    stages(["d"])
                    pe.drain().then_inc(batch_done, 1)
            if STAGES >= 8:
                pe.wait_ge(batch_go, 2 * NB + 2)
                pe.sem_inc(batch_seen, 1)
                experts(1)

        @block.scalar
        def _(act):
            steps_done = Count()
            after = chain(act, s.act_step, steps_done)
            copy = lambda o, i: act.activation(o, i, ACT.Copy)

            def linear_attention():
                act.wait_ge(s.a_xT_ps, 1)
                copy(xT[:, :], ps[:, 0, :]).then_inc(s.a_xT, 1)

                def squares(j):
                    act.wait_ge(s.a_proj, j + 1)
                    act.activation(a_sqr.rearrange("p (b n) -> p b n", b=4), ps[:, 0:4, :], ACT.Square)\
                        .then_inc(s.a_sq, 1)
                    copy(a_v[:, j, :].rearrange("p (b n) -> p b n", b=2), ps[:, 4:6, :]).then_inc(s.a_vcopy, 1)

                act.wait_ge(s.a_gate_in, 1)
                after(act.activation(a_gate[:, :], a_gate[:, :], ACT.Exp, scale=-1.0))
                act.activation(a_gate[:, :], a_gate[:, :], ACT.Ln, bias=1.0).then_inc(s.a_decay, 1)
                squares(0)
                for j in range(NT):
                    if j + 1 < NT:
                        squares(j + 1)
                    for g in range(2):
                        T = 4 * j + g
                        act.wait_ge(s.a_tps, T + 1)
                        if T:
                            act.wait_ge(s.a_tcopy, T)
                        copy(a_qT[:, 4 * g:4 * g + 4, j * P:(j + 1) * P],
                             ps[:, 6 + T % 2, :].rearrange("p (h t) -> p h t", h=4)).then_inc(s.a_tcopy, 1)
                act.wait_ge(s.a_gsum, 1)
                act.activation(a_gam[:, :, :, :],
                               ps[:, 0, 0:64].rearrange("p (z j h) -> p z j h", z=2, j=NT), ACT.Exp, scale=-1.0)\
                    .then_inc(s.a_gamma, 1)
                for i in range(HA + 1):
                    if i < HA:
                        act.wait_ge(s.a_max, i + 1)
                        if i >= 2:
                            act.wait_ge(s.a_pT_ps, i - 1)
                        for j in range(NT):
                            c = 4 * (i % 2) + j
                            last = act.activation(a_p[:, i % 2, j, :], a_sc[:, i % 2, j, :], ACT.Exp,
                                                  bias=nma[:, c:c + 1], scale=float(P) ** -0.5,
                                                  accum_out=rsa[:, c:c + 1])
                        last.then_inc(s.a_exp, 1)
                    if i:
                        h = i - 1
                        act.wait_ge(s.a_pT_ps, h + 1)
                        if h:
                            act.wait_ge(s.a_y_ps, h)
                        copy(a_pT[:, :, :], ps[:, 6, :].rearrange("p (j t) -> p j t", j=NT)).then_inc(s.a_pT_in, 1)
                        act.wait_ge(s.a_y_ps, h + 1)
                        copy(a_yT[:, h, :], ps[:, 7, :]).then_inc(s.a_yT_in, 1)

            def window_layer(k, l):
                u0 = NT * k

                def squares(j):
                    u = u0 + j
                    act.wait_ge(s.f_proj, u + 1)
                    act.activation(f_sqr.rearrange("p (b n) -> p b n", b=2), ps[:, 0:2, :], ACT.Square)\
                        .then_inc(s.f_sq, 1)
                    copy(f_v[:, j, :], ps[:, 2, :]).then_inc(s.f_vcopy, 1)

                squares(0)
                for j in range(NT):
                    u = u0 + j
                    act.wait_ge(s.f_q_ps, u + 1)
                    copy(f_qT, ps[:, 3, :].rearrange("p (c t) -> p c t", c=4)).then_inc(s.f_q_in, 1)
                    act.wait_ge(s.f_k_ps, u + 1)
                    copy(f_kT[:, :, j * P:(j + 1) * P], ps[:, 3, :].rearrange("p (c t) -> p c t", c=4))\
                        .then_inc(s.f_k_in, 1)
                    if j + 1 < NT:
                        squares(j + 1)
                    lo = 0 if j else WIN
                    for g in range(2):
                        act.wait_ge(s.f_max, 2 * u + g + 1)
                        for i in range(4):
                            h = 4 * g + i
                            last = act.activation(f_p[:, h, 64 + lo:256], f_sc[:, h, lo:KW], ACT.Exp,
                                                  bias=f_nm[:, h:h + 1], accum_out=f_rs[:, h:h + 1])
                        last.then_inc(s.f_exp, 1)
                    for g in range(2):
                        act.wait_ge(s.f_pT_ps, 2 * u + g + 1)
                        side = 0 if j else 1
                        copy(f_pT[:, 4 * g:4 * g + 2, side:2, :],
                             ps[:, 6, :].rearrange("p (h s t) -> p h s t", h=2, s=2)[:, :, side:2, :])\
                            .then_inc(s.f_pT_a, 1)
                    act.wait_ge(s.f_oT_ps, u + 1)
                    copy(f_oT, ps[:, 3, :].rearrange("p (c t) -> p c t", c=4)).then_inc(s.f_oT_in, 1)
                act.wait_ge(s.f_sh, k + 1)
                copy(f_h[:, :, 0:64], Y[:, :, 0:64])
                copy(f_h[:, :, 64:128], ps[:, 0, 0:256].rearrange("p (j d) -> p j d", j=NT)).then_inc(s.f_h_in, 1)
                act.wait_ge(s.f_hnT_ps, k + 1)
                act.activation(f_hnT, ps[:, 1, :], ACT.Identity, scale=W("f_cols", 8 * l, 8 * l + 1),
                               bias=W("f_cols", 8 * l + 1, 8 * l + 2)).then_inc(s.f_hnT_in, 1)
                for c, m in enumerate(HID_C):
                    act.wait_ge(s.f_up, 3 * k + c + 1)
                    bias = W("f_cols", 8 * l + 2 + c, 8 * l + 3 + c)
                    act.activation(f_gb[0:m, c, :], ps[0:m, 2 + 2 * c, :], ACT.Gelu, bias=bias[0:m, :])\
                        .then_inc(s.f_gelu, 1)

            def small_heads(k):
                glob = k == 0
                act.wait_ge(s.b_xT_ps, k + 1)
                act.activation(xT[:, :], ps[:, 0, :], ACT.Copy, scale=W("b_norm", k, k + 1)).then_inc(s.b_hT, 1)
                if glob:
                    act.wait_ge(s.b_lat_ps, 1)
                    copy(b_latT[0:32, :], ps[0:32, 1, :]).then_inc(s.b_lat_in, 1)
                act.wait_ge(s.b_kvq, k + 1)
                kv = ps[:, 2, 0:256].rearrange("p (j n) -> p j n", j=NT)
                copy(b_qk[:, :, 0:HB, :], ps[:, 3, :].rearrange("p (j h d) -> p j h d", j=NT, h=HB))
                copy(b_qk[:, :, HB:20, :], kv[:, :, 0:32].rearrange("p j (h d) -> p j h d", h=NG))
                copy(b_vx[:, :, :, 0:HD], kv[:, :, 32:64].rearrange("p j (h d) -> p j h d", h=NG))\
                    .then_inc(s.b_qk_in, 1)
                act.wait_ge(s.b_tps, k + 1)
                copy(b_qT, ps[:, 4, :]).then_inc(s.b_qT_in, 1)
                for u in range(8):
                    if u >= 2:
                        act.wait_ge(s.b_pv, 8 * k + u - 1)
                    for j in range(NT):
                        st = 4 * u + j
                        act.wait_ge(s.b_s, 32 * k + st + 1)
                        n, at = small_width(glob, j), small_at(glob, j)
                        b = 2 * (st % 3)
                        act.activation(b_p[:, u % 2, :, at:at + n], ps[:, b:b + 2, 0:n], ACT.Exp,
                                       scale=float(HD) ** -0.5).then_inc(s.b_exp, 1)
                act.wait_ge(s.b_oT_ps, k + 1)
                copy(b_oT, ps[:, 0, :]).then_inc(s.b_oT_in, 1)

            def head_attention():
                act.wait_ge(s.c_xT_ps, 1)
                copy(xT[:, :], ps[:, 0, :]).then_inc(s.c_xT, 1)
                act.wait_ge(s.c_proj, 1)
                copy(c_qkv, ps[:, 1:1 + NT, 0:384]).then_inc(s.c_qkv_in, 1)
                for j in range(NT):
                    act.wait_ge(s.c_shift, j + 1)
                    if j >= 2:
                        act.wait_ge(s.c_prod, j - 1)
                    act.activation(c_e[:, j % 2], c_sc[:, j % 2], ACT.Exp, scale=float(HD) ** -0.5)\
                        .then_inc(s.c_exp, 1)
                act.wait_ge(s.c_oT_ps, 1)
                copy(c_oT, ps[:, 0, :]).then_inc(s.c_oT_in, 1)

            def full_attention():
                act.wait_ge(s.m_xT_ps, 1)
                act.activation(xT[:, :], ps[:, 0, :], ACT.Identity, scale=W("d_cols", 0, 1),
                               bias=W("d_cols", 1, 2)).then_inc(s.m_xT, 1)
                act.wait_ge(s.m_proj, 1)
                act.activation(m_sq.rearrange("p (b n) -> p b n", b=2), ps[:, 1:3, :], ACT.Square)\
                    .then_inc(s.m_sq, 1)
                copy(m_v, ps[:, 3, :].rearrange("p (j n) -> p j n", j=NT))
                act.wait_ge(s.m_tps, 1)
                act.activation(m_qT, ps[:, 4, :], ACT.Copy, scale=W("d_cols", 2, 3)).then_inc(s.m_qv_in, 1)
                steps, heads = full_steps(), 2
                scale = float(DF) ** -0.5
                for st in range(len(steps) + 1):
                    if st < len(steps):
                        i, hs = steps[st]
                        act.wait_ge(s.m_max, st + 1)
                        for hh, (h, _) in enumerate(hs):
                            c = 2 * (st % 2) + hh
                            last = act.activation(m_p[:, st % 2, hh, :], ps[:, 2 * (st % 2) + hh, :], ACT.Exp,
                                                  bias=nma[:, c:c + 1], scale=scale,
                                                  accum_out=m_rs[:, i * heads + h:i * heads + h + 1])
                        last.then_inc(s.m_exp, 1)
                    if st:
                        act.wait_ge(s.m_tp, st)
                        if st >= 2:
                            act.wait_ge(s.m_pv, st - 1)
                        copy(m_pT[:, 0], ps[:, 4, :].rearrange("p (j t) -> p j t", j=NT)).then_inc(s.m_pT_a, 1)
                act.wait_ge(s.m_oT_ps, 1)
                copy(m_oT, ps[:, 0, :]).then_inc(s.m_oT_in, 1)

            def experts(k):
                for c in range(NB):
                    act.wait_ge(es.e_xT_ps, NB * k + c + 1)
                    copy(e_xT[:, c * 512:(c + 1) * 512], ps[:, c % 2, :]).then_inc(es.e_xT_in, 1)
                act.wait_ge(es.e_shift, k + 1)
                act.activation(e_ex, e_lg, ACT.Exp).then_inc(es.e_expd, 1)
                for c in range(NB):
                    act.wait_ge(es.e_xsT_ps, NB * k + c + 1)
                    copy(e_xT[:, c * 512:(c + 1) * 512], ps[:, c % 2, :]).then_inc(es.e_xsT_in, 1)
                act.wait_ge(es.e_oT_ps, k + 1)
                copy(e_ohT[0:E, :].rearrange("p (b n) -> p b n", b=4), ps[0:E, 4:8, :]).then_inc(es.e_oT_in, 1)
                act.wait_ge(es.e_b2_ps, k + 1)
                copy(e_acc.rearrange("p i d -> p (i d)").rearrange("p (b n) -> p b n", b=4), ps[:, 4:8, :])\
                    .then_inc(es.e_b2_in, 1)
                n = E * NB
                for q in range(n):
                    e = q // NB
                    act.wait_ge(es.e_up, n * k + q + 1)
                    if q >= 2:
                        act.wait_ge(es.e_down, n * k + q - 1)
                    act.activation(e_h[:, q % 2, :], ps[:, 4 + q % 2, :], ACT.Relu, bias=W("e_b1", e, e + 1))\
                        .then_inc(es.e_relu, 1)

            def stages(which):
                f = 0
                for i, st in enumerate(which):
                    if st == "a":
                        linear_attention()
                    elif st == "f":
                        for l in range(2):
                            window_layer(f, l)
                            f += 1
                    elif st == "b":
                        small_heads(0)
                        small_heads(1)
                    elif st == "c":
                        head_attention()
                    else:
                        full_attention()
                    stage_done(act, i + 1)

            act.wait_ge(s_loaded, 64)
            with act.Fori(0, NB) as b:
                act.wait_ge(batch_go, b + 1)
                act.sem_inc(batch_seen, 1)
                steps_done.n = 0
                stages(in_loop)
                act.drain().then_inc(batch_done, 1)
            if STAGES >= 6:
                act.wait_ge(batch_go, NB + 1)
                act.sem_inc(batch_seen, 1)
                experts(0)
            if STAGES >= 7:
                with act.Fori(0, NB) as b:
                    act.wait_ge(batch_go, b + NB + 2)
                    act.sem_inc(batch_seen, 1)
                    stages(["d"])
                    act.drain().then_inc(batch_done, 1)
            if STAGES >= 8:
                act.wait_ge(batch_go, 2 * NB + 2)
                act.sem_inc(batch_seen, 1)
                experts(1)

        @block.vector
        def _(dve):
            steps_done, asked = Count(), Count()
            after = chain(dve, s.dve_step, steps_done)
            tt, ts, stt = dve.tensor_tensor, dve.tensor_scalar, dve.scalar_tensor_tensor

            def root(n, ins):
                ins.then_inc(s.pow_in, 1)
                asked.next()

            def rooted():
                dve.wait_ge(s.pow_out, asked.n)

            def layer_norm(src, dst, n, eps):
                for i in range(n):
                    last = dve.bn_stats(stats[:, i, :], src[:, i, :])
                after(last)
                for i in range(n):
                    last = dve.bn_aggr(mv[:, i, :], stats[:, i, :])
                after(last)
                root(n, ts(rstd[:, 0:n], mv[:, 0:n, 1], eps, None, ALU.add))
                rooted()
                for i in range(n):
                    last = ts(dst[:, i, :], src[:, i, :], mv[:, i, 0:1], rstd[:, i:i + 1], ALU.subtract, ALU.mult)
                return last

            def wide(ap, shape, axis):
                return ap.unsqueeze(axis).broadcast_to(shape)

            def linear_attention():
                layer_norm(XB, Y, NT, EPS5).then_inc(s.ln_out, 1)
                dve.wait_ge(s.a_gate_ps, 1)
                z = a_gate[:, :].rearrange("p (j h) -> p j h", j=NT)
                after(tt(z, ps[:, 7, 0:32].rearrange("p (j h) -> p j h", j=NT), wide(R("bg"), [P, NT, HA], 1), ALU.add))
                ts(a_gate[:, :], a_gate[:, :], -43.0, None, ALU.max).then_inc(s.a_gate_in, 1)

                def normalise(j):
                    dve.wait_ge(s.a_sq, j + 1)
                    if j:
                        dve.wait_ge(s.a_tps, 4 * j - 2)
                    after(dve.tensor_reduce(rstd[:, 0:16], a_sqr.rearrange("p (h d) -> p h d", h=16), AX, ALU.add))
                    root(16, ts(rstd[:, 0:16], rstd[:, 0:16], 1.0 / P, EPS6, ALU.mult, ALU.add))
                    rooted()
                    after(ts(small[:, 4, :], rstd[:, 0:16], 1.0, None, ALU.mult))
                    after(ts(small[:, 4, 0:8], small[:, 4, 0:8], R("gain"), None, ALU.mult))
                    view = lambda a: ps[:, a:a + 2, :].rearrange("p b (h d) -> p (b h) d", d=P)
                    tt(a_qn, view(0), wide(small[:, 4, 0:8], [P, HA, P], 2), ALU.mult)
                    tt(a_kn[:, j], view(2), wide(small[:, 4, 8:16], [P, HA, P], 2), ALU.mult).then_inc(s.a_norm, 1)

                normalise(0)
                for j in range(NT):
                    for g in (2, 3):
                        T = 4 * j + g
                        dve.wait_ge(s.a_tps, T + 1)
                        dve.wait_ge(s.a_tcopy, T)
                        dve.tensor_copy(a_kT[:, 4 * (g - 2):4 * (g - 2) + 4, j * P:(j + 1) * P],
                                        ps[:, 6 + T % 2, :].rearrange("p (h t) -> p h t", h=4))\
                            .then_inc(s.a_tcopy, 1)
                    if j + 1 < NT:
                        normalise(j + 1)
                dve.wait_ge(s.a_gamma, 1)

                def state(h):
                    dve.wait_ge(s.a_kv, h + 1)
                    if h >= 2:
                        dve.wait_ge(s.a_y_ps, h - 1)
                    kv = lambda n: ps[:, 2 * (h % 2) + n % 2, (n // 2) * P:(n // 2 + 1) * P]
                    after(dve.tensor_copy(a_st[:, h % 2, 1, :], kv(0)))
                    for n in range(1, NCH - 1):
                        ins = stt(a_st[:, h % 2, n + 1, :], a_st[:, h % 2, n, :], a_gam[:, n % 2, n // 2, h:h + 1],
                                  kv(n), ALU.mult, ALU.add)
                        if n < NCH - 2:
                            after(ins)
                    ins.then_inc(s.a_state, 1)

                def maxima(h):
                    dve.wait_ge(s.a_scores, h + 1)
                    c = 4 * (h % 2)
                    for j in range(NT):
                        ins = dve.tensor_tensor_reduce(a_sc[:, h % 2, j, :], ps[:, 4 + h % 2, j * P:(j + 1) * P],
                                                       C("mask_a"), 1.0, -3e38, ALU.add, ALU.max,
                                                       mxa[:, c + j:c + j + 1])
                    after(ins)
                    ts(nma[:, c:c + 4], mxa[:, c:c + 4], -float(P) ** -0.5, None, ALU.mult).then_inc(s.a_max, 1)

                def divide(h):
                    dve.wait_ge(s.a_exp, h + 1)
                    c = 4 * (h % 2)
                    after(dve.reciprocal(ria[:, c:c + 4], rsa[:, c:c + 4]))
                    tt(a_p[:, h % 2], a_p[:, h % 2], wide(ria[:, c:c + 4], [P, NT, P], 2), ALU.mult)\
                        .then_inc(s.a_prob, 1)

                for i in range(HA + 1):
                    if i < HA:
                        maxima(i)
                    if i:
                        divide(i - 1)
                    if i < HA:
                        state(i)
                dve.wait_ge(s.a_o, 1)
                after(tt(XB[:, :, :], XB[:, :, :], ps[:, 0, :].rearrange("p (j d) -> p j d", j=NT), ALU.add))

            def window_layer(k, l):
                u0 = NT * k
                dve.wait_ge(s.f_yT_ps, k + 1)
                dve.tensor_copy(f_hT[0:64, :], ps[0:64, 0, :])
                dve.tensor_copy(f_hT[64:128, 1:S], ps[64:128, 0, 0:S - 1]).then_inc(s.f_hT_in, 1)

                def turned(bank, t1, t2, out, cos, sin):
                    v = ps[:, bank, :].rearrange("p (h d) -> p h d", h=HF)
                    w = lambda t: t.rearrange("p (h d) -> p h d", h=HF)
                    tt(w(t1), v, wide(cos, [P, HF, DF], 1), ALU.mult)
                    after(tt(w(t2), v, wide(sin, [P, HF, DF], 1), ALU.mult))
                    tt(w(out)[:, :, 0:32], w(t1)[:, :, 0:32], w(t2)[:, :, 32:64], ALU.add)
                    return tt(w(out)[:, :, 32:64], w(t1)[:, :, 32:64], w(t2)[:, :, 0:32], ALU.add)

                def table(n, j):
                    return tabs[:, l, n, j * DF:(j + 1) * DF]

                def rope_q(j):
                    dve.wait_ge(s.f_sq, u0 + j + 1)
                    after(dve.tensor_reduce(rstd[:, 0:16], f_sqr.rearrange("p (h d) -> p h d", h=16), AX, ALU.add))
                    root(16, ts(rstd[:, 0:16], rstd[:, 0:16], 1e-24, None, ALU.max))
                    turned(0, f_t1, f_t2, f_qr, table(0, j), table(1, j))

                def rope_k(j):
                    after(turned(1, f_t3, f_t4, f_t3, table(2, j), table(3, j)))
                    rooted()
                    ts(f_rn[:, 0:8], rstd[:, 0:8], 1.0, None, ALU.mult)
                    w = lambda t: t.rearrange("p (h d) -> p h d", h=HF)
                    tt(w(f_kr), w(f_t3), wide(rstd[:, 8:16], [P, HF, DF], 2), ALU.mult).then_inc(s.f_rope, 1)

                def maxima(j, g):
                    n = 2 * (u0 + j) + g
                    dve.wait_ge(s.f_sc_ps, n + 1)
                    lo = 0 if j else WIN
                    for i in range(4):
                        h = 4 * g + i
                        at = KW * (i // 2)
                        ins = dve.tensor_tensor_reduce(f_sc[:, h, lo:KW], ps[:, 4 + h % 2, at + lo:at + KW],
                                                       C("mask_f", lo, KW), f_rn[:, h:h + 1], -3e38, ALU.add, ALU.max,
                                                       f_mx[:, h:h + 1])
                    after(ins)
                    ts(f_nm[:, 4 * g:4 * g + 4], f_mx[:, 4 * g:4 * g + 4], -1.0, None, ALU.mult).then_inc(s.f_max, 1)

                def copy_probs(j, g):
                    n = 2 * (u0 + j) + g
                    dve.wait_ge(s.f_pT_ps, n + 1)
                    side = 0 if j else 1
                    dve.tensor_copy(f_pT[:, 4 * g + 2:4 * g + 4, side:2, :],
                                    ps[:, 7, :].rearrange("p (h s t) -> p h s t", h=2, s=2)[:, :, side:2, :])\
                        .then_inc(s.f_pT_b, 1)

                rope_q(0)
                rope_k(0)
                for j in range(NT):
                    u = u0 + j
                    maxima(j, 0)
                    maxima(j, 1)
                    copy_probs(j, 0)
                    if j + 1 < NT:
                        rope_q(j + 1)
                    copy_probs(j, 1)
                    dve.wait_ge(s.f_exp, 2 * u + 2)
                    after(dve.reciprocal(f_ri[:, 0:8], f_rs[:, 0:8]))
                    dve.wait_ge(s.f_o_ps, 2 * u + 2)
                    w = lambda t: t.rearrange("p (h d) -> p h d", h=HF)
                    tt(w(f_os), w(ps[:, 3, :]), wide(f_ri[:, 0:8], [P, HF, DF], 2), ALU.mult).then_inc(s.f_o_in, 1)
                    if j + 1 < NT:
                        rope_k(j + 1)
                    dve.wait_ge(s.f_attn, u + 1)
                    tt(Y[:, j, :], Y[:, j, :], ps[:, 3, 0:D], ALU.add).then_inc(s.f_y, 1)
                dve.wait_ge(s.f_h_in, k + 1)
                layer_norm(f_h, f_h, NT, EPS5).then_inc(s.ln_out, 1)
                for c, m in enumerate(HID_C):
                    dve.wait_ge(s.f_gelu, 3 * k + c + 1)
                    bias = W("f_cols", 8 * l + 5 + c, 8 * l + 6 + c)
                    stt(f_hm[0:m, c, :], ps[0:m, 3 + 2 * c, :], bias[0:m, :], f_gb[0:m, c, :], ALU.add, ALU.mult)\
                        .then_inc(s.f_mid, 1)
                dve.wait_ge(s.f_down, k + 1)
                after(tt(Y[:, :, :], Y[:, :, :], ps[:, 0, :].rearrange("p (j d) -> p j d", j=NT), ALU.add))
                tt(Y[:, :, :], Y[:, :, :], wide(R("b2", D * l, D * l + D), [P, NT, D], 1), ALU.add)\
                    .then_inc(s.f_fin, 1)
                dve.wait_ge(s.f_fin, k + 1)

            def small_heads(k):
                glob = k == 0
                flat = lambda a: a.rearrange("p j h d -> p (j h) d")
                hn = b_hn
                after(tt(hn, Y[:, :, :], Y[:, :, :], ALU.mult))
                after(dve.tensor_reduce(rstd[:, 0:NT], hn, AX, ALU.add))
                root(NT, ts(rstd[:, 0:NT], rstd[:, 0:NT], 1.0 / D, EPS6, ALU.mult, ALU.add))
                rooted()
                tt(hn, Y[:, :, :], wide(rstd[:, 0:NT], [P, NT, D], 2), ALU.mult).then_inc(s.b_hn_in, 1)
                dve.wait_ge(s.b_qk_in, k + 1)
                nm = "g" if glob else "l"
                cos = wide(C("cos_" + nm).rearrange("p (j d) -> p j d", j=NT), [P, NT, 20, 4], 2)
                sin = wide(C("sin_" + nm).rearrange("p (j d) -> p j d", j=NT), [P, NT, 20, 4], 2)
                even, odd = b_qk[:, :, :, 0:HD:2], b_qk[:, :, :, 1:HD:2]
                tt(b_t[0], even, cos, ALU.mult)
                tt(b_t[1], odd, sin, ALU.mult)
                tt(b_t[2], even, sin, ALU.mult)
                after(tt(b_t[3], odd, cos, ALU.mult))
                tt(b_qr[:, :, :, 0:HD:2], b_t[0], b_t[1], ALU.subtract)
                after(tt(b_qr[:, :, :, 1:HD:2], b_t[2], b_t[3], ALU.add))
                sq = b_sq.rearrange("p (n d) -> p n d", d=HD)
                after(tt(sq, flat(b_qr), flat(b_qr), ALU.mult))
                after(dve.tensor_reduce(rstd[:, 0:80], sq, AX, ALU.add))
                root(80, ts(rstd[:, 0:80], rstd[:, 0:80], 1.0 / HD, EPS6, ALU.mult, ALU.add))
                rooted()
                after(tt(flat(b_qr), flat(b_qr), wide(rstd[:, 0:80], [P, 80, HD], 2), ALU.mult))
                for r in range(NR):
                    ins = dve.tensor_copy(b_kr[:, :, :, r, :], b_qr[:, :, HB:20, :])
                ins.then_inc(s.b_rope, 1)
                dve.wait_ge(s.b_tps, k + 1)
                for r in range(NR):
                    ins = ts(b_kT[:, r, :], ps[:, 5, :], C("rows", r, r + 1), None, ALU.mult)
                ins.then_inc(s.b_kT_in, 1)
                dve.wait_ge(s.b_pv, 8 * (k + 1))
                o = [ps[:, 6 + i, 0:288].rearrange("p (i h d) -> p i h d", i=2, h=HB) for i in range(2)]
                for i in range(2):
                    ins = dve.reciprocal(b_ri[:, 2 * i:2 * i + 2, :], o[i][:, :, :, HD])
                after(ins)
                for i in range(2):
                    ins = tt(b_os[:, 2 * i:2 * i + 2], o[i][:, :, :, 0:HD],
                             wide(b_ri[:, 2 * i:2 * i + 2, :], [P, 2, HB, HD], 3), ALU.mult)
                ins.then_inc(s.b_os_in, 1)
                dve.wait_ge(s.b_out, k + 1)
                after(tt(Y[:, :, :], Y[:, :, :], ps[:, 1, :].rearrange("p (j d) -> p j d", j=NT), ALU.add))

            def head_attention():
                layer_norm(XB, Y, NT, EPS5).then_inc(s.ln_out, 1)
                dve.wait_ge(s.c_qkv_in, 1)
                part = lambda j, n: c_qkv[:, j, 128 * n:128 * n + 128].rearrange("p (h d) -> p h d", h=HB)
                full = [P, HB, HB, HD]

                def scores(j):
                    z = j % 2
                    prod = c_prod.rearrange("p (h t d) -> p h t d", h=HB, t=HB)
                    after(tt(prod, part(j, 0).unsqueeze(2).broadcast_to(full),
                             part(j, 1).unsqueeze(1).broadcast_to(full), ALU.mult))
                    if j >= 2:
                        dve.wait_ge(s.c_exp, j - 1)
                    after(dve.tensor_reduce(c_sc[:, z], prod, AX, ALU.add))
                    after(dve.tensor_reduce(mxa[:, :], c_sc[:, z], AX, ALU.max))
                    tt(c_sc[:, z], c_sc[:, z], wide(mxa[:, :], [P, HB, HB], 2), ALU.subtract).then_inc(s.c_shift, 1)

                def weights(j):
                    z = j % 2
                    dve.wait_ge(s.c_exp, j + 1)
                    after(dve.tensor_reduce(rsa[:, :], c_e[:, z], AX, ALU.add))
                    after(dve.reciprocal(ria[:, :], rsa[:, :]))
                    tt(c_e[:, z], c_e[:, z], wide(ria[:, :], [P, HB, HB], 2), ALU.mult).then_inc(s.c_wts, 1)

                def summed(j):
                    dve.wait_ge(s.c_prod, j + 1)
                    ins = dve.tensor_reduce(c_os[:, j * P:(j + 1) * P],
                                            c_mix[:, j % 2].rearrange("p (n t) -> p n t", t=HB), AX, ALU.add)
                    if j == NT - 1:
                        ins.then_inc(s.c_os_in, 1)
                    else:
                        ins.then_inc(s.c_red, 1)

                for i in range(NT + 2):
                    if i < NT:
                        scores(i)
                    if i >= 2:
                        summed(i - 2)
                    if 1 <= i <= NT:
                        weights(i - 1)
                dve.wait_ge(s.c_out, 1)
                after(tt(XB[:, :, :], XB[:, :, :], ps[:, 5, :].rearrange("p (j d) -> p j d", j=NT), ALU.add))

            def full_attention():
                layer_norm(XB, Y, NT, EPS5).then_inc(s.ln_out, 1)
                dve.wait_ge(s.ln_out, 1)
                layer_norm(Y, Y, NT, EPS5).then_inc(s.ln_out, 1)
                dve.wait_ge(s.m_sq, 1)
                after(dve.tensor_reduce(rstd[:, 0:16], m_sq.rearrange("p (n d) -> p n d", d=DF), AX, ALU.add))
                root(16, ts(rstd[:, 0:16], rstd[:, 0:16], 1.0 / DF, 1e-16, ALU.mult, ALU.max))
                rooted()
                for c in range(2):
                    src = ps[:, 1 + c, :].rearrange("p (j h d) -> p j h d", j=NT, h=2)
                    rn = rstd[:, 8 * c:8 * c + 8].rearrange("p (j h) -> p j h", j=NT)
                    dst = m_qk[:, :, 128 * c:128 * c + 128].rearrange("p j (h d) -> p j h d", h=2)
                    ins = tt(dst, src, wide(rn, [P, NT, 2, DF], 3), ALU.mult)
                ins.then_inc(s.m_qk_in, 1)
                dve.wait_ge(s.m_tps, 1)
                ts(m_kT, ps[:, 5, :], W("d_cols", 3, 4), None, ALU.mult).then_inc(s.m_kT_in, 1)
                steps, heads, dv = full_steps(), 2, DF
                scale = float(DF) ** -0.5
                for st in range(len(steps) + 1):
                    if st < len(steps):
                        dve.wait_ge(s.m_s, st + 1)
                        if st >= 2:
                            dve.wait_ge(s.m_exp, st - 1)
                        b = 2 * (st % 2)
                        after(dve.tensor_reduce(mxa[:, b:b + 2], ps[:, b:b + 2, :], AX, ALU.max))
                        ts(nma[:, b:b + 2], mxa[:, b:b + 2], -scale, None, ALU.mult).then_inc(s.m_max, 1)
                    if st:
                        dve.wait_ge(s.m_tp, st)
                        if st >= 2:
                            dve.wait_ge(s.m_pv, st - 1)
                        dve.tensor_copy(m_pT[:, 1], ps[:, 5, :].rearrange("p (j t) -> p j t", j=NT))\
                            .then_inc(s.m_pT_b, 1)
                dve.wait_ge(s.m_pv, len(steps))
                n = NT * heads
                after(dve.reciprocal(m_rs[:, 0:n], m_rs[:, 0:n]))
                tt(m_os.rearrange("p (n d) -> p n d", n=n), ps[:, 6, :].rearrange("p (n d) -> p n d", n=n),
                   wide(m_rs[:, 0:n], [P, n, dv], 2), ALU.mult).then_inc(s.m_os_in, 1)
                dve.wait_ge(s.m_out, 1)
                after(tt(XB[:, :, :], XB[:, :, :], ps[:, 1, :].rearrange("p (j d) -> p j d", j=NT), ALU.add))
                after(tt(XB[:, :, :], XB[:, :, :], wide(R("bo"), [P, NT, D], 1), ALU.add))

            def experts(k):
                def step(ins):
                    after(ins)

                def three(ap):
                    return ap.unsqueeze(2).broadcast_to([P, TT, E])

                layer_norm(X, e_xl, TT, EPS5).then_inc(es.e_ln, 1)
                dve.wait_ge(es.e_lg_ps, k + 1)
                step(tt(e_lg, ps[:, 2, 0:128].rearrange("p (i e) -> p i e", i=TT), wide(R("bs"), [P, TT, E], 1), ALU.add))
                step(dve.tensor_reduce(e_m[:, 0], e_lg, AX, ALU.max))
                tt(e_lg, e_lg, three(e_m[:, 0]), ALU.subtract).then_inc(es.e_shift, 1)
                dve.wait_ge(es.e_expd, k + 1)
                step(dve.tensor_reduce(e_m[:, 1], e_ex, AX, ALU.add))
                step(dve.reciprocal(e_m[:, 2], e_m[:, 1]))
                step(tt(e_pr, e_ex, three(e_m[:, 2]), ALU.mult))
                step(dve.tensor_reduce(e_m[:, 3], e_pr, AX, ALU.max))
                step(tt(e_cand, e_pr, three(e_m[:, 3]), ALU.is_equal))
                step(tt(e_cand, e_cand, wide(C("iota8"), [P, TT, E], 1), ALU.mult))
                step(dve.tensor_reduce(e_m[:, 4], e_cand, AX, ALU.min))
                tt(e_oh, wide(C("iota8"), [P, TT, E], 1), three(e_m[:, 4]), ALU.is_equal)
                tt(e_xl, e_xl, e_m[:, 3].unsqueeze(2).broadcast_to([P, TT, D]), ALU.mult).then_inc(es.e_probs, 1)
                dve.wait_ge(es.e_rank_ps, k + 1)
                rank = ps[:, 3, 0:128].rearrange("p (i e) -> p i e", i=TT)
                dve.memset(e_pre[:, 0, :], 0.0)
                dve.memset(e_eo[:, 0:1], 0.0)
                step(dve.tensor_copy(e_tot, ps[:, 3, 128:256].rearrange("p (i e) -> p i e", i=TT)))
                for i in range(TT - 1):
                    step(tt(e_pre[:, i + 1, :], e_pre[:, i, :], e_tot[:, i, :], ALU.add))
                step(tt(e_tot[:, 0, :], e_pre[:, TT - 1, :], e_tot[:, TT - 1, :], ALU.add))
                for e in range(E - 1):
                    step(tt(e_eo[:, e + 1:e + 2], e_eo[:, e:e + 1], e_tot[:, 0, e:e + 1], ALU.add))
                step(tt(e_pos, rank, e_pre, ALU.add))
                step(tt(e_pos, e_pos, wide(e_eo, [P, TT, E], 1), ALU.add))
                step(tt(e_pos, e_pos, e_oh, ALU.mult))
                step(dve.tensor_reduce(e_m[:, 5], e_pos, AX, ALU.add))
                dve.tensor_copy(e_idx[:, :], e_m[:, 5]).then_inc(es.e_idx_in, 1)
                n = E * NB
                dve.wait_ge(es.e_b2_in, k + 1)
                for q in range(n):
                    e, c = q // NB, q % NB
                    dve.wait_ge(es.e_down, n * k + q + 1)
                    if q >= NB:
                        dve.wait_ge(es.e_acc_in, n * k + q - NB + 1)
                    for j in range(NT):
                        i = NT * c + j
                        ins = stt(e_acc[:, i, :], ps[:, 6 + q % 2, j * P:(j + 1) * P], e_oh[:, i, e:e + 1],
                                  e_acc[:, i, :], ALU.mult, ALU.add)
                    ins.then_inc(es.e_acc_in, 1)
                dve.wait_ge(es.e_back_in, 16 * (k + 1))
                tt(X[:, :, :], X[:, :, :], e_back, ALU.add).then_inc(es.e_out, 1)
                dve.wait_ge(es.e_out, k + 1)

            def stages(which):
                f = 0
                for i, st in enumerate(which):
                    if st == "a":
                        linear_attention()
                    elif st == "f":
                        layer_norm(XB, Y, NT, EPS5).then_inc(s.ln_out, 1)
                        for l in range(2):
                            window_layer(f, l)
                            f += 1
                        after(tt(XB[:, :, :], XB[:, :, :], Y[:, :, :], ALU.add))
                    elif st == "b":
                        after(layer_norm(XB, Y, NT, EPS5))
                        small_heads(0)
                        small_heads(1)
                        after(tt(XB[:, :, :], XB[:, :, :], Y[:, :, :], ALU.add))
                    elif st == "c":
                        head_attention()
                    else:
                        full_attention()
                    stage_done(dve, i + 1)

            dve.memset(f_hT[64:128, 0:1], 0.0)
            dve.memset(b_vx[:, :, :, HD:HD + 1], 1.0)
            dve.drain()
            dve.wait_ge(s_loaded, 64)
            for l in range(2):
                for n, (tab, gain) in enumerate((("cos_q", "qs"), ("sin_q", "qs"), ("cos_k", "ks"), ("sin_k", "ks"))):
                    ins = tt(tabs[:, l, n, :].rearrange("p (j d) -> p j d", j=NT),
                             C(tab).rearrange("p (j d) -> p j d", j=NT),
                             wide(R(gain, DF * l, DF * l + DF), [P, NT, DF], 1), ALU.mult)
            ins.then_inc(s_tabs, 1)
            dve.wait_ge(s_tabs, 1)
            with dve.Fori(0, NB) as b:
                dve.wait_ge(batch_go, b + 1)
                dve.sem_inc(batch_seen, 1)
                steps_done.n = asked.n = 0
                after(ts(XB[:, :, :], X[:, bass.ds(b * NT, NT), :], 1.0, None, ALU.mult))
                stages(in_loop)
                ts(X[:, bass.ds(b * NT, NT), :], XB[:, :, :], 1.0, None, ALU.mult).then_inc(batch_done, 1)
            steps_done.n = asked.n = 0
            if STAGES >= 6:
                dve.wait_ge(batch_go, NB + 1)
                dve.sem_inc(batch_seen, 1)
                experts(0)
            if STAGES >= 7:
                dve.drain().then_inc(batch_done, 1)
                with dve.Fori(0, NB) as b:
                    dve.wait_ge(batch_go, b + NB + 2)
                    dve.sem_inc(batch_seen, 1)
                    steps_done.n = asked.n = 0
                    after(ts(XB[:, :, :], X[:, bass.ds(b * NT, NT), :], 1.0, None, ALU.mult))
                    stages(["d"])
                    ts(X[:, bass.ds(b * NT, NT), :], XB[:, :, :], 1.0, None, ALU.mult).then_inc(batch_done, 1)
            if STAGES >= 8:
                steps_done.n = asked.n = 0
                dve.wait_ge(batch_go, 2 * NB + 2)
                dve.sem_inc(batch_seen, 1)
                experts(1)
            dve.drain().then_inc(s_tabs, 1)

        @block.gpsimd
        def _(pool):
            asked = Count()

            def root(n):
                pool.wait_ge(s.pow_in, asked.next())
                pool.tensor_tensor(rstd[:, 0:n], rstd[:, 0:n], C("neghalf", 0, n), ALU.pow).then_inc(s.pow_out, 1)

            def stages(which):
                for i, st in enumerate(which):
                    if st == "a":
                        root(NT)
                        for j in range(NT):
                            root(16)
                    elif st == "f":
                        pool.memset(f_p[:, :, 0:256 - KW], 0.0).then_inc(s.f_zero, 1)
                        root(NT)
                        for l in range(2):
                            for j in range(NT):
                                root(16)
                            root(NT)
                    elif st == "b":
                        root(NT)
                        for k in range(2):
                            glob = k == 0
                            root(NT)
                            root(80)
                            m = C("causal") if glob else C("local")
                            for u in range(8):
                                for j in range(NT):
                                    pool.wait_ge(s.b_exp, 32 * k + 4 * u + j + 1)
                                    n = min(small_width(glob, j), P if glob else P + LW)
                                    at = small_at(glob, j)
                                    v = b_p[:, u % 2, :, at:at + n]
                                    pool.tensor_tensor(v, v, m[:, 0:n].unsqueeze(1).broadcast_to([P, 2, n]), ALU.mult)\
                                        .then_inc(s.b_mask, 1)
                    elif st == "c":
                        root(NT)
                        for j in range(NT):
                            pool.wait_ge(s.c_wts, j + 1)
                            if j >= 2:
                                pool.wait_ge(s.c_red, j - 1)
                            full = [P, HB, HD, HB]
                            vals = c_qkv[:, j, 256:384].rearrange("p (t d) -> p d t", t=HB)
                            pool.tensor_tensor(c_mix[:, j % 2].rearrange("p (h d t) -> p h d t", h=HB, t=HB),
                                               c_e[:, j % 2].unsqueeze(2).broadcast_to(full),
                                               vals.unsqueeze(1).broadcast_to(full), ALU.mult).then_inc(s.c_prod, 1)
                    else:
                        root(NT)
                        root(NT)
                        root(16)
                    stage_done(pool, i + 1)

            def experts(k):
                root(TT)
                pool.wait_ge(es.e_idx_in, k + 1)
                pool.wait_ge(es.e_acc_in, E * NB * (k + 1))
                for i in range(TT):
                    pool.indirect_dma_start(scratch[:, :], bass.IndirectOffsetOnAxis(ap=e_idx[:, i:i + 1], axis=0),
                                            e_acc[:, i, :], None).then_inc(es.e_sent, 16)

            pool.wait_ge(s_loaded, 64)
            with pool.Fori(0, NB) as b:
                pool.wait_ge(batch_go, b + 1)
                pool.sem_inc(batch_seen, 1)
                asked.n = 0
                stages(in_loop)
                pool.drain().then_inc(batch_done, 1)
            asked.n = 0
            if STAGES >= 6:
                pool.wait_ge(batch_go, NB + 1)
                pool.sem_inc(batch_seen, 1)
                experts(0)
            if STAGES >= 7:
                with pool.Fori(0, NB) as b:
                    pool.wait_ge(batch_go, b + NB + 2)
                    pool.sem_inc(batch_seen, 1)
                    asked.n = 0
                    stages(["d"])
                    pool.drain().then_inc(batch_done, 1)
            if STAGES >= 8:
                asked.n = 0
                pool.wait_ge(batch_go, 2 * NB + 2)
                pool.sem_inc(batch_seen, 1)
                experts(1)

        @block.sync
        def _(sp):
            sp.dma_start(X[:, :, :], x_in.rearrange("b (t p) d -> p (b t) d", p=P)).then_inc(s_loaded, 16)
            sp.dma_start(Ct[:, :], c_in).then_inc(s_loaded, 16)
            sp.dma_start(Rt[:, :], r_in.broadcast_to([P, r_cols])).then_inc(s_loaded, 16)
            sp.dma_start(Wt[:, :], w_in).then_inc(s_loaded, 16)

            def clear():
                sp.sem_clear(range(first, first + len(names)))
                sp.sem_clear(batch_done)
                sp.sem_inc(batch_go, 1)

            def back(k):
                sp.wait_ge(es.e_sent, 16 * TT * (k + 1))
                sp.dma_start(e_back, scratch.rearrange("(i p) d -> p i d", p=P)).then_inc(es.e_back_in, 16)

            numbers = sorted(sem_number(sems[n]) for n in names)
            first = numbers[0]
            assert numbers == list(range(first, first + len(names)))
            sp.sem_inc(batch_go, 1)
            with sp.Fori(0, NB) as b:
                sp.wait_ge(batch_done, 4)
                clear()
            if STAGES >= 6:
                back(0)
            if STAGES >= 7:
                sp.wait_ge(batch_done, 1)
                clear()
                with sp.Fori(0, NB) as b:
                    sp.wait_ge(batch_done, 4)
                    clear()
            if STAGES >= 8:
                back(1)
            sp.wait_ge(s_tabs, 2)
            sp.dma_start(out.rearrange("b (t p) d -> p (b t) d", p=P), X[:, :, :]).then_inc(s_store, 16)
            sp.wait_ge(s_store, 16)


def sem_number(sem):
    return int(sem.num)


def small_width(glob, j):
    return S - j * P if glob else min(P + LW, S - j * P)


def small_at(glob, j):
    return sum(small_width(glob, i) for i in range(j))


def full_steps():
    return [(i, [(h, slice(64 * h, 64 * h + 64)) for h in range(2)]) for i in range(NT)]


def kernel(**inputs):
    import numpy as _np
    import concourse.bacc as _bacc
    from concourse import mybir as _mybir
    from concourse.bass_utils import run_bass_kernel_spmd as _run

    g = {k: _np.asarray(v) for k, v in inputs.items()}
    a = {k[len("L0_attn_a_"):]: v for k, v in g.items() if k.startswith("L0_attn_a_")}
    b = {k[len("L0_attn_b_"):]: v for k, v in g.items() if k.startswith("L0_attn_b_")}
    f = {k[len("L0_ffn_"):]: v for k, v in g.items() if k.startswith("L0_ffn_")}
    c = {k[len("L1_attn_a_"):]: v for k, v in g.items() if k.startswith("L1_attn_a_")}
    d = {k[len("L1_attn_b_"):]: v for k, v in g.items() if k.startswith("L1_attn_b_")}
    e = {k[len("L1_ffn_"):]: v for k, v in g.items() if k.startswith("L1_ffn_")}

    def pad(m):
        out = _np.zeros((P, m.shape[1]), m.dtype)
        out[:m.shape[0]] = m
        return out

    def col(v):
        return pad(v[:, None])

    side = lambda xs: _np.concatenate(xs, 1)
    blocks = {
        "a_qkv": side([a["Wq"].T, a["Wk"].T, a["Wv"].T]),
        "a_wo": a["Wo"].reshape(D, HA, 128).transpose(2, 1, 0).reshape(128, -1),
        "a_wg": a["Wg"].T,
        "f_wqkv": side([f["wqkv"][l] for l in range(2)]),
        "f_wo": side([f["wo"][l][128 * i:128 * i + 128] for l in range(2) for i in range(4)]),
        "f_w1": side([f["w1"][l] for l in range(2)]),
        "f_w2": side([pad(f["w2"][l][128 * i:min(128 * i + 128, HID)]) for l in range(2) for i in range(3)]),
        "f_cols": side([side([col(f["ln_g"][l]), col(f["ln_b"][l])]
                             + [col(f["b1"][l][HID + 128 * i:min(HID + 128 * i + 128, 2 * HID)]) for i in range(3)]
                             + [col(f["b1"][l][128 * i:min(128 * i + 128, HID)]) for i in range(3)]) for l in range(2)]),
        "b_norm": side([col(b["norm1_w"]), col(b["norm2_w"])]),
        "b_gq": b["g_wq"], "b_lq": b["l_wq"], "b_down": b["g_kv_down"],
        "b_up": pad(side([b["g_k_up"], b["g_v_up"]])), "b_lkv": side([b["l_wk"], b["l_wv"]]),
        "b_gwo": b["g_wo"], "b_lwo": b["l_wo"],
        "c_qkv": side([c["Wq"].T, c["Wk"].T, c["Wv"].T]), "c_fc": c["Wfc"].T,
        "d_qkv": side([d["w_q"].T, d["w_k"].T, d["w_v"].T]), "d_wo": d["w_o"].T,
        "d_cols": side([col(d["ln_gamma"]), col(d["ln_beta"]), col(_np.tile(d["q_gamma"], 2)),
                        col(_np.tile(d["k_gamma"], 2))]),
        "e_ws": e["Ws"].T, "e_w1": side([e["W1"][i] for i in range(E)]), "e_w2": side([e["W2"][i] for i in range(E)]),
        "e_b1": e["b1"].T, "e_b2": pad(e["b2"]),
    }
    for name, w in WEIGHTS:
        assert blocks[name].shape == (P, w), (name, blocks[name].shape, w)
    rows = {"bg": a["bg"], "gain": a["qk_gain"].reshape(1), "qs": f["q_scale"].reshape(-1),
            "ks": f["k_scale"].reshape(-1), "b2": f["b2"].reshape(-1), "bo": d["b_o"], "bs": e["bs"]}
    tables = constants()
    c_at, _ = places([(k, v.shape[1]) for k, v in tables.items()])
    arrays = {
        "in_x": _np.ascontiguousarray(a["x"]),
        "in_w": _np.ascontiguousarray(side([blocks[n] for n, _ in WEIGHTS])),
        "in_c": _np.ascontiguousarray(side(list(tables.values()))),
        "in_r": _np.ascontiguousarray(_np.concatenate([rows[n] for n, _ in ROWS])[None, :]),
    }
    nc = _bacc.Bacc("TRN2", target_bir_lowering=False, num_devices=1)
    f32 = _mybir.dt.float32
    args = [nc.dram_tensor(n, v.shape, f32, kind="ExternalInput").ap() for n, v in arrays.items()]
    out = nc.dram_tensor("out_0", (NB, S, D), f32, kind="ExternalOutput").ap()
    scratch = nc.dram_tensor("sorted_rows", (NB * S, D), f32, kind="Internal").ap()
    program(nc, *args, out, scratch, c_at)
    r = _run(nc, [arrays], core_ids=[0])
    return r.results[0]["out_0"]
```

```python
from contextlib import ExitStack

import numpy as np

import concourse.bass as bass
from concourse import mybir

STAGES = 8

ALU = mybir.AluOpType
ACT = mybir.ActivationFunctionType
F32 = mybir.dt.float32
U32 = mybir.dt.uint32
AX = mybir.AxisListType.X

P = 128
PAIR = 8
NP = 2
NB = 4
S = 512
NT = S // P
D = 128
HA, CH = 8, 64
NCH = S // CH
HF, DF = 8, 64
WIN = 64
KW = P + WIN
HID = 341
HID_C = [128, 128, HID - 256]
NG, NR, HD = 4, 4, 8
HB = NG * NR
LW = 32
E = 8
TT = NB * NT
EPS6, EPS5 = 1e-6, 1e-5
NEG = -1e30


def constants():
    f = np.float32
    p = np.arange(P)
    t = {}
    t["ident"] = np.eye(P)
    same = (p[:, None] // CH) == (p[None, :] // CH)
    t["mask_a"] = np.where(same & (p[None, :] <= p[:, None]), 0.0, NEG)
    c = np.arange(KW)
    t["mask_f"] = np.where((c[None, :] >= p[:, None]) & (c[None, :] - WIN <= p[:, None]), 0.0, -1e25)
    t["causal"] = (p[None, :] >= p[:, None]) * 1.0
    q = np.arange(P + LW)
    t["local"] = ((q[None, :] >= p[:, None]) & (q[None, :] < p[:, None] + LW)) * 1.0
    t["shift"] = np.eye(P, k=1)
    t["carry"] = np.zeros((P, P))
    t["carry"][P - 1, 0] = 1.0
    t["half0"] = np.repeat((p < CH)[:, None], P, 1) * 1.0
    t["half1"] = np.repeat((p >= CH)[:, None], P, 1) * 1.0
    t["rows"] = ((p[:, None] % 32) // HD == np.arange(NR)[None, :]) * 1.0
    t["neghalf"] = np.full((P, 80), -0.5)
    t["ones"] = np.ones((P, P))
    t["before"] = (p[:, None] < p[None, :]) * 1.0
    t["iota8"] = np.repeat((np.arange(E) - E)[None, :], P, 0) * 1.0
    half = np.arange(0, DF, 2, dtype=f)
    inv = (f(1) / np.power(10000.0, half.astype(np.float64) / DF).astype(f)).astype(f)
    pos = np.arange(S, dtype=f)
    fr = (pos[:, None] * inv[None, :]).astype(f).astype(np.float64)
    base = ((half + f(0.4 * DF)) / f(1.4 * DF)).astype(f).astype(np.float64)
    power = ((pos - S // 2) / f(WIN // 2)).astype(np.float64)
    sc = base[None, :] ** power[:, None]
    cos, sin = np.cos(fr), np.sin(fr)
    both = lambda a: np.concatenate([a, a], 1)
    sign = lambda a: np.concatenate([a, -a], 1)
    tile = lambda a: a.reshape(NT, P, -1).transpose(1, 0, 2).reshape(P, -1)
    t["cos_q"], t["sin_q"] = tile(both(cos * sc * 8.0)), tile(sign(sin * sc * 8.0))
    t["cos_k"], t["sin_k"] = tile(both(cos / sc)), tile(sign(sin / sc))
    for name, b in (("g", 1e6), ("l", 1e4)):
        iv = (f(1) / np.power(f(b), np.arange(0, HD, 2, dtype=f) / f(HD))).astype(f)
        fq = (pos[:, None] * iv[None, :]).astype(f).astype(np.float64)
        t["cos_" + name], t["sin_" + name] = tile(np.cos(fq)), tile(np.sin(fq))
    return {k: np.ascontiguousarray(v, dtype=f) for k, v in t.items()}


def places(blocks):
    at, out = 0, {}
    for name, w in blocks:
        out[name] = (at, w)
        at += w
    return out, at


WEIGHTS = [("a_qkv", 3072), ("a_wo", 1024), ("a_wg", 8),
           ("f_wqkv", 3072), ("f_wo", 1024), ("f_w1", 2 * 2 * HID), ("f_w2", 2 * 3 * 128),
           ("f_cols", 2 * 8),
           ("b_norm", 2), ("b_gq", 128), ("b_lq", 128), ("b_down", 32), ("b_up", 64), ("b_lkv", 64),
           ("b_gwo", 128), ("b_lwo", 128),
           ("c_qkv", 384), ("c_fc", 128),
           ("d_qkv", 384), ("d_wo", 128), ("d_cols", 4),
           ("e_ws", 8), ("e_w1", 1024), ("e_w2", 1024), ("e_b1", 8), ("e_b2", 128)]
ROWS = [("bg", HA), ("gain", 1), ("qs", 2 * DF), ("ks", 2 * DF), ("b2", 2 * D), ("bo", D), ("bs", E)]


def program(nc, x_in, w_in, c_in, r_in, out, scratch, c_at):
    w_at, w_cols = places(WEIGHTS)
    r_at, r_cols = places(ROWS)
    c_cols = sum(w for _, w in c_at.values())
    with ExitStack() as ctx:
        def sb(name, shape, dt=F32):
            return ctx.enter_context(nc.sbuf_tensor(name, shape, dt))

        Wt, Ct, Rt = sb("weights", [P, w_cols]), sb("consts", [P, c_cols]), sb("rows", [P, r_cols])

        def W(name, a=0, b=None):
            at, w = w_at[name]
            return Wt[:, at + a:at + (w if b is None else b)]

        def C(name, a=0, b=None):
            at, w = c_at[name]
            return Ct[:, at + a:at + (w if b is None else b)]

        def R(name, a=0, b=None):
            at, w = r_at[name]
            return Rt[:, at + a:at + (w if b is None else b)]

        ident = C("ident")
        ps = ctx.enter_context(nc.psum_tensor("ps", [P, 8, 512], F32))

        X = sb("X", [P, TT, D])
        XB = sb("XB", [P, 2 * NT, D])
        Y = sb("Y", [P, 2 * NT, D])
        stats = sb("stats", [P, TT, 6])
        mv = sb("mv", [P, TT, 2])
        rstd = sb("rstd", [P, 80])
        xT = sb("xT", [P, S])
        tabs = sb("tabs", [P, 2, 4, NT * DF])
        arena = sb("arena", [P, 24576])
        taken = [0]

        def carve(n):
            at = taken[0]
            taken[0] += n
            assert taken[0] <= 24576, taken
            return arena[:, at:at + n]

        a_kn = carve(4096).rearrange("p (j h d) -> p j h d", j=NT, h=HA)
        a_v = carve(4096).rearrange("p (j n) -> p j n", j=NT)
        a_qT = carve(4096).rearrange("p (h t) -> p h t", h=HA)
        a_kT = carve(4096).rearrange("p (h t) -> p h t", h=HA)
        a_union = taken[0]
        a_sqr = carve(2048)
        a_qn = carve(1024).rearrange("p (h d) -> p h d", h=HA)
        taken[0] = a_union
        a_st = carve(2048).rearrange("p (z n d) -> p z n d", z=2, n=NCH)
        a_yT = carve(4096).rearrange("p (h t) -> p h t", h=HA)
        a_sc = sb("a_sc", [P, 2, NT, P])
        a_p = sb("a_p", [P, 2, NT, P])
        a_pT = sb("a_pT", [P, NT, P])
        a_gate = sb("a_gate", [P, 32])
        a_gam = sb("a_gam", [P, 2, NT, HA])
        small = sb("small", [P, 6, 16])
        mxa, nma, rsa, ria = small[:, 0, :], small[:, 1, :], small[:, 2, :], small[:, 3, :]
        taken[0] = 0
        f_v = carve(2 * 2048).rearrange("p (i n) -> p i n", i=2 * NT)
        f_kT = carve(2 * 2048).rearrange("p (z c t) -> p z c t", z=2, c=4)
        f_sqr = carve(1024)
        f_qr, f_kr = carve(512), carve(512)
        f_qT = carve(512).rearrange("p (c t) -> p c t", c=4)
        f_p = carve(8 * 256).rearrange("p (h s) -> p h s", h=HF)
        f_os = carve(512)
        f_oT = carve(512).rearrange("p (c t) -> p c t", c=4)
        f_h = carve(1024).rearrange("p (i d) -> p i d", i=2 * NT)
        f_hnT = carve(1024).rearrange("p (z t) -> p z t", z=2)
        f_shared = taken[0]
        f_t1, f_t2, f_t3, f_t4 = carve(512), carve(512), carve(512), carve(512)
        f_sc = carve(8 * KW).rearrange("p (h s) -> p h s", h=HF)
        f_pT = carve(8 * 256).rearrange("p (h s t) -> p h s t", h=HF, s=2)
        taken[0] = f_shared
        f_gb = carve(3 * 512).rearrange("p (c t) -> p c t", c=3)
        f_hm = carve(2 * 3 * 512).rearrange("p (z c t) -> p z c t", z=2, c=3)
        f_hT = sb("f_hT", [P, 2, S])
        f_ss = sb("f_ss", [P, 16])
        f_small = sb("f_small", [P, 5, 8])
        f_mx, f_nm, f_ri = f_small[:, 0, :], f_small[:, 1, :], f_small[:, 2, :]
        f_rs = f_small[:, 3:5, :]
        taken[0] = 0
        b_sq = carve(4 * 160)
        b_qk = carve(4 * 160).rearrange("p (j h d) -> p j h d", j=NT, h=20)
        b_qr = carve(4 * 160).rearrange("p (j h d) -> p j h d", j=NT, h=20)
        b_t = [carve(4 * 80).rearrange("p (j h d) -> p j h d", j=NT, h=20) for _ in range(4)]
        b_kr = carve(512).rearrange("p (j g r d) -> p j g r d", j=NT, g=NG, r=NR)
        b_latT = carve(512)
        b_qT = carve(2 * 512).rearrange("p (k t) -> p k t", k=2)
        b_kT = carve(2 * 2048).rearrange("p (k r t) -> p k r t", k=2, r=NR)
        b_os = carve(512).rearrange("p (j g r d) -> p j g r d", j=NT, g=NG, r=NR)
        b_oT = carve(512)
        b_oR = carve(4 * 512).rearrange("p (r t) -> p r t", r=NR)
        b_hn = carve(512).rearrange("p (j d) -> p j d", j=NT)
        b_p = carve(2 * 2 * 1280).rearrange("p (z h t) -> p z h t", z=2, h=2)
        b_pitch = NG * (P + 32)
        b_vx = carve(2 * NT * b_pitch).rearrange("p (k j n) -> p k j n", k=2, j=NT)
        b_ri = sb("b_ri", [P, NR, NT, NG])
        taken[0] = 0
        c_qkv = carve(NT * 384).rearrange("p (j n) -> p j n", j=NT)
        c_prod = carve(2048)
        c_mix = carve(2 * 2048).rearrange("p (z n) -> p z n", z=2)
        c_sc = carve(2 * 256).rearrange("p (z h t) -> p z h t", z=2, h=HB)
        c_e = carve(2 * 256).rearrange("p (z h t) -> p z h t", z=2, h=HB)
        c_os = carve(512)
        c_oT = carve(512)
        taken[0] = 0
        m_qT = carve(512)
        m_kT = carve(512)
        m_v = carve(512).rearrange("p (j n) -> p j n", j=NT)
        m_p = carve(2048).rearrange("p (z h s) -> p z h s", z=2, h=2)
        m_pT = carve(1024).rearrange("p (h j t) -> p h j t", h=2, j=NT)
        m_os = carve(512)
        m_oT = carve(512)
        m_sq = carve(1024)
        m_qk = carve(1024).rearrange("p (j n) -> p j n", j=NT)
        m_rs = sb("m_rs", [P, NT * 2])
        taken[0] = 0
        e_xl = carve(2048).rearrange("p (i d) -> p i d", i=TT)
        e_xT = carve(2048)
        e_acc = carve(2048).rearrange("p (i d) -> p i d", i=TT)
        e_h = carve(1024).rearrange("p (z t) -> p z t", z=2)
        e_back = carve(2048).rearrange("p (i d) -> p i d", i=TT)
        e_ohT = carve(2048)
        e_small = carve(8 * 128).rearrange("p (k i e) -> p k i e", k=8, i=TT)
        e_lg, e_ex, e_pr, e_oh, e_cand, e_tot, e_pre, e_pos = (e_small[:, k] for k in range(8))
        e_m = carve(6 * 16).rearrange("p (k i) -> p k i", k=6)
        e_eo = carve(8)
        e_idx = sb("e_idx", [P, TT], U32)

        names = """ln_out pow_in pow_out dve_step act_step stage_end xb_in xb_out
            a_xT_ps a_xT a_gate_ps a_gate_in a_decay a_gsum a_gamma a_proj a_sq a_vcopy a_norm
            a_tps a_tcopy a_kv a_state a_scores a_max a_exp a_prob a_pT_ps a_pT_in a_y_ps a_yT_in a_o
            f_yT_ps f_hT_in f_proj f_sq f_vcopy f_ss_in f_root f_rq f_rt f_rk f_q_ps f_q_in f_k_ps f_k_in
            f_sc_ps f_max f_exp f_pT_ps f_pT_a f_pT_b f_o_ps f_o_in f_oT_ps f_oT_in f_attn f_y f_sh f_h_in
            f_hnT_ps f_hnT_in f_up f_gelu f_mid f_down f_fin f_zero pool_step
            b_zero b_ms b_rn b_hn_in b_xT_ps b_hT b_lat_ps b_lat_in b_kvq b_qk_in b_rope b_tps b_qT_in b_kT_in
            b_s b_exp b_mask_p b_mask_v b_pv b_o_in b_rT b_div b_oT_ps b_oT_in b_out
            c_xT_ps c_xT c_proj c_qkv_in c_shift c_exp c_wts c_prod c_red c_sum c_os_in c_oT_ps c_oT_in c_out
            m_xT_ps m_xT m_proj m_sq m_qk_in m_tps m_kT_in m_qv_in m_s m_max m_exp m_tp m_pT_a m_pT_b m_pv
            m_os_in m_oT_ps m_oT_in m_out""".split()
        sems = {n: ctx.enter_context(nc.semaphore(n)) for n in names}
        s = type("Sems", (), sems)
        batch_go = ctx.enter_context(nc.semaphore("batch_go"))
        batch_done = ctx.enter_context(nc.semaphore("batch_done"))
        batch_seen = ctx.enter_context(nc.semaphore("batch_seen"))
        s_loaded = ctx.enter_context(nc.semaphore("s_loaded"))
        s_tabs = ctx.enter_context(nc.semaphore("s_tabs"))
        s_store = ctx.enter_context(nc.semaphore("s_store"))
        e_names = """e_ln e_xT_ps e_xT_in e_lg_ps e_shift e_expd e_probs e_rank_ps e_idx_in e_xsT_ps
            e_xsT_in e_oT_ps e_oT_in e_b2_ps e_b2_in e_up e_relu e_down e_acc_in e_sent e_back_in e_out""".split()
        es = type("ESems", (), {n: ctx.enter_context(nc.semaphore(n)) for n in e_names})

        block = ctx.enter_context(nc.Block())

        class Count:
            def __init__(self):
                self.n = 0

            def next(self):
                self.n += 1
                return self.n

        def chain(eng, sem, count):
            def after(ins):
                ins.then_inc(sem, 1)
                eng.wait_ge(sem, count.next())
            return after

        def stage_done(eng, k):
            eng.drain().then_inc(s.stage_end, 1)
            eng.wait_ge(s.stage_end, 4 * k)

        in_loop = ["f", "b", "f", "c"][:min(STAGES, 5) - 1]

        @block.tensor
        def _(pe):
            mm, tr = pe.matmul, pe.transpose

            def transposes(bank, src):
                for j in range(NT):
                    last = tr(ps[:, bank, j * P:(j + 1) * P], src(j), ident)
                return last

            def linear_attention(ln):
                pe.wait_ge(s.ln_out, ln)
                transposes(0, lambda j: Y[:, j, :]).then_inc(s.a_xT_ps, 1)
                pe.wait_ge(s.a_xT, 1)
                for j in range(NT):
                    last = mm(ps[:, 7, j * HA:(j + 1) * HA], xT[:, j * P:(j + 1) * P], W("a_wg"),
                              start=True, stop=True)
                last.then_inc(s.a_gate_ps, 1)

                def project(j):
                    if j >= 1:
                        pe.wait_ge(s.a_norm, j)
                        pe.wait_ge(s.a_vcopy, j)
                    for c in range(6):
                        last = mm(ps[:, c, :], xT[:, j * P:(j + 1) * P], W("a_qkv", 512 * c, 512 * c + 512),
                                  start=True, stop=True)
                    last.then_inc(s.a_proj, 1)

                def turn(j):
                    pe.wait_ge(s.a_norm, j + 1)
                    for g in range(4):
                        T = 4 * j + g
                        if T == 1:
                            pe.wait_ge(s.a_gate_in, 1)
                        if T >= 2:
                            pe.wait_ge(s.a_tcopy, T - 1)
                        for i in range(4):
                            h = 4 * (g % 2) + i
                            src = a_qn[:, h, :] if g < 2 else a_kn[:, j, h, :]
                            last = tr(ps[:, 6 + T % 2, i * P:(i + 1) * P], src, ident)
                        last.then_inc(s.a_tps, 1)

                project(0)
                for j in range(NT):
                    if j + 1 < NT:
                        project(j + 1)
                    turn(j)
                pe.wait_ge(s.a_decay, 1)
                for half in range(2):
                    last = mm(ps[:, 0, 32 * half:32 * half + 32], C("half%d" % half), a_gate[:, :],
                              start=True, stop=True)
                last.then_inc(s.a_gsum, 1)
                pe.wait_ge(s.a_gamma, 1)
                pe.wait_ge(s.a_vcopy, NT)
                pe.wait_ge(s.a_tcopy, 4 * NT)

                def outer(h):
                    if h >= 2:
                        pe.wait_ge(s.a_state, h - 1)
                    for n in range(NCH - 1):
                        j, r = n // 2, n % 2
                        last = mm(ps[:, 2 * (h % 2) + r, j * P:(j + 1) * P],
                                  a_kn[64 * r:64 * r + 64, j, h, :],
                                  a_v[64 * r:64 * r + 64, j, h * P:(h + 1) * P], start=True, stop=True)
                    last.then_inc(s.a_kv, 1)

                def scores(h):
                    if h >= 2:
                        pe.wait_ge(s.a_max, h - 1)
                    for j in range(NT):
                        last = mm(ps[:, 4 + h % 2, j * P:(j + 1) * P], a_qT[:, h, j * P:(j + 1) * P],
                                  a_kT[:, h, j * P:(j + 1) * P], start=True, stop=True)
                    last.then_inc(s.a_scores, 1)

                def turn_probs(h):
                    pe.wait_ge(s.a_prob, h + 1)
                    if h >= 1:
                        pe.wait_ge(s.a_pT_in, h)
                    for j in range(NT):
                        last = tr(ps[:, 6, j * P:(j + 1) * P], a_p[:, h % 2, j, :], ident)
                    last.then_inc(s.a_pT_ps, 1)

                def mix(h):
                    pe.wait_ge(s.a_pT_in, h + 1)
                    pe.wait_ge(s.a_state, h + 1)
                    if h >= 1:
                        pe.wait_ge(s.a_yT_in, h)
                    for j in range(NT):
                        mm(ps[:, 7, j * P:(j + 1) * P], a_v[:, j, h * P:(h + 1) * P], a_pT[:, j, :],
                           start=True, stop=True, skip_group_check=True)
                        for n in (2 * j, 2 * j + 1):
                            if n:
                                last = mm(ps[:, 7, n * CH:(n + 1) * CH], a_st[:, h % 2, n, :],
                                          a_qT[:, h, n * CH:(n + 1) * CH], start=False, stop=True,
                                          skip_group_check=True)
                    last.then_inc(s.a_y_ps, 1)

                for i in range(HA + 1):
                    if i < HA:
                        outer(i)
                        scores(i)
                    if i:
                        turn_probs(i - 1)
                        mix(i - 1)
                pe.wait_ge(s.a_yT_in, HA)
                for j in range(NT):
                    for h in range(HA):
                        last = mm(ps[:, 0, j * P:(j + 1) * P], a_yT[:, h, j * P:(j + 1) * P],
                                  W("a_wo", 128 * h, 128 * h + 128), start=h == 0, stop=h == HA - 1)
                last.then_inc(s.a_o, 1)

            def window_layer(k, l, ln):
                n0 = PAIR * k
                pe.wait_ge(s.ln_out, ln)
                if l:
                    pe.wait_ge(s.f_fin, 2 * k)
                for z in range(2):
                    transposes(z, lambda j: Y[:, NT * z + j, :]).then_inc(s.f_yT_ps, 1)
                pe.wait_ge(s.f_hT_in, 2 * k + 2)

                def project(n):
                    N, z, j = n0 + n, n % 2, n // 2
                    if n >= 1:
                        pe.wait_ge(s.f_q_in, N)
                        pe.wait_ge(s.f_k_in, N)
                        pe.wait_ge(s.f_vcopy, N)
                    if n >= 2:
                        pe.wait_ge(s.f_oT_in, N - 1)
                    for c in range(3):
                        last = mm(ps[:, c, :], f_hT[:, z, j * P:(j + 1) * P],
                                  W("f_wqkv", 1536 * l + 512 * c, 1536 * l + 512 * c + 512), start=True, stop=True)
                    last.then_inc(s.f_proj, 1)

                def turn_qk(n):
                    N = n0 + n
                    pe.wait_ge(s.f_sq, N + 1)
                    pe.wait_ge(s.f_rq, N + 1)
                    for c in range(4):
                        last = tr(ps[:, 0, c * P:(c + 1) * P], f_qr[:, c * P:(c + 1) * P], ident)
                    last.then_inc(s.f_q_ps, 1)
                    pe.wait_ge(s.f_rk, N + 1)
                    for c in range(4):
                        last = tr(ps[:, 1, c * P:(c + 1) * P], f_kr[:, c * P:(c + 1) * P], ident)
                    last.then_inc(s.f_k_ps, 1)

                def scores(n, g):
                    N, z, j = n0 + n, n % 2, n // 2
                    pe.wait_ge(s.f_q_in, N + 1)
                    pe.wait_ge(s.f_k_in, N + 1)
                    if 2 * N + g >= 1:
                        pe.wait_ge(s.f_max, 2 * N + g)
                    lo = 0 if j else WIN
                    for i in range(4):
                        h = 4 * g + i
                        rows = slice(64 * (h % 2), 64 * (h % 2) + 64)
                        at = KW * (i // 2)
                        last = mm(ps[:, 4 + h % 2, at + lo:at + KW], f_qT[rows, h // 2, :],
                                  f_kT[rows, z, h // 2, j * P - WIN + lo:(j + 1) * P], start=True, stop=True)
                    last.then_inc(s.f_sc_ps, 1)

                def turn_probs(n, g):
                    N, j = n0 + n, n // 2
                    pe.wait_ge(s.f_zero, k // 2 + 1)
                    pe.wait_ge(s.f_exp, 2 * N + g + 1)
                    if 2 * N + g:
                        pe.wait_ge(s.f_pT_a, 2 * N + g)
                    if N:
                        pe.wait_ge(s.f_pT_b, N)
                    for i in range(4):
                        for side in ((0, 1) if j else (1,)):
                            last = tr(ps[:, 6 + i // 2, 256 * (i % 2) + 128 * side:256 * (i % 2) + 128 * side + 128],
                                      f_p[:, 4 * g + i, 128 * side:128 * side + 128], ident)
                    last.then_inc(s.f_pT_ps, 1)

                def values(n, g):
                    N, z, j = n0 + n, n % 2, n // 2
                    pe.wait_ge(s.f_vcopy, N + 1)
                    pe.wait_ge(s.f_pT_a, 2 * N + g + 1)
                    if g:
                        pe.wait_ge(s.f_pT_b, N + 1)
                    if N:
                        pe.wait_ge(s.f_y, N)
                    for i in range(4):
                        h = 4 * g + i
                        o = ps[:, 3, h * DF:(h + 1) * DF]
                        last = mm(o, f_pT[:, h, 1, :], f_v[:, NT * z + j, h * DF:(h + 1) * DF], start=True, stop=j == 0)
                        if j:
                            last = mm(o, f_pT[:, h, 0, :], f_v[:, NT * z + j - 1, h * DF:(h + 1) * DF],
                                      start=False, stop=True)
                    last.then_inc(s.f_o_ps, 1)

                def turn_out(n):
                    N = n0 + n
                    pe.wait_ge(s.f_o_in, N + 1)
                    if n + 1 < PAIR:
                        pe.wait_ge(s.f_vcopy, N + 2)
                    if N:
                        pe.wait_ge(s.f_oT_in, N)
                    for c in range(4):
                        last = tr(ps[:, 2, c * P:(c + 1) * P], f_os[:, c * P:(c + 1) * P], ident)
                    last.then_inc(s.f_oT_ps, 1)

                def out_rows(n):
                    N = n0 + n
                    pe.wait_ge(s.f_oT_in, N + 1)
                    for c in range(4):
                        last = mm(ps[:, 3, 0:D], f_oT[:, c, :], W("f_wo", 512 * l + 128 * c, 512 * l + 128 * c + 128),
                                  start=c == 0, stop=c == 3)
                    last.then_inc(s.f_attn, 1)

                project(0)
                for n in range(-1, PAIR):
                    more = n + 1 < PAIR
                    if more:
                        turn_qk(n + 1)
                    if n >= 0:
                        turn_out(n)
                    if more:
                        scores(n + 1, 0)
                    if n >= 0:
                        out_rows(n)
                    if more:
                        scores(n + 1, 1)
                        if n + 2 < PAIR:
                            project(n + 2)
                        for g in range(2):
                            turn_probs(n + 1, g)
                            values(n + 1, g)
                pe.wait_ge(s.f_y, n0 + PAIR)
                for z in range(2):
                    for j in range(NT):
                        o = ps[:, z, 64 * j:64 * j + 64]
                        last = mm(o, C("shift"), Y[:, NT * z + j, 64:128], start=True, stop=j == 0)
                        if j:
                            last = mm(o, C("carry"), Y[:, NT * z + j - 1, 64:128], start=False, stop=True)
                    last.then_inc(s.f_sh, 1)
                for z in range(2):
                    pe.wait_ge(s.ln_out, ln + 2 * l + 1 + z)
                    transposes(z, lambda j: f_h[:, NT * z + j, :]).then_inc(s.f_hnT_ps, 1)
                for z in range(2):
                    pe.wait_ge(s.f_hnT_in, 2 * k + z + 1)
                    for c, m in enumerate(HID_C):
                        if z:
                            pe.wait_ge(s.f_mid, 6 * k + c + 1)
                        for a in range(2):
                            at = 2 * HID * l + HID * (1 - a) + 128 * c
                            last = mm(ps[0:m, 2 + 2 * c + a, :], W("f_w1", at, at + m), f_hnT[:, z, :],
                                      start=True, stop=True)
                        last.then_inc(s.f_up, 1)
                for z in range(2):
                    pe.wait_ge(s.f_mid, 6 * k + 3 * z + 3)
                    for j in range(NT):
                        for c, m in enumerate(HID_C):
                            at = 384 * l + 128 * c
                            last = mm(ps[:, z, j * P:(j + 1) * P], f_hm[0:m, z, c, j * P:(j + 1) * P],
                                      W("f_w2", at, at + 128)[0:m, :], start=c == 0, stop=c == 2)
                    last.then_inc(s.f_down, 1)

            def small_heads():
                def finish(t, i):
                    if 1 <= i <= 4:
                        r = i - 1
                        pe.wait_ge(s.b_o_in, 4 * t + i)
                        if r >= 2:
                            pe.wait_ge(s.b_div, 4 * t + r - 1)
                        transposes(4 + r % 2, lambda j: b_oR[:, r, j * P:(j + 1) * P]).then_inc(s.b_rT, 1)
                    elif i == 5:
                        pe.wait_ge(s.b_div, 4 * t + 4)
                        transposes(4, lambda j: b_os[:, j].rearrange("p g r d -> p (g r d)")).then_inc(s.b_oT_ps, 1)
                    elif i == 6:
                        pe.wait_ge(s.b_oT_in, t + 1)
                        for j in range(NT):
                            last = mm(ps[:, 5, j * P:(j + 1) * P], b_oT[:, j * P:(j + 1) * P],
                                      W("b_gwo" if t < 2 else "b_lwo"), start=True, stop=True)
                        last.then_inc(s.b_out, 1)

                def prepare(k, i):
                    glob = k < 2
                    if i == 8:
                        pe.wait_ge(s.b_hn_in, k + 1)
                        transposes(4, lambda j: b_hn[:, j, :]).then_inc(s.b_xT_ps, 1)
                    elif i == 9 and glob:
                        pe.wait_ge(s.b_hT, k + 1)
                        mm(ps[0:32, 5, :], W("b_down"), xT[:, :], start=True, stop=True).then_inc(s.b_lat_ps, 1)
                    elif i == 10:
                        pe.wait_ge(s.b_hT, k + 1)
                        if glob:
                            pe.wait_ge(s.b_lat_in, k + 1)
                        for j in range(NT):
                            t = slice(j * P, (j + 1) * P)
                            if glob:
                                mm(ps[:, 5, 64 * j:64 * j + 64], b_latT[0:32, t], W("b_up")[0:32, :],
                                   start=True, stop=True)
                            else:
                                mm(ps[:, 5, 64 * j:64 * j + 64], xT[:, t], W("b_lkv"), start=True, stop=True)
                            last = mm(ps[:, 4, t], xT[:, t], W("b_gq" if glob else "b_lq"), start=True, stop=True)
                        last.then_inc(s.b_kvq, 1)
                    elif i == 14:
                        pe.wait_ge(s.b_rope, k + 1)
                        transposes(4, lambda j: b_qr[:, j, 0:HB, :].rearrange("p h d -> p (h d)"))
                        transposes(5, lambda j: b_kr[:, j].rearrange("p g r d -> p (g r d)")).then_inc(s.b_tps, 1)

                def scores(k, u, j):
                    st = 32 * k + 4 * u + j
                    if 4 * u + j == 0:
                        pe.wait_ge(s.b_qT_in, k + 1)
                        pe.wait_ge(s.b_kT_in, k + 1)
                    if st >= 2:
                        pe.wait_ge(s.b_exp, st - 1)
                    n = small_width(k < 2, j)
                    r, gp = u // 2, u % 2
                    for hh in range(2):
                        g = 2 * gp + hh
                        rows = slice(32 * g, 32 * g + 32)
                        last = mm(ps[:, 2 * (st % 2) + hh, 0:n], b_kT[rows, k % 2, r, j * P:(j + 1) * P],
                                  b_qT[rows, k % 2, j * P:j * P + n], start=True, stop=True)
                    last.then_inc(s.b_s, 1)

                def values(k, u, hh):
                    U, glob = 8 * k + u, k < 2
                    r, gp = u // 2, u % 2
                    pe.wait_ge(s.b_mask_p, 2 * U + 2)
                    pe.wait_ge(s.b_mask_v, 2 * U + 2)
                    first = gp == 0 and hh == 0
                    if first and U >= 4:
                        pe.wait_ge(s.b_o_in, U // 2 - 1)
                    g = 2 * gp + hh
                    for j in range(NT):
                        n, at = small_width(glob, j), small_at(glob, j)
                        last = mm(ps[:, 6 + r % 2, j * P:j * P + n],
                                  b_vx[:, k % 2, j, P * g:P * g + P], b_p[:, u % 2, hh, at:at + n],
                                  start=first and j == 0, stop=True, skip_group_check=True)
                    if hh:
                        last.then_inc(s.b_pv, 1)

                for i in range(16):
                    prepare(0, i)
                for U in range(33):
                    k, u = U // 8, U % 8
                    for half in range(2):
                        if U < 32:
                            scores(k, u, 2 * half)
                            scores(k, u, 2 * half + 1)
                        if U:
                            values((U - 1) // 8, (U - 1) % 8, half)
                        if U < 32:
                            if k >= 1:
                                finish(k - 1, 2 * u + half)
                            if k < 3:
                                prepare(k + 1, 2 * u + half)
                for i in range(16):
                    finish(3, i)

            def head_attention(ln, z):
                pe.wait_ge(s.ln_out, ln)
                if z:
                    pe.wait_ge(s.c_sum, z)
                transposes(0, lambda j: Y[:, NT * z + j, :]).then_inc(s.c_xT_ps, 1)
                pe.wait_ge(s.c_xT, z + 1)
                for j in range(NT):
                    last = mm(ps[:, 1 + j, 0:384], xT[:, j * P:(j + 1) * P], W("c_qkv"), start=True, stop=True)
                last.then_inc(s.c_proj, 1)
                pe.wait_ge(s.c_os_in, z + 1)
                transposes(0, lambda j: c_os[:, j * P:(j + 1) * P]).then_inc(s.c_oT_ps, 1)
                pe.wait_ge(s.c_oT_in, z + 1)
                for j in range(NT):
                    last = mm(ps[:, 5, j * P:(j + 1) * P], c_oT[:, j * P:(j + 1) * P], W("c_fc"),
                              start=True, stop=True)
                last.then_inc(s.c_out, 1)

            def full_attention(ln):
                pe.wait_ge(s.ln_out, ln)
                transposes(0, lambda j: Y[:, j, :]).then_inc(s.m_xT_ps, 1)
                pe.wait_ge(s.m_xT, 1)
                for j in range(NT):
                    for c in range(3):
                        last = mm(ps[:, 1 + c, j * P:(j + 1) * P], xT[:, j * P:(j + 1) * P],
                                  W("d_qkv", 128 * c, 128 * c + 128), start=True, stop=True)
                last.then_inc(s.m_proj, 1)
                pe.wait_ge(s.m_qk_in, 1)
                transposes(4, lambda j: m_qk[:, j, 0:128])
                transposes(5, lambda j: m_qk[:, j, 128:256]).then_inc(s.m_tps, 1)
                pe.wait_ge(s.m_qv_in, 1)
                pe.wait_ge(s.m_kT_in, 1)
                steps, dv = full_steps(), DF

                def scores(st):
                    if st >= 2:
                        pe.wait_ge(s.m_exp, st - 1)
                    i, hs = steps[st]
                    for hh, (h, rows) in enumerate(hs):
                        last = mm(ps[:, 2 * (st % 2) + hh, :], m_qT[rows, i * P:(i + 1) * P], m_kT[rows, :],
                                  start=True, stop=True)
                    last.then_inc(s.m_s, 1)

                def turn(st):
                    pe.wait_ge(s.m_exp, st + 1)
                    if st:
                        pe.wait_ge(s.m_pT_a, st)
                        pe.wait_ge(s.m_pT_b, st)
                    for hh in range(2):
                        for j in range(NT):
                            last = tr(ps[:, 4 + hh, j * P:(j + 1) * P], m_p[:, st % 2, hh, j * P:(j + 1) * P], ident)
                    last.then_inc(s.m_tp, 1)

                def values(st):
                    pe.wait_ge(s.m_pT_a, st + 1)
                    pe.wait_ge(s.m_pT_b, st + 1)
                    i, hs = steps[st]
                    for hh, (h, _) in enumerate(hs):
                        for j in range(NT):
                            last = mm(ps[:, 6, i * P + h * dv:i * P + (h + 1) * dv], m_pT[:, hh, j, :],
                                      m_v[:, j, h * dv:(h + 1) * dv], start=j == 0, stop=j == NT - 1)
                    last.then_inc(s.m_pv, 1)

                for st in range(len(steps) + 1):
                    if st < len(steps):
                        scores(st)
                    if st:
                        turn(st - 1)
                        values(st - 1)
                pe.wait_ge(s.m_os_in, 1)
                transposes(0, lambda j: m_os[:, j * P:(j + 1) * P]).then_inc(s.m_oT_ps, 1)
                pe.wait_ge(s.m_oT_in, 1)
                for j in range(NT):
                    last = mm(ps[:, 1, j * P:(j + 1) * P], m_oT[:, j * P:(j + 1) * P], W("d_wo"), start=True, stop=True)
                last.then_inc(s.m_out, 1)

            def experts(k):
                def all_turned(src, ps_sem, in_sem, base):
                    for c in range(NB):
                        if c >= 2:
                            pe.wait_ge(in_sem, base + c - 1)
                        transposes(c % 2, lambda j: src[:, NT * c + j, :]).then_inc(ps_sem, 1)

                pe.wait_ge(es.e_ln, k + 1)
                all_turned(e_xl, es.e_xT_ps, es.e_xT_in, NB * k)
                pe.wait_ge(es.e_xT_in, NB * (k + 1))
                for i in range(TT):
                    last = mm(ps[:, 2, E * i:E * i + E], e_xT[:, i * P:(i + 1) * P], W("e_ws"), start=True, stop=True)
                last.then_inc(es.e_lg_ps, 1)
                pe.wait_ge(es.e_probs, k + 1)
                oh = e_oh.rearrange("p i e -> p (i e)")
                mm(ps[:, 3, 0:128], C("before"), oh, start=True, stop=True)
                mm(ps[:, 3, 128:256], C("ones"), oh, start=True, stop=True).then_inc(es.e_rank_ps, 1)
                all_turned(e_xl, es.e_xsT_ps, es.e_xsT_in, NB * k)
                for c in range(NB):
                    for j in range(NT):
                        last = tr(ps[0:E, 4 + c, j * P:(j + 1) * P], e_oh[:, NT * c + j, :], ident)
                last.then_inc(es.e_oT_ps, 1)
                pe.wait_ge(es.e_oT_in, k + 1)
                for c in range(NB):
                    for j in range(NT):
                        i = NT * c + j
                        last = mm(ps[:, 4 + c, j * P:(j + 1) * P], e_ohT[0:E, i * P:(i + 1) * P],
                                  W("e_b2")[0:E, :], start=True, stop=True)
                last.then_inc(es.e_b2_ps, 1)
                pe.wait_ge(es.e_b2_in, k + 1)
                pe.wait_ge(es.e_xsT_in, NB * (k + 1))
                n = E * NB

                def up(q):
                    e, c = q // NB, q % NB
                    if q >= 2:
                        pe.wait_ge(es.e_relu, n * k + q - 1)
                    mm(ps[:, 4 + q % 2, :], W("e_w1", 128 * e, 128 * e + 128), e_xT[:, c * 512:(c + 1) * 512],
                       start=True, stop=True).then_inc(es.e_up, 1)

                def down(q):
                    e = q // NB
                    pe.wait_ge(es.e_relu, n * k + q + 1)
                    if q >= 2:
                        pe.wait_ge(es.e_acc_in, n * k + q - 1)
                    for j in range(NT):
                        last = mm(ps[:, 6 + q % 2, j * P:(j + 1) * P], e_h[:, q % 2, j * P:(j + 1) * P],
                                  W("e_w2", 128 * e, 128 * e + 128), start=True, stop=True)
                    last.then_inc(es.e_down, 1)

                for q in range(n + 1):
                    if q < n:
                        up(q)
                    if q:
                        down(q - 1)

            def stages(which):
                ln = f = 0
                for i, st in enumerate(which):
                    if st == "a":
                        ln += 1
                        linear_attention(ln)
                    elif st == "f":
                        for l in range(2):
                            window_layer(f, l, ln + 1)
                            f += 1
                        ln += 5
                    elif st == "b":
                        small_heads()
                    elif st == "c":
                        ln += 1
                        for z in range(2):
                            head_attention(ln, z)
                    else:
                        ln += 2
                        full_attention(ln)
                    stage_done(pe, i + 1)

            pe.wait_ge(s_loaded, 64)
            with pe.Fori(0, NB) as b:
                pe.wait_ge(batch_go, b + 1)
                pe.sem_inc(batch_seen, 1)
                stages(["a"])
                pe.drain().then_inc(batch_done, 1)
            if STAGES >= 2:
                with pe.Fori(0, NP) as b:
                    pe.wait_ge(batch_go, b + NB + 1)
                    pe.sem_inc(batch_seen, 1)
                    stages(in_loop)
                    pe.drain().then_inc(batch_done, 1)
            if STAGES >= 6:
                pe.wait_ge(batch_go, NB + NP + 1)
                pe.sem_inc(batch_seen, 1)
                experts(0)
            if STAGES >= 7:
                with pe.Fori(0, NB) as b:
                    pe.wait_ge(batch_go, b + NB + NP + 2)
                    pe.sem_inc(batch_seen, 1)
                    stages(["d"])
                    pe.drain().then_inc(batch_done, 1)
            if STAGES >= 8:
                pe.wait_ge(batch_go, 2 * NB + NP + 2)
                pe.sem_inc(batch_seen, 1)
                experts(1)

        @block.scalar
        def _(act):
            steps_done = Count()
            after = chain(act, s.act_step, steps_done)
            copy = lambda o, i: act.activation(o, i, ACT.Copy)

            def linear_attention():
                act.wait_ge(s.a_xT_ps, 1)
                copy(xT[:, :], ps[:, 0, :]).then_inc(s.a_xT, 1)

                def squares(j):
                    act.wait_ge(s.a_proj, j + 1)
                    act.activation(a_sqr.rearrange("p (b n) -> p b n", b=4), ps[:, 0:4, :], ACT.Square)\
                        .then_inc(s.a_sq, 1)
                    copy(a_v[:, j, :].rearrange("p (b n) -> p b n", b=2), ps[:, 4:6, :]).then_inc(s.a_vcopy, 1)

                act.wait_ge(s.a_gate_in, 1)
                after(act.activation(a_gate[:, :], a_gate[:, :], ACT.Exp, scale=-1.0))
                act.activation(a_gate[:, :], a_gate[:, :], ACT.Ln, bias=1.0).then_inc(s.a_decay, 1)
                squares(0)
                for j in range(NT):
                    if j + 1 < NT:
                        squares(j + 1)
                    for g in range(2):
                        T = 4 * j + g
                        act.wait_ge(s.a_tps, T + 1)
                        if T:
                            act.wait_ge(s.a_tcopy, T)
                        copy(a_qT[:, 4 * g:4 * g + 4, j * P:(j + 1) * P],
                             ps[:, 6 + T % 2, :].rearrange("p (h t) -> p h t", h=4)).then_inc(s.a_tcopy, 1)
                act.wait_ge(s.a_gsum, 1)
                act.activation(a_gam[:, :, :, :],
                               ps[:, 0, 0:64].rearrange("p (z j h) -> p z j h", z=2, j=NT), ACT.Exp, scale=-1.0)\
                    .then_inc(s.a_gamma, 1)
                for i in range(HA + 1):
                    if i < HA:
                        act.wait_ge(s.a_max, i + 1)
                        if i >= 2:
                            act.wait_ge(s.a_pT_ps, i - 1)
                        for j in range(NT):
                            c = 4 * (i % 2) + j
                            last = act.activation(a_p[:, i % 2, j, :], a_sc[:, i % 2, j, :], ACT.Exp,
                                                  bias=nma[:, c:c + 1], scale=float(P) ** -0.5,
                                                  accum_out=rsa[:, c:c + 1])
                        last.then_inc(s.a_exp, 1)
                    if i:
                        h = i - 1
                        act.wait_ge(s.a_pT_ps, h + 1)
                        if h:
                            act.wait_ge(s.a_y_ps, h)
                        copy(a_pT[:, :, :], ps[:, 6, :].rearrange("p (j t) -> p j t", j=NT)).then_inc(s.a_pT_in, 1)
                        act.wait_ge(s.a_y_ps, h + 1)
                        copy(a_yT[:, h, :], ps[:, 7, :]).then_inc(s.a_yT_in, 1)

            def window_layer(k, l):
                n0 = PAIR * k

                def squares(n):
                    N = n0 + n
                    act.wait_ge(s.f_proj, N + 1)
                    if N:
                        act.wait_ge(s.f_rq, N)
                    act.activation(f_sqr.rearrange("p (b n) -> p b n", b=2), ps[:, 0:2, :], ACT.Square)\
                        .then_inc(s.f_sq, 1)

                def keep_values(n):
                    act.wait_ge(s.f_proj, n0 + n + 1)
                    copy(f_v[:, NT * (n % 2) + n // 2, :], ps[:, 2, :]).then_inc(s.f_vcopy, 1)

                def keep_qk(n):
                    N, z, j = n0 + n, n % 2, n // 2
                    act.wait_ge(s.f_q_ps, N + 1)
                    if N:
                        act.wait_ge(s.f_sc_ps, 2 * N)
                    copy(f_qT, ps[:, 0, :].rearrange("p (c t) -> p c t", c=4)).then_inc(s.f_q_in, 1)
                    act.wait_ge(s.f_k_ps, N + 1)
                    copy(f_kT[:, z, :, j * P:(j + 1) * P], ps[:, 1, :].rearrange("p (c t) -> p c t", c=4))\
                        .then_inc(s.f_k_in, 1)

                def keep_out(n):
                    N = n0 + n
                    act.wait_ge(s.f_oT_ps, N + 1)
                    if N:
                        act.wait_ge(s.f_attn, N)
                    copy(f_oT, ps[:, 2, :].rearrange("p (c t) -> p c t", c=4)).then_inc(s.f_oT_in, 1)

                def exps(n, g):
                    N = n0 + n
                    lo = 0 if n // 2 else WIN
                    act.wait_ge(s.f_max, 2 * N + g + 1)
                    if N:
                        act.wait_ge(s.f_pT_ps, 2 * N + g - 1)
                    for i in range(4):
                        h = 4 * g + i
                        last = act.activation(f_p[:, h, 64 + lo:256], f_sc[:, h, lo:KW], ACT.Exp,
                                              bias=f_nm[:, h:h + 1], accum_out=f_rs[:, n % 2, h:h + 1])
                    last.then_inc(s.f_exp, 1)

                def keep_probs(n, g):
                    N = n0 + n
                    act.wait_ge(s.f_pT_ps, 2 * N + g + 1)
                    if N:
                        act.wait_ge(s.f_o_ps, 2 * N + g - 1)
                    side = 0 if n // 2 else 1
                    for i in range(2 - g):
                        last = copy(f_pT[:, 4 * g + 2 * i:4 * g + 2 * i + 2, side:2, :],
                                    ps[:, 6 + i, :].rearrange("p (h s t) -> p h s t", h=2, s=2)[:, :, side:2, :])
                    last.then_inc(s.f_pT_a, 1)

                squares(0)
                keep_values(0)
                for n in range(-1, PAIR):
                    more, far = n + 1 < PAIR, n + 2 < PAIR
                    if more:
                        keep_qk(n + 1)
                    if n >= 0:
                        keep_out(n)
                    if more:
                        exps(n + 1, 0)
                        if far:
                            squares(n + 2)
                        exps(n + 1, 1)
                        if far:
                            keep_values(n + 2)
                        keep_probs(n + 1, 0)
                        keep_probs(n + 1, 1)
                for z in range(2):
                    act.wait_ge(s.f_sh, 2 * k + z + 1)
                    t = slice(NT * z, NT * z + NT)
                    copy(f_h[:, t, 0:64], Y[:, t, 0:64])
                    copy(f_h[:, t, 64:128], ps[:, z, 0:256].rearrange("p (j d) -> p j d", j=NT)).then_inc(s.f_h_in, 1)
                for z in range(2):
                    act.wait_ge(s.f_hnT_ps, 2 * k + z + 1)
                    act.activation(f_hnT[:, z, :], ps[:, z, :], ACT.Identity, scale=W("f_cols", 8 * l, 8 * l + 1),
                                   bias=W("f_cols", 8 * l + 1, 8 * l + 2)).then_inc(s.f_hnT_in, 1)
                for z in range(2):
                    for c, m in enumerate(HID_C):
                        act.wait_ge(s.f_up, 6 * k + 3 * z + c + 1)
                        bias = W("f_cols", 8 * l + 2 + c, 8 * l + 3 + c)
                        act.activation(f_gb[0:m, c, :], ps[0:m, 2 + 2 * c, :], ACT.Gelu, bias=bias[0:m, :])\
                            .then_inc(s.f_gelu, 1)

            def small_heads():
                def finish(t, i):
                    if i == 5:
                        act.wait_ge(s.b_oT_ps, t + 1)
                        copy(b_oT, ps[:, 4, :]).then_inc(s.b_oT_in, 1)

                def inverse_root(n, k):
                    act.wait_ge(s.b_ms, k)
                    after(act.activation(rstd[:, 0:n], rstd[:, 0:n], ACT.Ln))
                    act.activation(rstd[:, 0:n], rstd[:, 0:n], ACT.Exp, scale=-0.5).then_inc(s.b_rn, 1)

                def prepare(k, i):
                    glob = k < 2
                    if i == 7:
                        inverse_root(NT, 2 * k + 1)
                    elif i == 8:
                        act.wait_ge(s.b_xT_ps, k + 1)
                        act.activation(xT[:, :], ps[:, 4, :], ACT.Copy, scale=W("b_norm", 1 - glob, 2 - glob))\
                            .then_inc(s.b_hT, 1)
                    elif i == 9 and glob:
                        act.wait_ge(s.b_lat_ps, k + 1)
                        copy(b_latT[0:32, :], ps[0:32, 5, :]).then_inc(s.b_lat_in, 1)
                    elif i == 10:
                        act.wait_ge(s.b_kvq, k + 1)
                        act.wait_ge(s.b_zero, 1)
                        kv = ps[:, 5, 0:256].rearrange("p (j n) -> p j n", j=NT)
                        copy(b_qk[:, :, 0:HB, :], ps[:, 4, :].rearrange("p (j h d) -> p j h d", j=NT, h=HB))
                        copy(b_qk[:, :, HB:20, :], kv[:, :, 0:32].rearrange("p j (h d) -> p j h d", h=NG))
                        copy(b_vx[:, k % 2].rearrange("p j (g n) -> p j g n", g=NG)[:, :, :, 0:HD],
                             kv[:, :, 32:64].rearrange("p j (h d) -> p j h d", h=NG)).then_inc(s.b_qk_in, 1)
                    elif i == 12:
                        inverse_root(80, 2 * k + 2)
                    elif i == 14:
                        act.wait_ge(s.b_tps, k + 1)
                        copy(b_qT[:, k % 2], ps[:, 4, :]).then_inc(s.b_qT_in, 1)

                for i in range(16):
                    prepare(0, i)
                for U in range(32):
                    k, u = U // 8, U % 8
                    if U >= 2:
                        act.wait_ge(s.b_pv, U - 1)
                    for j in range(NT):
                        st = 4 * U + j
                        act.wait_ge(s.b_s, st + 1)
                        n, at, b = small_width(k < 2, j), small_at(k < 2, j), 2 * (st % 2)
                        act.activation(b_p[:, u % 2, :, at:at + n], ps[:, b:b + 2, 0:n], ACT.Exp,
                                       scale=float(HD) ** -0.5).then_inc(s.b_exp, 1)
                        if j % 2:
                            if k >= 1:
                                finish(k - 1, 2 * u + j // 2)
                            if k < 3:
                                prepare(k + 1, 2 * u + j // 2)
                for i in range(16):
                    finish(3, i)

            def head_attention(z):
                act.wait_ge(s.c_xT_ps, z + 1)
                copy(xT[:, :], ps[:, 0, :]).then_inc(s.c_xT, 1)
                act.wait_ge(s.c_proj, z + 1)
                copy(c_qkv, ps[:, 1:1 + NT, 0:384]).then_inc(s.c_qkv_in, 1)
                for j in range(NT):
                    u = NT * z + j
                    act.wait_ge(s.c_shift, u + 1)
                    if u >= 2:
                        act.wait_ge(s.c_prod, u - 1)
                    act.activation(c_e[:, j % 2], c_sc[:, j % 2], ACT.Exp, scale=float(HD) ** -0.5)\
                        .then_inc(s.c_exp, 1)
                act.wait_ge(s.c_oT_ps, z + 1)
                copy(c_oT, ps[:, 0, :]).then_inc(s.c_oT_in, 1)

            def full_attention():
                act.wait_ge(s.m_xT_ps, 1)
                act.activation(xT[:, :], ps[:, 0, :], ACT.Identity, scale=W("d_cols", 0, 1),
                               bias=W("d_cols", 1, 2)).then_inc(s.m_xT, 1)
                act.wait_ge(s.m_proj, 1)
                act.activation(m_sq.rearrange("p (b n) -> p b n", b=2), ps[:, 1:3, :], ACT.Square)\
                    .then_inc(s.m_sq, 1)
                copy(m_v, ps[:, 3, :].rearrange("p (j n) -> p j n", j=NT))
                act.wait_ge(s.m_tps, 1)
                act.activation(m_qT, ps[:, 4, :], ACT.Copy, scale=W("d_cols", 2, 3)).then_inc(s.m_qv_in, 1)
                steps, heads = full_steps(), 2
                scale = float(DF) ** -0.5
                for st in range(len(steps) + 1):
                    if st < len(steps):
                        i, hs = steps[st]
                        act.wait_ge(s.m_max, st + 1)
                        for hh, (h, _) in enumerate(hs):
                            c = 2 * (st % 2) + hh
                            last = act.activation(m_p[:, st % 2, hh, :], ps[:, 2 * (st % 2) + hh, :], ACT.Exp,
                                                  bias=nma[:, c:c + 1], scale=scale,
                                                  accum_out=m_rs[:, i * heads + h:i * heads + h + 1])
                        last.then_inc(s.m_exp, 1)
                    if st:
                        act.wait_ge(s.m_tp, st)
                        if st >= 2:
                            act.wait_ge(s.m_pv, st - 1)
                        copy(m_pT[:, 0], ps[:, 4, :].rearrange("p (j t) -> p j t", j=NT)).then_inc(s.m_pT_a, 1)
                act.wait_ge(s.m_oT_ps, 1)
                copy(m_oT, ps[:, 0, :]).then_inc(s.m_oT_in, 1)

            def experts(k):
                for c in range(NB):
                    act.wait_ge(es.e_xT_ps, NB * k + c + 1)
                    copy(e_xT[:, c * 512:(c + 1) * 512], ps[:, c % 2, :]).then_inc(es.e_xT_in, 1)
                act.wait_ge(es.e_shift, k + 1)
                act.activation(e_ex, e_lg, ACT.Exp).then_inc(es.e_expd, 1)
                for c in range(NB):
                    act.wait_ge(es.e_xsT_ps, NB * k + c + 1)
                    copy(e_xT[:, c * 512:(c + 1) * 512], ps[:, c % 2, :]).then_inc(es.e_xsT_in, 1)
                act.wait_ge(es.e_oT_ps, k + 1)
                copy(e_ohT[0:E, :].rearrange("p (b n) -> p b n", b=4), ps[0:E, 4:8, :]).then_inc(es.e_oT_in, 1)
                act.wait_ge(es.e_b2_ps, k + 1)
                copy(e_acc.rearrange("p i d -> p (i d)").rearrange("p (b n) -> p b n", b=4), ps[:, 4:8, :])\
                    .then_inc(es.e_b2_in, 1)
                n = E * NB
                for q in range(n):
                    e = q // NB
                    act.wait_ge(es.e_up, n * k + q + 1)
                    if q >= 2:
                        act.wait_ge(es.e_down, n * k + q - 1)
                    act.activation(e_h[:, q % 2, :], ps[:, 4 + q % 2, :], ACT.Relu, bias=W("e_b1", e, e + 1))\
                        .then_inc(es.e_relu, 1)

            def stages(which):
                f = 0
                for i, st in enumerate(which):
                    if st == "a":
                        linear_attention()
                    elif st == "f":
                        for l in range(2):
                            window_layer(f, l)
                            f += 1
                    elif st == "b":
                        small_heads()
                    elif st == "c":
                        for z in range(2):
                            head_attention(z)
                    else:
                        full_attention()
                    stage_done(act, i + 1)

            act.wait_ge(s_loaded, 64)
            with act.Fori(0, NB) as b:
                act.wait_ge(batch_go, b + 1)
                act.sem_inc(batch_seen, 1)
                steps_done.n = 0
                stages(["a"])
                act.drain().then_inc(batch_done, 1)
            if STAGES >= 2:
                with act.Fori(0, NP) as b:
                    act.wait_ge(batch_go, b + NB + 1)
                    act.sem_inc(batch_seen, 1)
                    steps_done.n = 0
                    stages(in_loop)
                    act.drain().then_inc(batch_done, 1)
            if STAGES >= 6:
                act.wait_ge(batch_go, NB + NP + 1)
                act.sem_inc(batch_seen, 1)
                experts(0)
            if STAGES >= 7:
                with act.Fori(0, NB) as b:
                    act.wait_ge(batch_go, b + NB + NP + 2)
                    act.sem_inc(batch_seen, 1)
                    stages(["d"])
                    act.drain().then_inc(batch_done, 1)
            if STAGES >= 8:
                act.wait_ge(batch_go, 2 * NB + NP + 2)
                act.sem_inc(batch_seen, 1)
                experts(1)

        @block.vector
        def _(dve):
            steps_done, asked = Count(), Count()
            after = chain(dve, s.dve_step, steps_done)
            tt, ts, stt = dve.tensor_tensor, dve.tensor_scalar, dve.scalar_tensor_tensor

            def root(n, ins):
                ins.then_inc(s.pow_in, 1)
                asked.next()

            def rooted():
                dve.wait_ge(s.pow_out, asked.n)

            def layer_norm(src, dst, n, eps):
                for i in range(n):
                    last = dve.bn_stats(stats[:, i, :], src[:, i, :])
                after(last)
                for i in range(n):
                    last = dve.bn_aggr(mv[:, i, :], stats[:, i, :])
                after(last)
                root(n, ts(rstd[:, 0:n], mv[:, 0:n, 1], eps, None, ALU.add))
                rooted()
                for i in range(n):
                    last = ts(dst[:, i, :], src[:, i, :], mv[:, i, 0:1], rstd[:, i:i + 1], ALU.subtract, ALU.mult)
                return last

            def wide(ap, shape, axis):
                return ap.unsqueeze(axis).broadcast_to(shape)

            def linear_attention():
                layer_norm(XB[:, 0:NT, :], Y[:, 0:NT, :], NT, EPS5).then_inc(s.ln_out, 1)
                dve.wait_ge(s.a_gate_ps, 1)
                z = a_gate[:, :].rearrange("p (j h) -> p j h", j=NT)
                after(tt(z, ps[:, 7, 0:32].rearrange("p (j h) -> p j h", j=NT), wide(R("bg"), [P, NT, HA], 1), ALU.add))
                ts(a_gate[:, :], a_gate[:, :], -43.0, None, ALU.max).then_inc(s.a_gate_in, 1)

                def normalise(j):
                    dve.wait_ge(s.a_sq, j + 1)
                    if j:
                        dve.wait_ge(s.a_tps, 4 * j - 2)
                    after(dve.tensor_reduce(rstd[:, 0:16], a_sqr.rearrange("p (h d) -> p h d", h=16), AX, ALU.add))
                    root(16, ts(rstd[:, 0:16], rstd[:, 0:16], 1.0 / P, EPS6, ALU.mult, ALU.add))
                    rooted()
                    after(ts(small[:, 4, :], rstd[:, 0:16], 1.0, None, ALU.mult))
                    after(ts(small[:, 4, 0:8], small[:, 4, 0:8], R("gain"), None, ALU.mult))
                    view = lambda a: ps[:, a:a + 2, :].rearrange("p b (h d) -> p (b h) d", d=P)
                    tt(a_qn, view(0), wide(small[:, 4, 0:8], [P, HA, P], 2), ALU.mult)
                    tt(a_kn[:, j], view(2), wide(small[:, 4, 8:16], [P, HA, P], 2), ALU.mult).then_inc(s.a_norm, 1)

                normalise(0)
                for j in range(NT):
                    for g in (2, 3):
                        T = 4 * j + g
                        dve.wait_ge(s.a_tps, T + 1)
                        dve.wait_ge(s.a_tcopy, T)
                        dve.tensor_copy(a_kT[:, 4 * (g - 2):4 * (g - 2) + 4, j * P:(j + 1) * P],
                                        ps[:, 6 + T % 2, :].rearrange("p (h t) -> p h t", h=4))\
                            .then_inc(s.a_tcopy, 1)
                    if j + 1 < NT:
                        normalise(j + 1)
                dve.wait_ge(s.a_gamma, 1)

                def state(h):
                    dve.wait_ge(s.a_kv, h + 1)
                    if h >= 2:
                        dve.wait_ge(s.a_y_ps, h - 1)
                    kv = lambda n: ps[:, 2 * (h % 2) + n % 2, (n // 2) * P:(n // 2 + 1) * P]
                    after(dve.tensor_copy(a_st[:, h % 2, 1, :], kv(0)))
                    for n in range(1, NCH - 1):
                        ins = stt(a_st[:, h % 2, n + 1, :], a_st[:, h % 2, n, :], a_gam[:, n % 2, n // 2, h:h + 1],
                                  kv(n), ALU.mult, ALU.add)
                        if n < NCH - 2:
                            after(ins)
                    ins.then_inc(s.a_state, 1)

                def maxima(h):
                    dve.wait_ge(s.a_scores, h + 1)
                    c = 4 * (h % 2)
                    for j in range(NT):
                        ins = dve.tensor_tensor_reduce(a_sc[:, h % 2, j, :], ps[:, 4 + h % 2, j * P:(j + 1) * P],
                                                       C("mask_a"), 1.0, -3e38, ALU.add, ALU.max,
                                                       mxa[:, c + j:c + j + 1])
                    after(ins)
                    ts(nma[:, c:c + 4], mxa[:, c:c + 4], -float(P) ** -0.5, None, ALU.mult).then_inc(s.a_max, 1)

                def divide(h):
                    dve.wait_ge(s.a_exp, h + 1)
                    c = 4 * (h % 2)
                    after(dve.reciprocal(ria[:, c:c + 4], rsa[:, c:c + 4]))
                    tt(a_p[:, h % 2], a_p[:, h % 2], wide(ria[:, c:c + 4], [P, NT, P], 2), ALU.mult)\
                        .then_inc(s.a_prob, 1)

                for i in range(HA + 1):
                    if i < HA:
                        maxima(i)
                    if i:
                        divide(i - 1)
                    if i < HA:
                        state(i)
                dve.wait_ge(s.a_o, 1)
                after(tt(XB[:, 0:NT, :], XB[:, 0:NT, :], ps[:, 0, :].rearrange("p (j d) -> p j d", j=NT), ALU.add))

            def window_layer(k, l):
                n0 = PAIR * k
                heads = lambda t: t.rearrange("p (h d) -> p h d", h=HF)
                for z in range(2):
                    dve.wait_ge(s.f_yT_ps, 2 * k + z + 1)
                    dve.tensor_copy(f_hT[0:64, z, :], ps[0:64, z, :])
                    dve.tensor_copy(f_hT[64:128, z, 1:S], ps[64:128, z, 0:S - 1]).then_inc(s.f_hT_in, 1)

                def rope(n):
                    N, j = n0 + n, n // 2
                    table = lambda i: wide(tabs[:, l, i, j * DF:(j + 1) * DF], [P, HF, DF], 1)
                    dve.wait_ge(s.f_sq, N + 1)
                    tt(heads(f_t1), heads(ps[:, 0, :]), table(0), ALU.mult)
                    tt(heads(f_t2), heads(ps[:, 0, :]), table(1), ALU.mult)
                    after(dve.tensor_reduce(f_ss[:, :], f_sqr.rearrange("p (h d) -> p h d", h=16), AX, ALU.add))
                    ts(f_ss[:, :], f_ss[:, :], 1e-24, None, ALU.max).then_inc(s.f_ss_in, 1)
                    tt(heads(f_t3), heads(ps[:, 1, :]), table(2), ALU.mult)
                    tt(heads(f_t4), heads(ps[:, 1, :]), table(3), ALU.mult).then_inc(s.f_rt, 1)
                    tt(heads(f_qr)[:, :, 0:32], heads(f_t1)[:, :, 0:32], heads(f_t2)[:, :, 32:64], ALU.add)
                    tt(heads(f_qr)[:, :, 32:64], heads(f_t1)[:, :, 32:64], heads(f_t2)[:, :, 0:32], ALU.add)\
                        .then_inc(s.f_rq, 1)

                def maxima(n, g):
                    N = n0 + n
                    dve.wait_ge(s.f_sc_ps, 2 * N + g + 1)
                    dve.wait_ge(s.f_root, N + 1)
                    lo = 0 if n // 2 else WIN
                    for i in range(4):
                        h = 4 * g + i
                        at = KW * (i // 2)
                        ins = dve.tensor_tensor_reduce(f_sc[:, h, lo:KW], ps[:, 4 + h % 2, at + lo:at + KW],
                                                       C("mask_f", lo, KW), f_ss[:, h:h + 1], -3e38, ALU.add, ALU.max,
                                                       f_mx[:, h:h + 1])
                    after(ins)
                    ts(f_nm[:, 4 * g:4 * g + 4], f_mx[:, 4 * g:4 * g + 4], -1.0, None, ALU.mult).then_inc(s.f_max, 1)

                def add_out(n):
                    i = NT * (n % 2) + n // 2
                    dve.wait_ge(s.f_attn, n0 + n + 1)
                    tt(Y[:, i, :], Y[:, i, :], ps[:, 3, 0:D], ALU.add).then_inc(s.f_y, 1)

                def keep_probs(n):
                    N = n0 + n
                    dve.wait_ge(s.f_pT_ps, 2 * N + 2)
                    if N:
                        dve.wait_ge(s.f_o_ps, 2 * N)
                    side = 0 if n // 2 else 1
                    dve.tensor_copy(f_pT[:, 6:8, side:2, :],
                                    ps[:, 7, :].rearrange("p (h s t) -> p h s t", h=2, s=2)[:, :, side:2, :])\
                        .then_inc(s.f_pT_b, 1)

                def divide(n):
                    N = n0 + n
                    dve.wait_ge(s.f_exp, 2 * N + 2)
                    after(dve.reciprocal(f_ri, f_rs[:, n % 2, :]))
                    dve.wait_ge(s.f_o_ps, 2 * N + 2)
                    if N:
                        dve.wait_ge(s.f_oT_ps, N)
                    tt(heads(f_os), heads(ps[:, 3, :]), wide(f_ri, [P, HF, DF], 2), ALU.mult).then_inc(s.f_o_in, 1)

                rope(0)
                for n in range(-1, PAIR):
                    more = n + 1 < PAIR
                    if more:
                        maxima(n + 1, 0)
                    if n >= 0:
                        add_out(n)
                    if more:
                        maxima(n + 1, 1)
                        if n + 2 < PAIR:
                            rope(n + 2)
                        keep_probs(n + 1)
                        divide(n + 1)
                for z in range(2):
                    dve.wait_ge(s.f_h_in, 2 * k + z + 1)
                    h = f_h[:, NT * z:NT * z + NT, :]
                    layer_norm(h, h, NT, EPS5).then_inc(s.ln_out, 1)
                for z in range(2):
                    for c, m in enumerate(HID_C):
                        dve.wait_ge(s.f_gelu, 6 * k + 3 * z + c + 1)
                        bias = W("f_cols", 8 * l + 5 + c, 8 * l + 6 + c)
                        stt(f_hm[0:m, z, c, :], ps[0:m, 3 + 2 * c, :], bias[0:m, :], f_gb[0:m, c, :],
                            ALU.add, ALU.mult).then_inc(s.f_mid, 1)
                for z in range(2):
                    y = Y[:, NT * z:NT * z + NT, :]
                    dve.wait_ge(s.f_down, 2 * k + z + 1)
                    after(tt(y, y, ps[:, z, :].rearrange("p (j d) -> p j d", j=NT), ALU.add))
                    tt(y, y, wide(R("b2", D * l, D * l + D), [P, NT, D], 1), ALU.add).then_inc(s.f_fin, 1)
                dve.wait_ge(s.f_fin, 2 * k + 2)

            def small_heads():
                flat = lambda a: a.rearrange("p j h d -> p (j h) d")
                stream = lambda k: Y[:, NT * (k % 2):NT * (k % 2) + NT, :]

                def keep_sums(k, r):
                    dve.wait_ge(s.b_pv, 8 * k + 2 * r + 2)
                    if k:
                        dve.wait_ge(s.b_rT, 4 * k - 3 + r)
                    dve.tensor_copy(b_oR[:, r, :], ps[:, 6 + r % 2, :]).then_inc(s.b_o_in, 1)

                def finish(t, i):
                    if 1 <= i <= 4:
                        r = i - 1
                        dve.wait_ge(s.b_rT, 4 * t + i)
                        if t and r == 0:
                            dve.wait_ge(s.b_oT_ps, t)
                        o = ps[:, 4 + r % 2, :].rearrange("p (j g n) -> p j g n", j=NT, g=NG)
                        after(dve.reciprocal(b_ri[:, r], o[:, :, :, HD]))
                        tt(b_os[:, :, :, r, :], o[:, :, :, 0:HD], wide(b_ri[:, r], [P, NT, NG, HD], 3), ALU.mult)\
                            .then_inc(s.b_div, 1)
                    elif i == 6:
                        dve.wait_ge(s.b_out, t + 1)
                        after(tt(stream(t), stream(t), ps[:, 5, :].rearrange("p (j d) -> p j d", j=NT), ALU.add))

                def prepare(k, i):
                    y = stream(k)
                    if i == 6:
                        if k:
                            dve.wait_ge(s.b_xT_ps, k)
                        after(tt(b_hn, y, y, ALU.mult))
                        after(dve.tensor_reduce(rstd[:, 0:NT], b_hn, AX, ALU.add))
                        ts(rstd[:, 0:NT], rstd[:, 0:NT], 1.0 / D, EPS6, ALU.mult, ALU.add).then_inc(s.b_ms, 1)
                    elif i == 7:
                        dve.wait_ge(s.b_rn, 2 * k + 1)
                        tt(b_hn, y, wide(rstd[:, 0:NT], [P, NT, D], 2), ALU.mult).then_inc(s.b_hn_in, 1)
                    elif i == 11:
                        dve.wait_ge(s.b_qk_in, k + 1)
                        nm = "g" if k < 2 else "l"
                        cos = wide(C("cos_" + nm).rearrange("p (j d) -> p j d", j=NT), [P, NT, 20, 4], 2)
                        sin = wide(C("sin_" + nm).rearrange("p (j d) -> p j d", j=NT), [P, NT, 20, 4], 2)
                        even, odd = b_qk[:, :, :, 0:HD:2], b_qk[:, :, :, 1:HD:2]
                        tt(b_t[0], even, cos, ALU.mult)
                        tt(b_t[1], odd, sin, ALU.mult)
                        tt(b_t[2], even, sin, ALU.mult)
                        after(tt(b_t[3], odd, cos, ALU.mult))
                        tt(b_qr[:, :, :, 0:HD:2], b_t[0], b_t[1], ALU.subtract)
                        after(tt(b_qr[:, :, :, 1:HD:2], b_t[2], b_t[3], ALU.add))
                        sq = b_sq.rearrange("p (n d) -> p n d", d=HD)
                        after(tt(sq, flat(b_qr), flat(b_qr), ALU.mult))
                        after(dve.tensor_reduce(rstd[:, 0:80], sq, AX, ALU.add))
                        ts(rstd[:, 0:80], rstd[:, 0:80], 1.0 / HD, EPS6, ALU.mult, ALU.add).then_inc(s.b_ms, 1)
                    elif i == 13:
                        dve.wait_ge(s.b_rn, 2 * k + 2)
                        after(tt(flat(b_qr), flat(b_qr), wide(rstd[:, 0:80], [P, 80, HD], 2), ALU.mult))
                        for r in range(NR):
                            ins = dve.tensor_copy(b_kr[:, :, :, r, :], b_qr[:, :, HB:20, :])
                        ins.then_inc(s.b_rope, 1)
                    elif i == 14:
                        dve.wait_ge(s.b_tps, k + 1)
                        for r in range(NR):
                            ins = ts(b_kT[:, k % 2, r, :], ps[:, 5, :], C("rows", r, r + 1), None, ALU.mult)
                        ins.then_inc(s.b_kT_in, 1)

                def mask(U, j):
                    dve.wait_ge(s.b_exp, 4 * U + j + 1)
                    glob = U < 16
                    n, at = small_masked(glob, j), small_at(glob, j)
                    v = b_p[:, U % 2, :, at:at + n]
                    m = C("causal" if glob else "local", 0, n)
                    tt(v, v, m.unsqueeze(1).broadcast_to([P, 2, n]), ALU.mult).then_inc(s.b_mask_v, 1)

                for i in range(16):
                    prepare(0, i)
                for U in range(32):
                    k, u = U // 8, U % 8
                    for half in range(2):
                        mask(U, 2 * half + 1)
                        if half and U and u % 2 == 0:
                            keep_sums((U - 1) // 8, (U - 1) % 8 // 2)
                        if k >= 1:
                            finish(k - 1, 2 * u + half)
                        if k < 3:
                            prepare(k + 1, 2 * u + half)
                keep_sums(3, 3)
                for i in range(16):
                    finish(3, i)

            def head_attention(z):
                dve.wait_ge(s.c_qkv_in, z + 1)
                part = lambda j, n: c_qkv[:, j, 128 * n:128 * n + 128].rearrange("p (h d) -> p h d", h=HB)
                full = [P, HB, HB, HD]

                def scores(j):
                    b, u = j % 2, NT * z + j
                    prod = c_prod.rearrange("p (h t d) -> p h t d", h=HB, t=HB)
                    after(tt(prod, part(j, 0).unsqueeze(2).broadcast_to(full),
                             part(j, 1).unsqueeze(1).broadcast_to(full), ALU.mult))
                    if u >= 2:
                        dve.wait_ge(s.c_exp, u - 1)
                    after(dve.tensor_reduce(c_sc[:, b], prod, AX, ALU.add))
                    after(dve.tensor_reduce(mxa[:, :], c_sc[:, b], AX, ALU.max))
                    tt(c_sc[:, b], c_sc[:, b], wide(mxa[:, :], [P, HB, HB], 2), ALU.subtract).then_inc(s.c_shift, 1)

                def weights(j):
                    b = j % 2
                    dve.wait_ge(s.c_exp, NT * z + j + 1)
                    after(dve.tensor_reduce(rsa[:, :], c_e[:, b], AX, ALU.add))
                    after(dve.reciprocal(ria[:, :], rsa[:, :]))
                    tt(c_e[:, b], c_e[:, b], wide(ria[:, :], [P, HB, HB], 2), ALU.mult).then_inc(s.c_wts, 1)

                def summed(j):
                    dve.wait_ge(s.c_prod, NT * z + j + 1)
                    ins = dve.tensor_reduce(c_os[:, j * P:(j + 1) * P],
                                            c_mix[:, j % 2].rearrange("p (n t) -> p n t", t=HB), AX, ALU.add)
                    after(ins)
                    dve.sem_inc(s.c_red, 1)
                    if j == NT - 1:
                        dve.sem_inc(s.c_os_in, 1)

                for i in range(NT + 2):
                    if i < NT:
                        scores(i)
                    if i >= 2:
                        summed(i - 2)
                    if 1 <= i <= NT:
                        weights(i - 1)
                dve.wait_ge(s.c_out, z + 1)
                xb = XB[:, NT * z:NT * z + NT, :]
                tt(xb, xb, ps[:, 5, :].rearrange("p (j d) -> p j d", j=NT), ALU.add).then_inc(s.c_sum, 1)
                dve.wait_ge(s.c_sum, z + 1)

            def full_attention():
                layer_norm(XB[:, 0:NT, :], Y[:, 0:NT, :], NT, EPS5).then_inc(s.ln_out, 1)
                dve.wait_ge(s.ln_out, 1)
                layer_norm(Y[:, 0:NT, :], Y[:, 0:NT, :], NT, EPS5).then_inc(s.ln_out, 1)
                dve.wait_ge(s.m_sq, 1)
                after(dve.tensor_reduce(rstd[:, 0:16], m_sq.rearrange("p (n d) -> p n d", d=DF), AX, ALU.add))
                root(16, ts(rstd[:, 0:16], rstd[:, 0:16], 1.0 / DF, 1e-16, ALU.mult, ALU.max))
                rooted()
                for c in range(2):
                    src = ps[:, 1 + c, :].rearrange("p (j h d) -> p j h d", j=NT, h=2)
                    rn = rstd[:, 8 * c:8 * c + 8].rearrange("p (j h) -> p j h", j=NT)
                    dst = m_qk[:, :, 128 * c:128 * c + 128].rearrange("p j (h d) -> p j h d", h=2)
                    ins = tt(dst, src, wide(rn, [P, NT, 2, DF], 3), ALU.mult)
                ins.then_inc(s.m_qk_in, 1)
                dve.wait_ge(s.m_tps, 1)
                ts(m_kT, ps[:, 5, :], W("d_cols", 3, 4), None, ALU.mult).then_inc(s.m_kT_in, 1)
                steps, heads, dv = full_steps(), 2, DF
                scale = float(DF) ** -0.5
                for st in range(len(steps) + 1):
                    if st < len(steps):
                        dve.wait_ge(s.m_s, st + 1)
                        if st >= 2:
                            dve.wait_ge(s.m_exp, st - 1)
                        b = 2 * (st % 2)
                        after(dve.tensor_reduce(mxa[:, b:b + 2], ps[:, b:b + 2, :], AX, ALU.max))
                        ts(nma[:, b:b + 2], mxa[:, b:b + 2], -scale, None, ALU.mult).then_inc(s.m_max, 1)
                    if st:
                        dve.wait_ge(s.m_tp, st)
                        if st >= 2:
                            dve.wait_ge(s.m_pv, st - 1)
                        dve.tensor_copy(m_pT[:, 1], ps[:, 5, :].rearrange("p (j t) -> p j t", j=NT))\
                            .then_inc(s.m_pT_b, 1)
                dve.wait_ge(s.m_pv, len(steps))
                n = NT * heads
                after(dve.reciprocal(m_rs[:, 0:n], m_rs[:, 0:n]))
                tt(m_os.rearrange("p (n d) -> p n d", n=n), ps[:, 6, :].rearrange("p (n d) -> p n d", n=n),
                   wide(m_rs[:, 0:n], [P, n, dv], 2), ALU.mult).then_inc(s.m_os_in, 1)
                dve.wait_ge(s.m_out, 1)
                xb = XB[:, 0:NT, :]
                after(tt(xb, xb, ps[:, 1, :].rearrange("p (j d) -> p j d", j=NT), ALU.add))
                after(tt(xb, xb, wide(R("bo"), [P, NT, D], 1), ALU.add))

            def experts(k):
                def step(ins):
                    after(ins)

                def three(ap):
                    return ap.unsqueeze(2).broadcast_to([P, TT, E])

                layer_norm(X, e_xl, TT, EPS5).then_inc(es.e_ln, 1)
                dve.wait_ge(es.e_lg_ps, k + 1)
                step(tt(e_lg, ps[:, 2, 0:128].rearrange("p (i e) -> p i e", i=TT), wide(R("bs"), [P, TT, E], 1), ALU.add))
                step(dve.tensor_reduce(e_m[:, 0], e_lg, AX, ALU.max))
                tt(e_lg, e_lg, three(e_m[:, 0]), ALU.subtract).then_inc(es.e_shift, 1)
                dve.wait_ge(es.e_expd, k + 1)
                step(dve.tensor_reduce(e_m[:, 1], e_ex, AX, ALU.add))
                step(dve.reciprocal(e_m[:, 2], e_m[:, 1]))
                step(tt(e_pr, e_ex, three(e_m[:, 2]), ALU.mult))
                step(dve.tensor_reduce(e_m[:, 3], e_pr, AX, ALU.max))
                step(tt(e_cand, e_pr, three(e_m[:, 3]), ALU.is_equal))
                step(tt(e_cand, e_cand, wide(C("iota8"), [P, TT, E], 1), ALU.mult))
                step(dve.tensor_reduce(e_m[:, 4], e_cand, AX, ALU.min))
                tt(e_oh, wide(C("iota8"), [P, TT, E], 1), three(e_m[:, 4]), ALU.is_equal)
                tt(e_xl, e_xl, e_m[:, 3].unsqueeze(2).broadcast_to([P, TT, D]), ALU.mult).then_inc(es.e_probs, 1)
                dve.wait_ge(es.e_rank_ps, k + 1)
                rank = ps[:, 3, 0:128].rearrange("p (i e) -> p i e", i=TT)
                dve.memset(e_pre[:, 0, :], 0.0)
                dve.memset(e_eo[:, 0:1], 0.0)
                step(dve.tensor_copy(e_tot, ps[:, 3, 128:256].rearrange("p (i e) -> p i e", i=TT)))
                for i in range(TT - 1):
                    step(tt(e_pre[:, i + 1, :], e_pre[:, i, :], e_tot[:, i, :], ALU.add))
                step(tt(e_tot[:, 0, :], e_pre[:, TT - 1, :], e_tot[:, TT - 1, :], ALU.add))
                for e in range(E - 1):
                    step(tt(e_eo[:, e + 1:e + 2], e_eo[:, e:e + 1], e_tot[:, 0, e:e + 1], ALU.add))
                step(tt(e_pos, rank, e_pre, ALU.add))
                step(tt(e_pos, e_pos, wide(e_eo, [P, TT, E], 1), ALU.add))
                step(tt(e_pos, e_pos, e_oh, ALU.mult))
                step(dve.tensor_reduce(e_m[:, 5], e_pos, AX, ALU.add))
                dve.tensor_copy(e_idx[:, :], e_m[:, 5]).then_inc(es.e_idx_in, 1)
                n = E * NB
                dve.wait_ge(es.e_b2_in, k + 1)
                for q in range(n):
                    e, c = q // NB, q % NB
                    dve.wait_ge(es.e_down, n * k + q + 1)
                    if q >= NB:
                        dve.wait_ge(es.e_acc_in, n * k + q - NB + 1)
                    for j in range(NT):
                        i = NT * c + j
                        ins = stt(e_acc[:, i, :], ps[:, 6 + q % 2, j * P:(j + 1) * P], e_oh[:, i, e:e + 1],
                                  e_acc[:, i, :], ALU.mult, ALU.add)
                    ins.then_inc(es.e_acc_in, 1)
                dve.wait_ge(es.e_back_in, 16 * (k + 1))
                tt(X[:, :, :], X[:, :, :], e_back, ALU.add).then_inc(es.e_out, 1)
                dve.wait_ge(es.e_out, k + 1)

            def stages(which):
                f = 0
                for i, st in enumerate(which):
                    if st == "a":
                        linear_attention()
                    elif st == "f":
                        layer_norm(XB, Y, 2 * NT, EPS5).then_inc(s.ln_out, 1)
                        for l in range(2):
                            window_layer(f, l)
                            f += 1
                        after(tt(XB[:, :, :], XB[:, :, :], Y[:, :, :], ALU.add))
                    elif st == "b":
                        after(layer_norm(XB, Y, 2 * NT, EPS5))
                        small_heads()
                        after(tt(XB[:, :, :], XB[:, :, :], Y[:, :, :], ALU.add))
                    elif st == "c":
                        layer_norm(XB, Y, 2 * NT, EPS5).then_inc(s.ln_out, 1)
                        for z in range(2):
                            head_attention(z)
                    else:
                        full_attention()
                    stage_done(dve, i + 1)

            dve.memset(f_hT[64:128, :, 0:1], 0.0)
            dve.drain()
            dve.wait_ge(s_loaded, 64)
            for l in range(2):
                for n, (tab, gain) in enumerate((("cos_q", "qs"), ("sin_q", "qs"), ("cos_k", "ks"), ("sin_k", "ks"))):
                    ins = tt(tabs[:, l, n, :].rearrange("p (j d) -> p j d", j=NT),
                             C(tab).rearrange("p (j d) -> p j d", j=NT),
                             wide(R(gain, DF * l, DF * l + DF), [P, NT, DF], 1), ALU.mult)
            ins.then_inc(s_tabs, 1)
            dve.wait_ge(s_tabs, 1)
            with dve.Fori(0, NB) as b:
                dve.wait_ge(batch_go, b + 1)
                dve.sem_inc(batch_seen, 1)
                steps_done.n = asked.n = 0
                after(ts(XB[:, 0:NT, :], X[:, bass.ds(b * NT, NT), :], 1.0, None, ALU.mult))
                stages(["a"])
                ts(X[:, bass.ds(b * NT, NT), :], XB[:, 0:NT, :], 1.0, None, ALU.mult).then_inc(batch_done, 1)
            if STAGES >= 2:
                with dve.Fori(0, NP) as b:
                    dve.wait_ge(batch_go, b + NB + 1)
                    dve.sem_inc(batch_seen, 1)
                    steps_done.n = asked.n = 0
                    after(ts(XB[:, :, :], X[:, bass.ds(b * PAIR, PAIR), :], 1.0, None, ALU.mult))
                    stages(in_loop)
                    ts(X[:, bass.ds(b * PAIR, PAIR), :], XB[:, :, :], 1.0, None, ALU.mult).then_inc(batch_done, 1)
            steps_done.n = asked.n = 0
            if STAGES >= 6:
                dve.wait_ge(batch_go, NB + NP + 1)
                dve.sem_inc(batch_seen, 1)
                experts(0)
            if STAGES >= 7:
                dve.drain().then_inc(batch_done, 1)
                with dve.Fori(0, NB) as b:
                    dve.wait_ge(batch_go, b + NB + NP + 2)
                    dve.sem_inc(batch_seen, 1)
                    steps_done.n = asked.n = 0
                    after(ts(XB[:, 0:NT, :], X[:, bass.ds(b * NT, NT), :], 1.0, None, ALU.mult))
                    stages(["d"])
                    ts(X[:, bass.ds(b * NT, NT), :], XB[:, 0:NT, :], 1.0, None, ALU.mult).then_inc(batch_done, 1)
            if STAGES >= 8:
                steps_done.n = asked.n = 0
                dve.wait_ge(batch_go, 2 * NB + NP + 2)
                dve.sem_inc(batch_seen, 1)
                experts(1)
            dve.drain().then_inc(s_tabs, 1)

        @block.gpsimd
        def _(pool):
            asked, steps_done = Count(), Count()
            after = chain(pool, s.pool_step, steps_done)

            def root(n):
                pool.wait_ge(s.pow_in, asked.next())
                pool.tensor_tensor(rstd[:, 0:n], rstd[:, 0:n], C("neghalf", 0, n), ALU.pow).then_inc(s.pow_out, 1)

            def window_layer(k):
                heads = lambda t: t.rearrange("p (h d) -> p h d", h=HF)
                for n in range(PAIR):
                    N = PAIR * k + n
                    pool.wait_ge(s.f_ss_in, N + 1)
                    pool.tensor_tensor(f_ss[:, :], f_ss[:, :], C("neghalf", 0, 16), ALU.pow).then_inc(s.f_root, 1)
                    pool.wait_ge(s.f_rt, N + 1)
                    pool.tensor_tensor(heads(f_kr)[:, :, 0:32], heads(f_t3)[:, :, 0:32],
                                       heads(f_t4)[:, :, 32:64], ALU.add)
                    after(pool.tensor_tensor(heads(f_kr)[:, :, 32:64], heads(f_t3)[:, :, 32:64],
                                             heads(f_t4)[:, :, 0:32], ALU.add))
                    pool.tensor_tensor(heads(f_kr), heads(f_kr),
                                       f_ss[:, 8:16].unsqueeze(2).broadcast_to([P, HF, DF]), ALU.mult)\
                        .then_inc(s.f_rk, 1)

            def stages(which):
                f = 0
                for i, st in enumerate(which):
                    if st == "a":
                        root(NT)
                        for j in range(NT):
                            root(16)
                    elif st == "f":
                        pool.memset(f_p[:, :, 0:256 - KW], 0.0).then_inc(s.f_zero, 1)
                        root(2 * NT)
                        for l in range(2):
                            window_layer(f)
                            f += 1
                            root(NT)
                            root(NT)
                    elif st == "b":
                        root(2 * NT)
                        pool.memset(b_vx, 0.0)
                        pool.drain()
                        pool.memset(b_vx.rearrange("p k j (g n) -> p (k j g) n", g=NG)[:, :, HD:HD + 1], 1.0)\
                            .then_inc(s.b_zero, 1)
                        for U in range(32):
                            glob = U < 16
                            m = C("causal") if glob else C("local")
                            for j in (0, 2):
                                pool.wait_ge(s.b_exp, 4 * U + j + 1)
                                n, at = small_masked(glob, j), small_at(glob, j)
                                v = b_p[:, U % 2, :, at:at + n]
                                pool.tensor_tensor(v, v, m[:, 0:n].unsqueeze(1).broadcast_to([P, 2, n]), ALU.mult)\
                                    .then_inc(s.b_mask_p, 1)
                    elif st == "c":
                        root(2 * NT)
                        for z in range(2):
                            for j in range(NT):
                                u = NT * z + j
                                pool.wait_ge(s.c_wts, u + 1)
                                if u >= 2:
                                    pool.wait_ge(s.c_red, u - 1)
                                full = [P, HB, HD, HB]
                                vals = c_qkv[:, j, 256:384].rearrange("p (t d) -> p d t", t=HB)
                                pool.tensor_tensor(c_mix[:, j % 2].rearrange("p (h d t) -> p h d t", h=HB, t=HB),
                                                   c_e[:, j % 2].unsqueeze(2).broadcast_to(full),
                                                   vals.unsqueeze(1).broadcast_to(full), ALU.mult)\
                                    .then_inc(s.c_prod, 1)
                    else:
                        root(NT)
                        root(NT)
                        root(16)
                    stage_done(pool, i + 1)

            def experts(k):
                root(TT)
                pool.wait_ge(es.e_idx_in, k + 1)
                pool.wait_ge(es.e_acc_in, E * NB * (k + 1))
                for i in range(TT):
                    pool.indirect_dma_start(scratch[:, :], bass.IndirectOffsetOnAxis(ap=e_idx[:, i:i + 1], axis=0),
                                            e_acc[:, i, :], None).then_inc(es.e_sent, 16)

            pool.wait_ge(s_loaded, 64)
            with pool.Fori(0, NB) as b:
                pool.wait_ge(batch_go, b + 1)
                pool.sem_inc(batch_seen, 1)
                asked.n = steps_done.n = 0
                stages(["a"])
                pool.drain().then_inc(batch_done, 1)
            if STAGES >= 2:
                with pool.Fori(0, NP) as b:
                    pool.wait_ge(batch_go, b + NB + 1)
                    pool.sem_inc(batch_seen, 1)
                    asked.n = steps_done.n = 0
                    stages(in_loop)
                    pool.drain().then_inc(batch_done, 1)
            asked.n = 0
            if STAGES >= 6:
                pool.wait_ge(batch_go, NB + NP + 1)
                pool.sem_inc(batch_seen, 1)
                experts(0)
            if STAGES >= 7:
                with pool.Fori(0, NB) as b:
                    pool.wait_ge(batch_go, b + NB + NP + 2)
                    pool.sem_inc(batch_seen, 1)
                    asked.n = 0
                    stages(["d"])
                    pool.drain().then_inc(batch_done, 1)
            if STAGES >= 8:
                asked.n = 0
                pool.wait_ge(batch_go, 2 * NB + NP + 2)
                pool.sem_inc(batch_seen, 1)
                experts(1)

        @block.sync
        def _(sp):
            sp.dma_start(X[:, :, :], x_in.rearrange("b (t p) d -> p (b t) d", p=P)).then_inc(s_loaded, 16)
            sp.dma_start(Ct[:, :], c_in).then_inc(s_loaded, 16)
            sp.dma_start(Rt[:, :], r_in.broadcast_to([P, r_cols])).then_inc(s_loaded, 16)
            sp.dma_start(Wt[:, :], w_in).then_inc(s_loaded, 16)

            def clear():
                sp.sem_clear(range(first, first + len(names)))
                sp.sem_clear(batch_done)
                sp.sem_inc(batch_go, 1)

            def back(k):
                sp.wait_ge(es.e_sent, 16 * TT * (k + 1))
                sp.dma_start(e_back, scratch.rearrange("(i p) d -> p i d", p=P)).then_inc(es.e_back_in, 16)

            numbers = sorted(sem_number(sems[n]) for n in names)
            first = numbers[0]
            assert numbers == list(range(first, first + len(names)))
            sp.sem_inc(batch_go, 1)
            with sp.Fori(0, NB) as b:
                sp.wait_ge(batch_done, 4)
                clear()
            if STAGES >= 2:
                with sp.Fori(0, NP) as b:
                    sp.wait_ge(batch_done, 4)
                    clear()
            if STAGES >= 6:
                back(0)
            if STAGES >= 7:
                sp.wait_ge(batch_done, 1)
                clear()
                with sp.Fori(0, NB) as b:
                    sp.wait_ge(batch_done, 4)
                    clear()
            if STAGES >= 8:
                back(1)
            sp.wait_ge(s_tabs, 2)
            sp.dma_start(out.rearrange("b (t p) d -> p (b t) d", p=P), X[:, :, :]).then_inc(s_store, 16)
            sp.wait_ge(s_store, 16)


def sem_number(sem):
    return int(sem.num)


def small_width(glob, j):
    return S - j * P if glob else min(P + LW, S - j * P)


def small_masked(glob, j):
    return min(small_width(glob, j), P if glob else P + LW)


def small_at(glob, j):
    return sum(small_width(glob, i) for i in range(j))


def full_steps():
    return [(i, [(h, slice(64 * h, 64 * h + 64)) for h in range(2)]) for i in range(NT)]


def kernel(**inputs):
    import numpy as _np
    import concourse.bacc as _bacc
    from concourse import mybir as _mybir
    from concourse.bass_utils import run_bass_kernel_spmd as _run

    g = {k: _np.asarray(v) for k, v in inputs.items()}
    a = {k[len("L0_attn_a_"):]: v for k, v in g.items() if k.startswith("L0_attn_a_")}
    b = {k[len("L0_attn_b_"):]: v for k, v in g.items() if k.startswith("L0_attn_b_")}
    f = {k[len("L0_ffn_"):]: v for k, v in g.items() if k.startswith("L0_ffn_")}
    c = {k[len("L1_attn_a_"):]: v for k, v in g.items() if k.startswith("L1_attn_a_")}
    d = {k[len("L1_attn_b_"):]: v for k, v in g.items() if k.startswith("L1_attn_b_")}
    e = {k[len("L1_ffn_"):]: v for k, v in g.items() if k.startswith("L1_ffn_")}

    def pad(m):
        out = _np.zeros((P, m.shape[1]), m.dtype)
        out[:m.shape[0]] = m
        return out

    def col(v):
        return pad(v[:, None])

    side = lambda xs: _np.concatenate(xs, 1)
    blocks = {
        "a_qkv": side([a["Wq"].T, a["Wk"].T, a["Wv"].T]),
        "a_wo": a["Wo"].reshape(D, HA, 128).transpose(2, 1, 0).reshape(128, -1),
        "a_wg": a["Wg"].T,
        "f_wqkv": side([f["wqkv"][l] for l in range(2)]),
        "f_wo": side([f["wo"][l][128 * i:128 * i + 128] for l in range(2) for i in range(4)]),
        "f_w1": side([f["w1"][l] for l in range(2)]),
        "f_w2": side([pad(f["w2"][l][128 * i:min(128 * i + 128, HID)]) for l in range(2) for i in range(3)]),
        "f_cols": side([side([col(f["ln_g"][l]), col(f["ln_b"][l])]
                             + [col(f["b1"][l][HID + 128 * i:min(HID + 128 * i + 128, 2 * HID)]) for i in range(3)]
                             + [col(f["b1"][l][128 * i:min(128 * i + 128, HID)]) for i in range(3)]) for l in range(2)]),
        "b_norm": side([col(b["norm1_w"]), col(b["norm2_w"])]),
        "b_gq": b["g_wq"], "b_lq": b["l_wq"], "b_down": b["g_kv_down"],
        "b_up": pad(side([b["g_k_up"], b["g_v_up"]])), "b_lkv": side([b["l_wk"], b["l_wv"]]),
        "b_gwo": b["g_wo"], "b_lwo": b["l_wo"],
        "c_qkv": side([c["Wq"].T, c["Wk"].T, c["Wv"].T]), "c_fc": c["Wfc"].T,
        "d_qkv": side([d["w_q"].T, d["w_k"].T, d["w_v"].T]), "d_wo": d["w_o"].T,
        "d_cols": side([col(d["ln_gamma"]), col(d["ln_beta"]), col(_np.tile(d["q_gamma"], 2)),
                        col(_np.tile(d["k_gamma"], 2))]),
        "e_ws": e["Ws"].T, "e_w1": side([e["W1"][i] for i in range(E)]), "e_w2": side([e["W2"][i] for i in range(E)]),
        "e_b1": e["b1"].T, "e_b2": pad(e["b2"]),
    }
    for name, w in WEIGHTS:
        assert blocks[name].shape == (P, w), (name, blocks[name].shape, w)
    rows = {"bg": a["bg"], "gain": a["qk_gain"].reshape(1), "qs": f["q_scale"].reshape(-1),
            "ks": f["k_scale"].reshape(-1), "b2": f["b2"].reshape(-1), "bo": d["b_o"], "bs": e["bs"]}
    tables = constants()
    c_at, _ = places([(k, v.shape[1]) for k, v in tables.items()])
    arrays = {
        "in_x": _np.ascontiguousarray(a["x"]),
        "in_w": _np.ascontiguousarray(side([blocks[n] for n, _ in WEIGHTS])),
        "in_c": _np.ascontiguousarray(side(list(tables.values()))),
        "in_r": _np.ascontiguousarray(_np.concatenate([rows[n] for n, _ in ROWS])[None, :]),
    }
    nc = _bacc.Bacc("TRN2", target_bir_lowering=False, num_devices=1)
    f32 = _mybir.dt.float32
    args = [nc.dram_tensor(n, v.shape, f32, kind="ExternalInput").ap() for n, v in arrays.items()]
    out = nc.dram_tensor("out_0", (NB, S, D), f32, kind="ExternalOutput").ap()
    scratch = nc.dram_tensor("sorted_rows", (NB * S, D), f32, kind="Internal").ap()
    program(nc, *args, out, scratch, c_at)
    r = _run(nc, [arrays], core_ids=[0])
    return r.results[0]["out_0"]
```

```python
from contextlib import ExitStack

import numpy as np

import concourse.bass as bass
from concourse import mybir

STAGES = 8

ALU = mybir.AluOpType
ACT = mybir.ActivationFunctionType
F32 = mybir.dt.float32
U32 = mybir.dt.uint32
AX = mybir.AxisListType.X

P = 128
PAIR = 8
NP = 2
NB = 4
S = 512
NT = S // P
D = 128
HA, CH = 8, 64
NCH = S // CH
HF, DF = 8, 64
WIN = 64
KW = P + WIN
HID = 341
HID_C = [128, 128, HID - 256]
NG, NR, HD = 4, 4, 8
HB = NG * NR
LW = 32
E = 8
TT = NB * NT
EPS6, EPS5 = 1e-6, 1e-5
NEG = -1e30


def constants():
    f = np.float32
    p = np.arange(P)
    t = {}
    t["ident"] = np.eye(P)
    same = (p[:, None] // CH) == (p[None, :] // CH)
    t["mask_a"] = np.where(same & (p[None, :] <= p[:, None]), 0.0, NEG)
    c = np.arange(KW)
    t["mask_f"] = np.where((c[None, :] >= p[:, None]) & (c[None, :] - WIN <= p[:, None]), 0.0, -1e25)
    t["causal"] = (p[None, :] >= p[:, None]) * 1.0
    q = np.arange(P + LW)
    t["local"] = ((q[None, :] >= p[:, None]) & (q[None, :] < p[:, None] + LW)) * 1.0
    t["shift"] = np.eye(P, k=1)
    t["carry"] = np.zeros((P, P))
    t["carry"][P - 1, 0] = 1.0
    t["half0"] = np.repeat((p < CH)[:, None], P, 1) * 1.0
    t["half1"] = np.repeat((p >= CH)[:, None], P, 1) * 1.0
    t["rows"] = ((p[:, None] % 32) // HD == np.arange(NR)[None, :]) * 1.0
    t["neghalf"] = np.full((P, 80), -0.5)
    t["ones"] = np.ones((P, P))
    t["before"] = (p[:, None] < p[None, :]) * 1.0
    t["iota8"] = np.repeat((np.arange(E) - E)[None, :], P, 0) * 1.0
    half = np.arange(0, DF, 2, dtype=f)
    inv = (f(1) / np.power(10000.0, half.astype(np.float64) / DF).astype(f)).astype(f)
    pos = np.arange(S, dtype=f)
    fr = (pos[:, None] * inv[None, :]).astype(f).astype(np.float64)
    base = ((half + f(0.4 * DF)) / f(1.4 * DF)).astype(f).astype(np.float64)
    power = ((pos - S // 2) / f(WIN // 2)).astype(np.float64)
    sc = base[None, :] ** power[:, None]
    cos, sin = np.cos(fr), np.sin(fr)
    both = lambda a: np.concatenate([a, a], 1)
    sign = lambda a: np.concatenate([a, -a], 1)
    tile = lambda a: a.reshape(NT, P, -1).transpose(1, 0, 2).reshape(P, -1)
    t["cos_q"], t["sin_q"] = tile(both(cos * sc * 8.0)), tile(sign(sin * sc * 8.0))
    t["cos_k"], t["sin_k"] = tile(both(cos / sc)), tile(sign(sin / sc))
    for name, b in (("g", 1e6), ("l", 1e4)):
        iv = (f(1) / np.power(f(b), np.arange(0, HD, 2, dtype=f) / f(HD))).astype(f)
        fq = (pos[:, None] * iv[None, :]).astype(f).astype(np.float64)
        t["cos_" + name], t["sin_" + name] = tile(np.cos(fq)), tile(np.sin(fq))
    return {k: np.ascontiguousarray(v, dtype=f) for k, v in t.items()}


def places(blocks):
    at, out = 0, {}
    for name, w in blocks:
        out[name] = (at, w)
        at += w
    return out, at


WEIGHTS = [("a_qkv", 3072), ("a_wo", 1024), ("a_wg", 8),
           ("f_wqkv", 3072), ("f_wo", 1024), ("f_w1", 2 * 2 * HID), ("f_w2", 2 * 3 * 128),
           ("f_cols", 2 * 8),
           ("b_norm", 2), ("b_gq", 128), ("b_lq", 128), ("b_down", 32), ("b_up", 64), ("b_lkv", 64),
           ("b_gwo", 128), ("b_lwo", 128),
           ("c_qkv", 384), ("c_fc", 128),
           ("d_qkv", 384), ("d_wo", 128), ("d_cols", 4),
           ("e_ws", 8), ("e_w1", 1024), ("e_w2", 1024), ("e_b1", 8), ("e_b2", 128)]
ROWS = [("bg", HA), ("gain", 1), ("qs", 2 * DF), ("ks", 2 * DF), ("b2", 2 * D), ("bo", D), ("bs", E)]


def program(nc, x_in, w_in, c_in, r_in, out, scratch, c_at):
    w_at, w_cols = places(WEIGHTS)
    r_at, r_cols = places(ROWS)
    c_cols = sum(w for _, w in c_at.values())
    with ExitStack() as ctx:
        def sb(name, shape, dt=F32):
            return ctx.enter_context(nc.sbuf_tensor(name, shape, dt))

        Wt, Ct, Rt = sb("weights", [P, w_cols]), sb("consts", [P, c_cols]), sb("rows", [P, r_cols])

        def W(name, a=0, b=None):
            at, w = w_at[name]
            return Wt[:, at + a:at + (w if b is None else b)]

        def C(name, a=0, b=None):
            at, w = c_at[name]
            return Ct[:, at + a:at + (w if b is None else b)]

        def R(name, a=0, b=None):
            at, w = r_at[name]
            return Rt[:, at + a:at + (w if b is None else b)]

        ident = C("ident")
        ps = ctx.enter_context(nc.psum_tensor("ps", [P, 8, 512], F32))

        X = sb("X", [P, TT, D])
        XB = sb("XB", [P, 2 * NT, D])
        Y = sb("Y", [P, 2 * NT, D])
        stats = sb("stats", [P, TT, 6])
        mv = sb("mv", [P, TT, 2])
        rstd = sb("rstd", [P, 80])
        xT = sb("xT", [P, S])
        tabs = sb("tabs", [P, 2, 4, NT * DF])
        arena = sb("arena", [P, 24576])
        taken = [0]

        def carve(n):
            at = taken[0]
            taken[0] += n
            assert taken[0] <= 24576, taken
            return arena[:, at:at + n]

        a_kn = carve(4096).rearrange("p (j h d) -> p j h d", j=NT, h=HA)
        a_v = carve(4096).rearrange("p (j n) -> p j n", j=NT)
        a_qT = carve(4096).rearrange("p (h t) -> p h t", h=HA)
        a_kT = carve(4096).rearrange("p (h t) -> p h t", h=HA)
        a_union = taken[0]
        a_sqr = carve(2048)
        a_qn = carve(1024).rearrange("p (h d) -> p h d", h=HA)
        taken[0] = a_union
        a_st = carve(2048).rearrange("p (z n d) -> p z n d", z=2, n=NCH)
        a_yT = carve(4096).rearrange("p (h t) -> p h t", h=HA)
        a_sc = sb("a_sc", [P, 2, NT, P])
        a_p = sb("a_p", [P, 2, NT, P])
        a_pT = sb("a_pT", [P, NT, P])
        a_gate = sb("a_gate", [P, 32])
        a_gam = sb("a_gam", [P, 2, NT, HA])
        small = sb("small", [P, 6, 16])
        mxa, nma, rsa, ria = small[:, 0, :], small[:, 1, :], small[:, 2, :], small[:, 3, :]
        taken[0] = 0
        f_v = carve(2 * 2048).rearrange("p (i n) -> p i n", i=2 * NT)
        f_kT = carve(2 * 2048).rearrange("p (z c t) -> p z c t", z=2, c=4)
        f_sqr = carve(1024)
        f_qr, f_kr = carve(512), carve(512)
        f_qT = carve(512).rearrange("p (c t) -> p c t", c=4)
        f_p = carve(2 * 8 * 256).rearrange("p (z h s) -> p z h s", z=2, h=HF)
        f_os = carve(512)
        f_oT = carve(512).rearrange("p (c t) -> p c t", c=4)
        f_h = carve(1024).rearrange("p (i d) -> p i d", i=2 * NT)
        f_hnT = carve(1024).rearrange("p (z t) -> p z t", z=2)
        f_shared = taken[0]
        f_t1, f_t2, f_t3, f_t4 = carve(512), carve(512), carve(512), carve(512)
        f_sc = carve(8 * KW).rearrange("p (h s) -> p h s", h=HF)
        f_pT = carve(8 * 256).rearrange("p (h s t) -> p h s t", h=HF, s=2)
        taken[0] = f_shared
        f_gb = carve(3 * 512).rearrange("p (c t) -> p c t", c=3)
        f_hm = carve(2 * 3 * 512).rearrange("p (z c t) -> p z c t", z=2, c=3)
        f_hT = sb("f_hT", [P, 2, S])
        f_ss = sb("f_ss", [P, 2, 16])
        f_small = sb("f_small", [P, 5, 8])
        f_mx, f_nm, f_ri = f_small[:, 0, :], f_small[:, 1, :], f_small[:, 2, :]
        f_rs = f_small[:, 3:5, :]
        taken[0] = 0
        b_sq = carve(4 * 160)
        b_qk = carve(4 * 160).rearrange("p (j h d) -> p j h d", j=NT, h=20)
        b_qr = carve(4 * 160).rearrange("p (j h d) -> p j h d", j=NT, h=20)
        b_t = [carve(4 * 80).rearrange("p (j h d) -> p j h d", j=NT, h=20) for _ in range(4)]
        b_kr = carve(512).rearrange("p (j g r d) -> p j g r d", j=NT, g=NG, r=NR)
        b_latT = carve(512)
        b_qT = carve(2 * 512).rearrange("p (k t) -> p k t", k=2)
        b_kT = carve(2 * 2048).rearrange("p (k r t) -> p k r t", k=2, r=NR)
        b_os = carve(512).rearrange("p (j g r d) -> p j g r d", j=NT, g=NG, r=NR)
        b_oT = carve(512)
        b_oR = carve(4 * 512).rearrange("p (r t) -> p r t", r=NR)
        b_hn = carve(512).rearrange("p (j d) -> p j d", j=NT)
        b_p = carve(2 * 2 * 1280).rearrange("p (z h t) -> p z h t", z=2, h=2)
        b_pitch = NG * (P + 32)
        b_vx = carve(2 * NT * b_pitch).rearrange("p (k j n) -> p k j n", k=2, j=NT)
        b_ri = sb("b_ri", [P, NR, NT, NG])
        taken[0] = 0
        c_qkv = carve(PAIR * 384).rearrange("p (j n) -> p j n", j=PAIR)
        c_prod = carve(2048)
        c_mix = carve(2 * 2048).rearrange("p (z n) -> p z n", z=2)
        c_sc = carve(2 * 256).rearrange("p (z h t) -> p z h t", z=2, h=HB)
        c_e = carve(2 * 256).rearrange("p (z h t) -> p z h t", z=2, h=HB)
        c_os = carve(PAIR * P)
        c_oT = carve(512)
        taken[0] = 0
        m_qT = carve(512)
        m_kT = carve(512)
        m_v = carve(512).rearrange("p (j n) -> p j n", j=NT)
        m_p = carve(2048).rearrange("p (z h s) -> p z h s", z=2, h=2)
        m_pT = carve(1024).rearrange("p (h j t) -> p h j t", h=2, j=NT)
        m_os = carve(512)
        m_oT = carve(512)
        m_sq = carve(1024)
        m_qk = carve(1024).rearrange("p (j n) -> p j n", j=NT)
        m_rs = sb("m_rs", [P, NT * 2])
        taken[0] = 0
        e_xl = carve(2048).rearrange("p (i d) -> p i d", i=TT)
        e_xT = carve(2048)
        e_acc = carve(2048).rearrange("p (i d) -> p i d", i=TT)
        e_h = carve(1024).rearrange("p (z t) -> p z t", z=2)
        e_back = carve(2048).rearrange("p (i d) -> p i d", i=TT)
        e_ohT = carve(2048)
        e_small = carve(8 * 128).rearrange("p (k i e) -> p k i e", k=8, i=TT)
        e_lg, e_ex, e_pr, e_oh, e_cand, e_tot, e_pre, e_pos = (e_small[:, k] for k in range(8))
        e_m = carve(6 * 16).rearrange("p (k i) -> p k i", k=6)
        e_eo = carve(8)
        e_idx = sb("e_idx", [P, TT], U32)

        names = """ln_out pow_in pow_out dve_step act_step stage_end
            a_xT_ps a_xT a_gate_ps a_gate_in a_decay a_gsum a_gamma a_proj a_vproj a_sq a_vcopy a_gain a_norm
            a_tps a_tcopy a_kv a_state a_scores a_max a_exp a_prob a_pT_ps a_pT_in a_y_ps a_yT_in a_o
            f_yT_ps f_hT_in f_proj f_sq f_vcopy f_ss_in f_root f_rq f_rt f_rk f_q_ps f_q_in f_k_ps f_k_in
            f_sc_ps f_max f_exp f_pT_ps f_pT_in f_o_ps f_o_in f_oT_ps f_oT_in f_attn f_y f_sh f_h_in
            f_hnT_ps f_hnT_in f_up f_gelu f_mid f_down f_fin f_zero pool_step
            b_zero b_ms b_rn b_hn_in b_xT_ps b_hT b_lat_ps b_lat_in b_kvq b_qk_in b_rope b_tps b_qT_in b_kT_in
            b_s b_exp b_mask_p b_mask_v b_pv b_o_in b_rT b_div b_oT_ps b_oT_in b_out
            c_xT_ps c_xT c_proj c_qkv_in c_shift c_exp c_wts c_prod c_red c_sum c_os_in c_oT_ps c_oT_in c_out
            m_xT_ps m_xT m_proj m_sq m_qk_in m_tps m_kT_in m_qv_in m_s m_max m_exp m_tp m_pT_a m_pT_b m_pv
            m_os_in m_oT_ps m_oT_in m_out""".split()
        sems = {n: ctx.enter_context(nc.semaphore(n)) for n in names}
        s = type("Sems", (), sems)
        batch_go = ctx.enter_context(nc.semaphore("batch_go"))
        batch_done = ctx.enter_context(nc.semaphore("batch_done"))
        batch_seen = ctx.enter_context(nc.semaphore("batch_seen"))
        s_loaded = ctx.enter_context(nc.semaphore("s_loaded"))
        s_rest = ctx.enter_context(nc.semaphore("s_rest"))
        s_tabs = ctx.enter_context(nc.semaphore("s_tabs"))
        s_store = ctx.enter_context(nc.semaphore("s_store"))
        e_names = """e_ln e_xT_ps e_xT_in e_lg_ps e_shift e_expd e_probs e_rank_ps e_idx_in e_xsT_ps
            e_xsT_in e_oT_ps e_oT_in e_b2_ps e_b2_in e_up e_relu e_down e_acc_in e_sent e_back_in e_out""".split()
        es = type("ESems", (), {n: ctx.enter_context(nc.semaphore(n)) for n in e_names})

        block = ctx.enter_context(nc.Block())

        class Count:
            def __init__(self):
                self.n = 0

            def next(self):
                self.n += 1
                return self.n

        def chain(eng, sem, count):
            def after(ins):
                ins.then_inc(sem, 1)
                eng.wait_ge(sem, count.next())
            return after

        def stage_done(eng, k):
            eng.drain().then_inc(s.stage_end, 1)
            eng.wait_ge(s.stage_end, 4 * k)

        in_loop = ["f", "b", "f", "c"][:min(STAGES, 5) - 1]

        @block.tensor
        def _(pe):
            mm, tr = pe.matmul, pe.transpose

            def transposes(bank, src):
                for j in range(NT):
                    last = tr(ps[:, bank, j * P:(j + 1) * P], src(j), ident)
                return last

            def linear_attention(ln):
                pe.wait_ge(s.ln_out, ln)
                transposes(0, lambda j: Y[:, j, :]).then_inc(s.a_xT_ps, 1)
                pe.wait_ge(s.a_xT, 1)
                for j in range(NT):
                    last = mm(ps[:, 7, j * HA:(j + 1) * HA], xT[:, j * P:(j + 1) * P], W("a_wg"),
                              start=True, stop=True)
                last.then_inc(s.a_gate_ps, 1)

                def project_qk(j):
                    for half, banks in enumerate(((2, 3), (0, 1))):
                        if j >= 1:
                            pe.wait_ge(s.a_norm, 2 * j - 1 + half)
                        for c in banks:
                            last = mm(ps[:, c, :], xT[:, j * P:(j + 1) * P], W("a_qkv", 512 * c, 512 * c + 512),
                                      start=True, stop=True)
                        last.then_inc(s.a_proj, 1)

                def project_v(j):
                    if j >= 1:
                        pe.wait_ge(s.a_vcopy, j)
                    for c in range(4, 6):
                        last = mm(ps[:, c, :], xT[:, j * P:(j + 1) * P], W("a_qkv", 512 * c, 512 * c + 512),
                                  start=True, stop=True)
                    last.then_inc(s.a_vproj, 1)

                def turn(j):
                    pe.wait_ge(s.a_norm, 2 * j + 2)
                    for g in range(4):
                        T = 4 * j + g
                        if T == 1:
                            pe.wait_ge(s.a_gate_in, 1)
                        if T >= 2:
                            pe.wait_ge(s.a_tcopy, T - 1)
                        for i in range(4):
                            h = 4 * (g % 2) + i
                            src = a_qn[:, h, :] if g < 2 else a_kn[:, j, h, :]
                            last = tr(ps[:, 6 + T % 2, i * P:(i + 1) * P], src, ident)
                        last.then_inc(s.a_tps, 1)

                project_qk(0)
                project_v(0)
                for j in range(NT):
                    if j + 1 < NT:
                        project_qk(j + 1)
                    turn(j)
                    if j + 1 < NT:
                        project_v(j + 1)
                pe.wait_ge(s.a_decay, 1)
                for half in range(2):
                    last = mm(ps[:, 0, 32 * half:32 * half + 32], C("half%d" % half), a_gate[:, :],
                              start=True, stop=True)
                last.then_inc(s.a_gsum, 1)
                pe.wait_ge(s.a_gamma, 1)
                pe.wait_ge(s.a_vcopy, NT)
                pe.wait_ge(s.a_tcopy, 4 * NT)

                def outer(h):
                    if h >= 2:
                        pe.wait_ge(s.a_state, h - 1)
                    for n in range(NCH - 1):
                        j, r = n // 2, n % 2
                        last = mm(ps[:, 2 * (h % 2) + r, j * P:(j + 1) * P],
                                  a_kn[64 * r:64 * r + 64, j, h, :],
                                  a_v[64 * r:64 * r + 64, j, h * P:(h + 1) * P], start=True, stop=True)
                    last.then_inc(s.a_kv, 1)

                def scores(h):
                    if h >= 2:
                        pe.wait_ge(s.a_max, h - 1)
                    for j in range(NT):
                        last = mm(ps[:, 4 + h % 2, j * P:(j + 1) * P], a_qT[:, h, j * P:(j + 1) * P],
                                  a_kT[:, h, j * P:(j + 1) * P], start=True, stop=True)
                    last.then_inc(s.a_scores, 1)

                def turn_probs(h):
                    pe.wait_ge(s.a_prob, h + 1)
                    if h >= 1:
                        pe.wait_ge(s.a_pT_in, h)
                    for j in range(NT):
                        last = tr(ps[:, 6, j * P:(j + 1) * P], a_p[:, h % 2, j, :], ident)
                    last.then_inc(s.a_pT_ps, 1)

                def mix(h):
                    pe.wait_ge(s.a_pT_in, h + 1)
                    pe.wait_ge(s.a_state, h + 1)
                    if h >= 1:
                        pe.wait_ge(s.a_yT_in, h)
                    for j in range(NT):
                        mm(ps[:, 7, j * P:(j + 1) * P], a_v[:, j, h * P:(h + 1) * P], a_pT[:, j, :],
                           start=True, stop=True, skip_group_check=True)
                        for n in (2 * j, 2 * j + 1):
                            if n:
                                last = mm(ps[:, 7, n * CH:(n + 1) * CH], a_st[:, h % 2, n, :],
                                          a_qT[:, h, n * CH:(n + 1) * CH], start=False, stop=True,
                                          skip_group_check=True)
                    last.then_inc(s.a_y_ps, 1)

                for i in range(HA + 1):
                    if i < HA:
                        outer(i)
                    if i:
                        turn_probs(i - 1)
                    if i < HA:
                        scores(i)
                    if i:
                        mix(i - 1)
                pe.wait_ge(s.a_yT_in, HA)
                for j in range(NT):
                    for h in range(HA):
                        last = mm(ps[:, 0, j * P:(j + 1) * P], a_yT[:, h, j * P:(j + 1) * P],
                                  W("a_wo", 128 * h, 128 * h + 128), start=h == 0, stop=h == HA - 1)
                last.then_inc(s.a_o, 1)

            def window_layer(k, l, ln):
                n0 = PAIR * k
                pe.wait_ge(s.ln_out, ln)
                if l:
                    pe.wait_ge(s.f_fin, 2 * k)
                for z in range(2):
                    transposes(z, lambda j: Y[:, NT * z + j, :]).then_inc(s.f_yT_ps, 1)
                pe.wait_ge(s.f_hT_in, 2 * k + 2)

                def project(n):
                    N, z, j = n0 + n, n % 2, n // 2
                    if n >= 1:
                        pe.wait_ge(s.f_q_in, N)
                        pe.wait_ge(s.f_k_in, N)
                        pe.wait_ge(s.f_vcopy, N)
                    for c in range(3):
                        last = mm(ps[:, c, :], f_hT[:, z, j * P:(j + 1) * P],
                                  W("f_wqkv", 1536 * l + 512 * c, 1536 * l + 512 * c + 512), start=True, stop=True)
                    last.then_inc(s.f_proj, 1)

                def turn_qk(n):
                    N = n0 + n
                    pe.wait_ge(s.f_sq, N + 1)
                    pe.wait_ge(s.f_rq, N + 1)
                    for c in range(4):
                        last = tr(ps[:, 0, c * P:(c + 1) * P], f_qr[:, c * P:(c + 1) * P], ident)
                    last.then_inc(s.f_q_ps, 1)
                    pe.wait_ge(s.f_rk, N + 1)
                    for c in range(4):
                        last = tr(ps[:, 1, c * P:(c + 1) * P], f_kr[:, c * P:(c + 1) * P], ident)
                    last.then_inc(s.f_k_ps, 1)

                def scores(n, g):
                    N, z, j = n0 + n, n % 2, n // 2
                    pe.wait_ge(s.f_q_in, N + 1)
                    pe.wait_ge(s.f_k_in, N + 1)
                    if 2 * N + g >= 1:
                        pe.wait_ge(s.f_max, 2 * N + g)
                    lo = 0 if j else WIN
                    for i in range(4):
                        h = 4 * g + i
                        rows = slice(64 * (h % 2), 64 * (h % 2) + 64)
                        at = KW * (i // 2)
                        last = mm(ps[:, 4 + h % 2, at + lo:at + KW], f_qT[rows, h // 2, :],
                                  f_kT[rows, z, h // 2, j * P - WIN + lo:(j + 1) * P], start=True, stop=True)
                    last.then_inc(s.f_sc_ps, 1)

                def turn_probs(n, p):
                    N, j = n0 + n, n // 2
                    pe.wait_ge(s.f_zero, k // 2 + 1)
                    pe.wait_ge(s.f_exp, 2 * N + p // 2 + 1)
                    if p >= 2:
                        pe.wait_ge(s.f_pT_in, 4 * N + p - 1)
                    for i in range(2):
                        for side in ((0, 1) if j else (1,)):
                            at = 256 * i + 128 * side
                            last = tr(ps[:, 6 + p % 2, at:at + 128],
                                      f_p[:, n % 2, 2 * p + i, 128 * side:128 * side + 128], ident)
                    last.then_inc(s.f_pT_ps, 1)

                def values(n, p):
                    N, z, j = n0 + n, n % 2, n // 2
                    if p == 0:
                        pe.wait_ge(s.f_vcopy, N + 1)
                        if N:
                            pe.wait_ge(s.f_y, N)
                    pe.wait_ge(s.f_pT_in, 4 * N + p + 1)
                    for h in (2 * p, 2 * p + 1):
                        o = ps[:, 3, h * DF:(h + 1) * DF]
                        last = mm(o, f_pT[:, h, 1, :], f_v[:, NT * z + j, h * DF:(h + 1) * DF], start=True, stop=j == 0)
                        if j:
                            last = mm(o, f_pT[:, h, 0, :], f_v[:, NT * z + j - 1, h * DF:(h + 1) * DF],
                                      start=False, stop=True)
                    last.then_inc(s.f_o_ps, 1)

                def turn_out(n):
                    N = n0 + n
                    pe.wait_ge(s.f_o_in, N + 1)
                    for c in range(4):
                        last = tr(ps[:, 7, c * P:(c + 1) * P], f_os[:, c * P:(c + 1) * P], ident)
                    last.then_inc(s.f_oT_ps, 1)

                def out_rows(n):
                    N = n0 + n
                    pe.wait_ge(s.f_oT_in, N + 1)
                    for c in range(4):
                        last = mm(ps[:, 3, 0:D], f_oT[:, c, :], W("f_wo", 512 * l + 128 * c, 512 * l + 128 * c + 128),
                                  start=c == 0, stop=c == 3)
                    last.then_inc(s.f_attn, 1)

                for t in range(-1, PAIR + 2):
                    if live(t + 1):
                        project(t + 1)
                    if live(t):
                        scores(t, 0)
                    if live(t - 2):
                        turn_out(t - 2)
                        out_rows(t - 2)
                    if live(t - 1):
                        turn_probs(t - 1, 0)
                        turn_probs(t - 1, 1)
                        values(t - 1, 0)
                        turn_probs(t - 1, 2)
                    if live(t):
                        scores(t, 1)
                    if live(t - 1):
                        values(t - 1, 1)
                        turn_probs(t - 1, 3)
                    if live(t + 1):
                        turn_qk(t + 1)
                    if live(t - 1):
                        values(t - 1, 2)
                        values(t - 1, 3)
                pe.wait_ge(s.f_y, n0 + PAIR)
                for z in range(2):
                    for j in range(NT):
                        o = ps[:, z, 64 * j:64 * j + 64]
                        last = mm(o, C("shift"), Y[:, NT * z + j, 64:128], start=True, stop=j == 0)
                        if j:
                            last = mm(o, C("carry"), Y[:, NT * z + j - 1, 64:128], start=False, stop=True)
                    last.then_inc(s.f_sh, 1)
                for z in range(2):
                    pe.wait_ge(s.ln_out, ln + 2 * l + 1 + z)
                    transposes(z, lambda j: f_h[:, NT * z + j, :]).then_inc(s.f_hnT_ps, 1)
                for z in range(2):
                    pe.wait_ge(s.f_hnT_in, 2 * k + z + 1)
                    for c, m in enumerate(HID_C):
                        if z:
                            pe.wait_ge(s.f_mid, 6 * k + c + 1)
                        for a in range(2):
                            at = 2 * HID * l + HID * (1 - a) + 128 * c
                            last = mm(ps[0:m, 2 + 2 * c + a, :], W("f_w1", at, at + m), f_hnT[:, z, :],
                                      start=True, stop=True)
                        last.then_inc(s.f_up, 1)
                for z in range(2):
                    pe.wait_ge(s.f_mid, 6 * k + 3 * z + 3)
                    for j in range(NT):
                        for c, m in enumerate(HID_C):
                            at = 384 * l + 128 * c
                            last = mm(ps[:, z, j * P:(j + 1) * P], f_hm[0:m, z, c, j * P:(j + 1) * P],
                                      W("f_w2", at, at + 128)[0:m, :], start=c == 0, stop=c == 2)
                    last.then_inc(s.f_down, 1)

            def small_heads():
                def finish(t, i):
                    if 1 <= i <= 4:
                        r = i - 1
                        pe.wait_ge(s.b_o_in, 4 * t + i)
                        if r >= 2:
                            pe.wait_ge(s.b_div, 4 * t + r - 1)
                        transposes(4 + r % 2, lambda j: b_oR[:, r, j * P:(j + 1) * P]).then_inc(s.b_rT, 1)
                    elif i == 5:
                        pe.wait_ge(s.b_div, 4 * t + 4)
                        transposes(4, lambda j: b_os[:, j].rearrange("p g r d -> p (g r d)")).then_inc(s.b_oT_ps, 1)
                    elif i == 6:
                        pe.wait_ge(s.b_oT_in, t + 1)
                        for j in range(NT):
                            last = mm(ps[:, 5, j * P:(j + 1) * P], b_oT[:, j * P:(j + 1) * P],
                                      W("b_gwo" if t < 2 else "b_lwo"), start=True, stop=True)
                        last.then_inc(s.b_out, 1)

                def prepare(k, i):
                    glob = k < 2
                    if i == 8:
                        pe.wait_ge(s.b_hn_in, k + 1)
                        transposes(4, lambda j: b_hn[:, j, :]).then_inc(s.b_xT_ps, 1)
                    elif i == 9 and glob:
                        pe.wait_ge(s.b_hT, k + 1)
                        mm(ps[0:32, 5, :], W("b_down"), xT[:, :], start=True, stop=True).then_inc(s.b_lat_ps, 1)
                    elif i == 10:
                        pe.wait_ge(s.b_hT, k + 1)
                        if glob:
                            pe.wait_ge(s.b_lat_in, k + 1)
                        for j in range(NT):
                            t = slice(j * P, (j + 1) * P)
                            if glob:
                                mm(ps[:, 5, 64 * j:64 * j + 64], b_latT[0:32, t], W("b_up")[0:32, :],
                                   start=True, stop=True)
                            else:
                                mm(ps[:, 5, 64 * j:64 * j + 64], xT[:, t], W("b_lkv"), start=True, stop=True)
                            last = mm(ps[:, 4, t], xT[:, t], W("b_gq" if glob else "b_lq"), start=True, stop=True)
                        last.then_inc(s.b_kvq, 1)
                    elif i == 14:
                        pe.wait_ge(s.b_rope, k + 1)
                        transposes(4, lambda j: b_qr[:, j, 0:HB, :].rearrange("p h d -> p (h d)"))
                        transposes(5, lambda j: b_kr[:, j].rearrange("p g r d -> p (g r d)")).then_inc(s.b_tps, 1)

                def scores(k, u, j):
                    st = 32 * k + 4 * u + j
                    if 4 * u + j == 0:
                        pe.wait_ge(s.b_qT_in, k + 1)
                        pe.wait_ge(s.b_kT_in, k + 1)
                    if st >= 2:
                        pe.wait_ge(s.b_exp, st - 1)
                    n = small_width(k < 2, j)
                    r, gp = u // 2, u % 2
                    for hh in range(2):
                        g = 2 * gp + hh
                        rows = slice(32 * g, 32 * g + 32)
                        last = mm(ps[:, 2 * (st % 2) + hh, 0:n], b_kT[rows, k % 2, r, j * P:(j + 1) * P],
                                  b_qT[rows, k % 2, j * P:j * P + n], start=True, stop=True)
                    last.then_inc(s.b_s, 1)

                def values(k, u, hh):
                    U, glob = 8 * k + u, k < 2
                    r, gp = u // 2, u % 2
                    pe.wait_ge(s.b_mask_p, 2 * U + 2)
                    pe.wait_ge(s.b_mask_v, 2 * U + 2)
                    first = gp == 0 and hh == 0
                    if first and U >= 4:
                        pe.wait_ge(s.b_o_in, U // 2 - 1)
                    g = 2 * gp + hh
                    for j in range(NT):
                        n, at = small_width(glob, j), small_at(glob, j)
                        last = mm(ps[:, 6 + r % 2, j * P:j * P + n],
                                  b_vx[:, k % 2, j, P * g:P * g + P], b_p[:, u % 2, hh, at:at + n],
                                  start=first and j == 0, stop=True, skip_group_check=True)
                    if hh:
                        last.then_inc(s.b_pv, 1)

                for i in range(16):
                    prepare(0, i)
                for U in range(33):
                    k, u = U // 8, U % 8
                    for half in range(2):
                        if U < 32:
                            scores(k, u, 2 * half)
                            scores(k, u, 2 * half + 1)
                        if U:
                            values((U - 1) // 8, (U - 1) % 8, half)
                        if U < 32:
                            if k >= 1:
                                finish(k - 1, 2 * u + half)
                            if k < 3:
                                prepare(k + 1, 2 * u + half)
                for i in range(16):
                    finish(3, i)

            def head_attention(ln):
                pe.wait_ge(s.ln_out, ln)
                for z in range(2):
                    transposes(0, lambda j: Y[:, NT * z + j, :]).then_inc(s.c_xT_ps, 1)
                    pe.wait_ge(s.c_xT, z + 1)
                    if z:
                        pe.wait_ge(s.c_qkv_in, z)
                    for j in range(NT):
                        last = mm(ps[:, 1 + j, 0:384], xT[:, j * P:(j + 1) * P], W("c_qkv"), start=True, stop=True)
                    last.then_inc(s.c_proj, 1)
                for z in range(2):
                    pe.wait_ge(s.c_os_in, z + 1)
                    transposes(0, lambda j: c_os[:, (NT * z + j) * P:(NT * z + j + 1) * P]).then_inc(s.c_oT_ps, 1)
                    pe.wait_ge(s.c_oT_in, z + 1)
                    for j in range(NT):
                        last = mm(ps[:, 5 + z, j * P:(j + 1) * P], c_oT[:, j * P:(j + 1) * P], W("c_fc"),
                                  start=True, stop=True)
                    last.then_inc(s.c_out, 1)

            def full_attention(ln):
                pe.wait_ge(s.ln_out, ln)
                transposes(0, lambda j: Y[:, j, :]).then_inc(s.m_xT_ps, 1)
                pe.wait_ge(s.m_xT, 1)
                for j in range(NT):
                    for c in range(3):
                        last = mm(ps[:, 1 + c, j * P:(j + 1) * P], xT[:, j * P:(j + 1) * P],
                                  W("d_qkv", 128 * c, 128 * c + 128), start=True, stop=True)
                last.then_inc(s.m_proj, 1)
                pe.wait_ge(s.m_qk_in, 1)
                transposes(4, lambda j: m_qk[:, j, 0:128])
                transposes(5, lambda j: m_qk[:, j, 128:256]).then_inc(s.m_tps, 1)
                pe.wait_ge(s.m_qv_in, 1)
                pe.wait_ge(s.m_kT_in, 1)
                steps, dv = full_steps(), DF

                def scores(st):
                    if st >= 2:
                        pe.wait_ge(s.m_exp, st - 1)
                    i, hs = steps[st]
                    for hh, (h, rows) in enumerate(hs):
                        last = mm(ps[:, 2 * (st % 2) + hh, :], m_qT[rows, i * P:(i + 1) * P], m_kT[rows, :],
                                  start=True, stop=True)
                    last.then_inc(s.m_s, 1)

                def turn(st):
                    pe.wait_ge(s.m_exp, st + 1)
                    if st:
                        pe.wait_ge(s.m_pT_a, st)
                        pe.wait_ge(s.m_pT_b, st)
                    for hh in range(2):
                        for j in range(NT):
                            last = tr(ps[:, 4 + hh, j * P:(j + 1) * P], m_p[:, st % 2, hh, j * P:(j + 1) * P], ident)
                    last.then_inc(s.m_tp, 1)

                def values(st):
                    pe.wait_ge(s.m_pT_a, st + 1)
                    pe.wait_ge(s.m_pT_b, st + 1)
                    i, hs = steps[st]
                    for hh, (h, _) in enumerate(hs):
                        for j in range(NT):
                            last = mm(ps[:, 6, i * P + h * dv:i * P + (h + 1) * dv], m_pT[:, hh, j, :],
                                      m_v[:, j, h * dv:(h + 1) * dv], start=j == 0, stop=j == NT - 1)
                    last.then_inc(s.m_pv, 1)

                scores(0)
                scores(1)
                for st in range(len(steps)):
                    turn(st)
                    if st + 2 < len(steps):
                        scores(st + 2)
                    values(st)
                pe.wait_ge(s.m_os_in, 1)
                transposes(0, lambda j: m_os[:, j * P:(j + 1) * P]).then_inc(s.m_oT_ps, 1)
                pe.wait_ge(s.m_oT_in, 1)
                for j in range(NT):
                    last = mm(ps[:, 1, j * P:(j + 1) * P], m_oT[:, j * P:(j + 1) * P], W("d_wo"), start=True, stop=True)
                last.then_inc(s.m_out, 1)

            def experts(k):
                def all_turned(src, ps_sem, in_sem, base):
                    for c in range(NB):
                        if c >= 2:
                            pe.wait_ge(in_sem, base + c - 1)
                        transposes(c % 2, lambda j: src[:, NT * c + j, :]).then_inc(ps_sem, 1)

                pe.wait_ge(es.e_ln, k + 1)
                all_turned(e_xl, es.e_xT_ps, es.e_xT_in, NB * k)
                pe.wait_ge(es.e_xT_in, NB * (k + 1))
                for i in range(TT):
                    last = mm(ps[:, 2, E * i:E * i + E], e_xT[:, i * P:(i + 1) * P], W("e_ws"), start=True, stop=True)
                last.then_inc(es.e_lg_ps, 1)
                pe.wait_ge(es.e_probs, k + 1)
                oh = e_oh.rearrange("p i e -> p (i e)")
                mm(ps[:, 3, 0:128], C("before"), oh, start=True, stop=True)
                mm(ps[:, 3, 128:256], C("ones"), oh, start=True, stop=True).then_inc(es.e_rank_ps, 1)
                all_turned(e_xl, es.e_xsT_ps, es.e_xsT_in, NB * k)
                for c in range(NB):
                    for j in range(NT):
                        last = tr(ps[0:E, 4 + c, j * P:(j + 1) * P], e_oh[:, NT * c + j, :], ident)
                last.then_inc(es.e_oT_ps, 1)
                pe.wait_ge(es.e_oT_in, k + 1)
                for c in range(NB):
                    for j in range(NT):
                        i = NT * c + j
                        last = mm(ps[:, 4 + c, j * P:(j + 1) * P], e_ohT[0:E, i * P:(i + 1) * P],
                                  W("e_b2")[0:E, :], start=True, stop=True)
                last.then_inc(es.e_b2_ps, 1)
                pe.wait_ge(es.e_b2_in, k + 1)
                pe.wait_ge(es.e_xsT_in, NB * (k + 1))
                n = E * NB

                def up(q):
                    e, c = q % E, q // E
                    if q >= 2:
                        pe.wait_ge(es.e_relu, n * k + q - 1)
                    mm(ps[:, 4 + q % 2, :], W("e_w1", 128 * e, 128 * e + 128), e_xT[:, c * 512:(c + 1) * 512],
                       start=True, stop=True).then_inc(es.e_up, 1)

                def down(q):
                    e = q % E
                    pe.wait_ge(es.e_relu, n * k + q + 1)
                    if q >= 2:
                        pe.wait_ge(es.e_acc_in, n * k + q - 1)
                    for j in range(NT):
                        last = mm(ps[:, 6 + q % 2, j * P:(j + 1) * P], e_h[:, q % 2, j * P:(j + 1) * P],
                                  W("e_w2", 128 * e, 128 * e + 128), start=True, stop=True)
                    last.then_inc(es.e_down, 1)

                for q in range(n + 1):
                    if q < n:
                        up(q)
                    if q:
                        down(q - 1)

            def stages(which):
                ln = f = 0
                for i, st in enumerate(which):
                    if st == "a":
                        ln += 1
                        linear_attention(ln)
                    elif st == "f":
                        for l in range(2):
                            window_layer(f, l, ln + 1)
                            f += 1
                        ln += 5
                    elif st == "b":
                        small_heads()
                    elif st == "c":
                        ln += 1
                        head_attention(ln)
                    else:
                        ln += 2
                        full_attention(ln)
                    stage_done(pe, i + 1)

            pe.wait_ge(s_loaded, 64)
            with pe.Fori(0, NB) as b:
                pe.wait_ge(batch_go, b + 1)
                pe.sem_inc(batch_seen, 1)
                stages(["a"])
                pe.drain().then_inc(batch_done, 1)
            if STAGES >= 2:
                pe.wait_ge(s_rest, 16)
                with pe.Fori(0, NP) as b:
                    pe.wait_ge(batch_go, b + NB + 1)
                    pe.sem_inc(batch_seen, 1)
                    stages(in_loop)
                    pe.drain().then_inc(batch_done, 1)
            if STAGES >= 6:
                pe.wait_ge(batch_go, NB + NP + 1)
                pe.sem_inc(batch_seen, 1)
                experts(0)
            if STAGES >= 7:
                with pe.Fori(0, NB) as b:
                    pe.wait_ge(batch_go, b + NB + NP + 2)
                    pe.sem_inc(batch_seen, 1)
                    stages(["d"])
                    pe.drain().then_inc(batch_done, 1)
            if STAGES >= 8:
                pe.wait_ge(batch_go, 2 * NB + NP + 2)
                pe.sem_inc(batch_seen, 1)
                experts(1)

        @block.scalar
        def _(act):
            steps_done = Count()
            after = chain(act, s.act_step, steps_done)
            copy = lambda o, i: act.activation(o, i, ACT.Copy)

            def linear_attention():
                act.wait_ge(s.a_xT_ps, 1)
                copy(xT[:, :], ps[:, 0, :]).then_inc(s.a_xT, 1)

                def squares(j):
                    for half in range(2):
                        act.wait_ge(s.a_proj, 2 * j + half + 1)
                        b = 2 - 2 * half
                        act.activation(a_sqr[:, 512 * b:512 * b + 1024].rearrange("p (b n) -> p b n", b=2),
                                       ps[:, b:b + 2, :], ACT.Square).then_inc(s.a_sq, 1)

                def keep_values(j):
                    act.wait_ge(s.a_vproj, j + 1)
                    copy(a_v[:, j, :].rearrange("p (b n) -> p b n", b=2), ps[:, 4:6, :]).then_inc(s.a_vcopy, 1)

                act.wait_ge(s.a_gate_in, 1)
                after(act.activation(a_gate[:, :], a_gate[:, :], ACT.Exp, scale=-1.0))
                act.activation(a_gate[:, :], a_gate[:, :], ACT.Ln, bias=1.0).then_inc(s.a_decay, 1)
                squares(0)
                keep_values(0)
                for j in range(NT):
                    if j + 1 < NT:
                        squares(j + 1)
                    for g in range(2):
                        T = 4 * j + g
                        act.wait_ge(s.a_tps, T + 1)
                        if T:
                            act.wait_ge(s.a_tcopy, T)
                        copy(a_qT[:, 4 * g:4 * g + 4, j * P:(j + 1) * P],
                             ps[:, 6 + T % 2, :].rearrange("p (h t) -> p h t", h=4)).then_inc(s.a_tcopy, 1)
                    if j + 1 < NT:
                        keep_values(j + 1)
                act.wait_ge(s.a_gsum, 1)
                act.activation(a_gam[:, :, :, :],
                               ps[:, 0, 0:64].rearrange("p (z j h) -> p z j h", z=2, j=NT), ACT.Exp, scale=-1.0)\
                    .then_inc(s.a_gamma, 1)
                for i in range(HA + 1):
                    if i:
                        h = i - 1
                        act.wait_ge(s.a_pT_ps, h + 1)
                        if h:
                            act.wait_ge(s.a_y_ps, h)
                        copy(a_pT[:, :, :], ps[:, 6, :].rearrange("p (j t) -> p j t", j=NT)).then_inc(s.a_pT_in, 1)
                    if i < HA:
                        act.wait_ge(s.a_max, i + 1)
                        for j in range(NT):
                            c = 4 * (i % 2) + j
                            last = act.activation(a_p[:, i % 2, j, :], a_sc[:, i % 2, j, :], ACT.Exp,
                                                  bias=nma[:, c:c + 1], scale=float(P) ** -0.5,
                                                  accum_out=rsa[:, c:c + 1])
                        last.then_inc(s.a_exp, 1)
                    if i:
                        act.wait_ge(s.a_y_ps, h + 1)
                        copy(a_yT[:, h, :], ps[:, 7, :]).then_inc(s.a_yT_in, 1)

            def window_layer(k, l):
                n0 = PAIR * k

                def squares(n):
                    N = n0 + n
                    act.wait_ge(s.f_proj, N + 1)
                    if N:
                        act.wait_ge(s.f_rq, N)
                    act.activation(f_sqr.rearrange("p (b n) -> p b n", b=2), ps[:, 0:2, :], ACT.Square)\
                        .then_inc(s.f_sq, 1)

                def keep_values(n):
                    act.wait_ge(s.f_proj, n0 + n + 1)
                    copy(f_v[:, NT * (n % 2) + n // 2, :], ps[:, 2, :]).then_inc(s.f_vcopy, 1)

                def keep_qk(n):
                    N, z, j = n0 + n, n % 2, n // 2
                    act.wait_ge(s.f_q_ps, N + 1)
                    if N:
                        act.wait_ge(s.f_sc_ps, 2 * N)
                    copy(f_qT, ps[:, 0, :].rearrange("p (c t) -> p c t", c=4)).then_inc(s.f_q_in, 1)
                    act.wait_ge(s.f_k_ps, N + 1)
                    copy(f_kT[:, z, :, j * P:(j + 1) * P], ps[:, 1, :].rearrange("p (c t) -> p c t", c=4))\
                        .then_inc(s.f_k_in, 1)

                def keep_out(n):
                    N = n0 + n
                    act.wait_ge(s.f_oT_ps, N + 1)
                    if N:
                        act.wait_ge(s.f_attn, N)
                    copy(f_oT, ps[:, 7, :].rearrange("p (c t) -> p c t", c=4)).then_inc(s.f_oT_in, 1)

                def exps(n, g):
                    N = n0 + n
                    lo = 0 if n // 2 else WIN
                    act.wait_ge(s.f_max, 2 * N + g + 1)
                    if N >= 2:
                        act.wait_ge(s.f_pT_ps, 4 * N - 6 + 2 * g)
                    for i in range(4):
                        h = 4 * g + i
                        last = act.activation(f_p[:, n % 2, h, 64 + lo:256], f_sc[:, h, lo:KW], ACT.Exp,
                                              bias=f_nm[:, h:h + 1], accum_out=f_rs[:, n % 2, h:h + 1])
                    last.then_inc(s.f_exp, 1)

                def keep_probs(n, p):
                    N = n0 + n
                    act.wait_ge(s.f_pT_ps, 4 * N + p + 1)
                    if N:
                        act.wait_ge(s.f_o_ps, 4 * N + p - 3)
                    side = 0 if n // 2 else 1
                    copy(f_pT[:, 2 * p:2 * p + 2, side:2, :],
                         ps[:, 6 + p % 2, :].rearrange("p (h s t) -> p h s t", h=2, s=2)[:, :, side:2, :])\
                        .then_inc(s.f_pT_in, 1)

                for t in range(-1, PAIR + 2):
                    if live(t + 1):
                        squares(t + 1)
                    if live(t - 2):
                        keep_out(t - 2)
                    if live(t - 1):
                        keep_probs(t - 1, 0)
                        keep_probs(t - 1, 1)
                    if live(t + 1):
                        keep_values(t + 1)
                    if live(t):
                        exps(t, 0)
                    if live(t - 1):
                        keep_probs(t - 1, 2)
                        keep_probs(t - 1, 3)
                    if live(t + 1):
                        keep_qk(t + 1)
                    if live(t):
                        exps(t, 1)
                for z in range(2):
                    act.wait_ge(s.f_sh, 2 * k + z + 1)
                    t = slice(NT * z, NT * z + NT)
                    copy(f_h[:, t, 0:64], Y[:, t, 0:64])
                    copy(f_h[:, t, 64:128], ps[:, z, 0:256].rearrange("p (j d) -> p j d", j=NT)).then_inc(s.f_h_in, 1)
                for z in range(2):
                    act.wait_ge(s.f_hnT_ps, 2 * k + z + 1)
                    act.activation(f_hnT[:, z, :], ps[:, z, :], ACT.Identity, scale=W("f_cols", 8 * l, 8 * l + 1),
                                   bias=W("f_cols", 8 * l + 1, 8 * l + 2)).then_inc(s.f_hnT_in, 1)
                for z in range(2):
                    for c, m in enumerate(HID_C):
                        act.wait_ge(s.f_up, 6 * k + 3 * z + c + 1)
                        bias = W("f_cols", 8 * l + 2 + c, 8 * l + 3 + c)
                        act.activation(f_gb[0:m, c, :], ps[0:m, 2 + 2 * c, :], ACT.Gelu, bias=bias[0:m, :])\
                            .then_inc(s.f_gelu, 1)

            def small_heads():
                def finish(t, i):
                    if i == 5:
                        act.wait_ge(s.b_oT_ps, t + 1)
                        copy(b_oT, ps[:, 4, :]).then_inc(s.b_oT_in, 1)

                def inverse_root(n, k):
                    act.wait_ge(s.b_ms, k)
                    after(act.activation(rstd[:, 0:n], rstd[:, 0:n], ACT.Ln))
                    act.activation(rstd[:, 0:n], rstd[:, 0:n], ACT.Exp, scale=-0.5).then_inc(s.b_rn, 1)

                def prepare(k, i):
                    glob = k < 2
                    if i == 7:
                        inverse_root(NT, 2 * k + 1)
                    elif i == 8:
                        act.wait_ge(s.b_xT_ps, k + 1)
                        act.activation(xT[:, :], ps[:, 4, :], ACT.Copy, scale=W("b_norm", 1 - glob, 2 - glob))\
                            .then_inc(s.b_hT, 1)
                    elif i == 9 and glob:
                        act.wait_ge(s.b_lat_ps, k + 1)
                        copy(b_latT[0:32, :], ps[0:32, 5, :]).then_inc(s.b_lat_in, 1)
                    elif i == 10:
                        act.wait_ge(s.b_kvq, k + 1)
                        act.wait_ge(s.b_zero, 1)
                        kv = ps[:, 5, 0:256].rearrange("p (j n) -> p j n", j=NT)
                        copy(b_qk[:, :, 0:HB, :], ps[:, 4, :].rearrange("p (j h d) -> p j h d", j=NT, h=HB))
                        copy(b_qk[:, :, HB:20, :], kv[:, :, 0:32].rearrange("p j (h d) -> p j h d", h=NG))
                        copy(b_vx[:, k % 2].rearrange("p j (g n) -> p j g n", g=NG)[:, :, :, 0:HD],
                             kv[:, :, 32:64].rearrange("p j (h d) -> p j h d", h=NG)).then_inc(s.b_qk_in, 1)
                    elif i == 12:
                        inverse_root(80, 2 * k + 2)
                    elif i == 14:
                        act.wait_ge(s.b_tps, k + 1)
                        copy(b_qT[:, k % 2], ps[:, 4, :]).then_inc(s.b_qT_in, 1)

                for i in range(16):
                    prepare(0, i)
                for U in range(32):
                    k, u = U // 8, U % 8
                    if U >= 2:
                        act.wait_ge(s.b_pv, U - 1)
                    for j in range(NT):
                        st = 4 * U + j
                        act.wait_ge(s.b_s, st + 1)
                        n, at, b = small_width(k < 2, j), small_at(k < 2, j), 2 * (st % 2)
                        act.activation(b_p[:, u % 2, :, at:at + n], ps[:, b:b + 2, 0:n], ACT.Exp,
                                       scale=float(HD) ** -0.5).then_inc(s.b_exp, 1)
                        if j % 2:
                            if k >= 1:
                                finish(k - 1, 2 * u + j // 2)
                            if k < 3:
                                prepare(k + 1, 2 * u + j // 2)
                for i in range(16):
                    finish(3, i)

            def head_attention():
                for z in range(2):
                    act.wait_ge(s.c_xT_ps, z + 1)
                    copy(xT[:, :], ps[:, 0, :]).then_inc(s.c_xT, 1)
                    act.wait_ge(s.c_proj, z + 1)
                    copy(c_qkv[:, NT * z:NT * z + NT, :], ps[:, 1:1 + NT, 0:384]).then_inc(s.c_qkv_in, 1)
                for u in range(PAIR):
                    act.wait_ge(s.c_shift, u + 1)
                    if u >= 2:
                        act.wait_ge(s.c_prod, u - 1)
                    act.activation(c_e[:, u % 2], c_sc[:, u % 2], ACT.Exp, scale=float(HD) ** -0.5)\
                        .then_inc(s.c_exp, 1)
                for z in range(2):
                    act.wait_ge(s.c_oT_ps, z + 1)
                    copy(c_oT, ps[:, 0, :]).then_inc(s.c_oT_in, 1)

            def full_attention():
                act.wait_ge(s.m_xT_ps, 1)
                act.activation(xT[:, :], ps[:, 0, :], ACT.Identity, scale=W("d_cols", 0, 1),
                               bias=W("d_cols", 1, 2)).then_inc(s.m_xT, 1)
                act.wait_ge(s.m_proj, 1)
                act.activation(m_sq.rearrange("p (b n) -> p b n", b=2), ps[:, 1:3, :], ACT.Square)\
                    .then_inc(s.m_sq, 1)
                copy(m_v, ps[:, 3, :].rearrange("p (j n) -> p j n", j=NT))
                act.wait_ge(s.m_tps, 1)
                act.activation(m_qT, ps[:, 4, :], ACT.Copy, scale=W("d_cols", 2, 3)).then_inc(s.m_qv_in, 1)
                steps, heads = full_steps(), 2
                scale = float(DF) ** -0.5

                def exps(st):
                    i, hs = steps[st]
                    act.wait_ge(s.m_max, st + 1)
                    if st >= 2:
                        act.wait_ge(s.m_tp, st - 1)
                    for hh, (h, _) in enumerate(hs):
                        c = 2 * (st % 2) + hh
                        last = act.activation(m_p[:, st % 2, hh, :], ps[:, 2 * (st % 2) + hh, :], ACT.Exp,
                                              bias=nma[:, c:c + 1], scale=scale,
                                              accum_out=m_rs[:, i * heads + h:i * heads + h + 1])
                    last.then_inc(s.m_exp, 1)

                exps(0)
                exps(1)
                for st in range(len(steps)):
                    act.wait_ge(s.m_tp, st + 1)
                    if st:
                        act.wait_ge(s.m_pv, st)
                    copy(m_pT[:, 0], ps[:, 4, :].rearrange("p (j t) -> p j t", j=NT)).then_inc(s.m_pT_a, 1)
                    if st + 2 < len(steps):
                        exps(st + 2)
                act.wait_ge(s.m_oT_ps, 1)
                copy(m_oT, ps[:, 0, :]).then_inc(s.m_oT_in, 1)

            def experts(k):
                for c in range(NB):
                    act.wait_ge(es.e_xT_ps, NB * k + c + 1)
                    copy(e_xT[:, c * 512:(c + 1) * 512], ps[:, c % 2, :]).then_inc(es.e_xT_in, 1)
                act.wait_ge(es.e_shift, k + 1)
                act.activation(e_ex, e_lg, ACT.Exp).then_inc(es.e_expd, 1)
                for c in range(NB):
                    act.wait_ge(es.e_xsT_ps, NB * k + c + 1)
                    copy(e_xT[:, c * 512:(c + 1) * 512], ps[:, c % 2, :]).then_inc(es.e_xsT_in, 1)
                act.wait_ge(es.e_oT_ps, k + 1)
                copy(e_ohT[0:E, :].rearrange("p (b n) -> p b n", b=4), ps[0:E, 4:8, :]).then_inc(es.e_oT_in, 1)
                act.wait_ge(es.e_b2_ps, k + 1)
                copy(e_acc.rearrange("p i d -> p (i d)").rearrange("p (b n) -> p b n", b=4), ps[:, 4:8, :])\
                    .then_inc(es.e_b2_in, 1)
                n = E * NB
                for q in range(n):
                    e = q % E
                    act.wait_ge(es.e_up, n * k + q + 1)
                    if q >= 2:
                        act.wait_ge(es.e_down, n * k + q - 1)
                    act.activation(e_h[:, q % 2, :], ps[:, 4 + q % 2, :], ACT.Relu, bias=W("e_b1", e, e + 1))\
                        .then_inc(es.e_relu, 1)

            def stages(which):
                f = 0
                for i, st in enumerate(which):
                    if st == "a":
                        linear_attention()
                    elif st == "f":
                        for l in range(2):
                            window_layer(f, l)
                            f += 1
                    elif st == "b":
                        small_heads()
                    elif st == "c":
                        head_attention()
                    else:
                        full_attention()
                    stage_done(act, i + 1)

            act.wait_ge(s_loaded, 64)
            with act.Fori(0, NB) as b:
                act.wait_ge(batch_go, b + 1)
                act.sem_inc(batch_seen, 1)
                steps_done.n = 0
                stages(["a"])
                act.drain().then_inc(batch_done, 1)
            if STAGES >= 2:
                act.wait_ge(s_rest, 16)
                with act.Fori(0, NP) as b:
                    act.wait_ge(batch_go, b + NB + 1)
                    act.sem_inc(batch_seen, 1)
                    steps_done.n = 0
                    stages(in_loop)
                    act.drain().then_inc(batch_done, 1)
            if STAGES >= 6:
                act.wait_ge(batch_go, NB + NP + 1)
                act.sem_inc(batch_seen, 1)
                experts(0)
            if STAGES >= 7:
                with act.Fori(0, NB) as b:
                    act.wait_ge(batch_go, b + NB + NP + 2)
                    act.sem_inc(batch_seen, 1)
                    stages(["d"])
                    act.drain().then_inc(batch_done, 1)
            if STAGES >= 8:
                act.wait_ge(batch_go, 2 * NB + NP + 2)
                act.sem_inc(batch_seen, 1)
                experts(1)

        @block.vector
        def _(dve):
            steps_done, asked = Count(), Count()
            after = chain(dve, s.dve_step, steps_done)
            tt, ts, stt = dve.tensor_tensor, dve.tensor_scalar, dve.scalar_tensor_tensor

            def root(n, ins):
                ins.then_inc(s.pow_in, 1)
                asked.next()

            def rooted():
                dve.wait_ge(s.pow_out, asked.n)

            def layer_norm(src, dst, n, eps):
                for i in range(n):
                    last = dve.bn_stats(stats[:, i, :], src[:, i, :])
                after(last)
                for i in range(n):
                    last = dve.bn_aggr(mv[:, i, :], stats[:, i, :])
                after(last)
                root(n, ts(rstd[:, 0:n], mv[:, 0:n, 1], eps, None, ALU.add))
                rooted()
                for i in range(n):
                    last = ts(dst[:, i, :], src[:, i, :], mv[:, i, 0:1], rstd[:, i:i + 1], ALU.subtract, ALU.mult)
                return last

            def wide(ap, shape, axis):
                return ap.unsqueeze(axis).broadcast_to(shape)

            def linear_attention():
                layer_norm(XB[:, 0:NT, :], Y[:, 0:NT, :], NT, EPS5).then_inc(s.ln_out, 1)
                dve.wait_ge(s.a_gate_ps, 1)
                z = a_gate[:, :].rearrange("p (j h) -> p j h", j=NT)
                after(tt(z, ps[:, 7, 0:32].rearrange("p (j h) -> p j h", j=NT), wide(R("bg"), [P, NT, HA], 1), ALU.add))
                ts(a_gate[:, :], a_gate[:, :], -43.0, None, ALU.max).then_inc(s.a_gate_in, 1)

                def sums(j):
                    for half in range(2):
                        dve.wait_ge(s.a_sq, 2 * j + half + 1)
                        at = 8 - 8 * half
                        r = rstd[:, at:at + 8]
                        after(dve.tensor_reduce(r, a_sqr[:, P * at:P * at + 1024].rearrange("p (h d) -> p h d", h=8),
                                                AX, ALU.add))
                        root(8, ts(r, r, 1.0 / P, EPS6, ALU.mult, ALU.add))

                def normalise(j):
                    view = lambda a: ps[:, a:a + 2, :].rearrange("p b (h d) -> p (b h) d", d=P)
                    dve.wait_ge(s.pow_out, asked.n - 1)
                    tt(a_kn[:, j], view(2), wide(rstd[:, 8:16], [P, HA, P], 2), ALU.mult).then_inc(s.a_norm, 1)
                    rooted()
                    ts(small[:, 4, 0:8], rstd[:, 0:8], R("gain"), None, ALU.mult).then_inc(s.a_gain, 1)
                    dve.wait_ge(s.a_gain, j + 1)
                    if j:
                        dve.wait_ge(s.a_tps, 4 * j - 2)
                    tt(a_qn, view(0), wide(small[:, 4, 0:8], [P, HA, P], 2), ALU.mult).then_inc(s.a_norm, 1)

                def keep_kT(j):
                    for g in (2, 3):
                        T = 4 * j + g
                        dve.wait_ge(s.a_tps, T + 1)
                        dve.wait_ge(s.a_tcopy, T)
                        dve.tensor_copy(a_kT[:, 4 * (g - 2):4 * (g - 2) + 4, j * P:(j + 1) * P],
                                        ps[:, 6 + T % 2, :].rearrange("p (h t) -> p h t", h=4))\
                            .then_inc(s.a_tcopy, 1)

                sums(0)
                normalise(0)
                for j in range(NT):
                    if j + 1 < NT:
                        sums(j + 1)
                        normalise(j + 1)
                    keep_kT(j)
                dve.wait_ge(s.a_gamma, 1)

                def state(h):
                    dve.wait_ge(s.a_kv, h + 1)
                    if h >= 2:
                        dve.wait_ge(s.a_y_ps, h - 1)
                    kv = lambda n: ps[:, 2 * (h % 2) + n % 2, (n // 2) * P:(n // 2 + 1) * P]
                    after(dve.tensor_copy(a_st[:, h % 2, 1, :], kv(0)))
                    for n in range(1, NCH - 1):
                        ins = stt(a_st[:, h % 2, n + 1, :], a_st[:, h % 2, n, :], a_gam[:, n % 2, n // 2, h:h + 1],
                                  kv(n), ALU.mult, ALU.add)
                        if n < NCH - 2:
                            after(ins)
                    ins.then_inc(s.a_state, 1)

                def maxima(h):
                    dve.wait_ge(s.a_scores, h + 1)
                    c = 4 * (h % 2)
                    for j in range(NT):
                        ins = dve.tensor_tensor_reduce(a_sc[:, h % 2, j, :], ps[:, 4 + h % 2, j * P:(j + 1) * P],
                                                       C("mask_a"), 1.0, -3e38, ALU.add, ALU.max,
                                                       mxa[:, c + j:c + j + 1])
                    after(ins)
                    ts(nma[:, c:c + 4], mxa[:, c:c + 4], -float(P) ** -0.5, None, ALU.mult).then_inc(s.a_max, 1)

                def divide(h):
                    dve.wait_ge(s.a_exp, h + 1)
                    c = 4 * (h % 2)
                    after(dve.reciprocal(ria[:, c:c + 4], rsa[:, c:c + 4]))
                    tt(a_p[:, h % 2], a_p[:, h % 2], wide(ria[:, c:c + 4], [P, NT, P], 2), ALU.mult)\
                        .then_inc(s.a_prob, 1)

                for i in range(HA + 1):
                    if i:
                        divide(i - 1)
                    if i < HA:
                        state(i)
                        maxima(i)
                dve.wait_ge(s.a_o, 1)
                after(tt(XB[:, 0:NT, :], XB[:, 0:NT, :], ps[:, 0, :].rearrange("p (j d) -> p j d", j=NT), ALU.add))

            def window_layer(k, l):
                n0 = PAIR * k
                heads = lambda t: t.rearrange("p (h d) -> p h d", h=HF)
                for z in range(2):
                    dve.wait_ge(s.f_yT_ps, 2 * k + z + 1)
                    dve.tensor_copy(f_hT[0:64, z, :], ps[0:64, z, :])
                    dve.tensor_copy(f_hT[64:128, z, 1:S], ps[64:128, z, 0:S - 1]).then_inc(s.f_hT_in, 1)

                def sums(n):
                    N = n0 + n
                    dve.wait_ge(s.f_sq, N + 1)
                    ss = f_ss[:, n % 2, :]
                    after(dve.tensor_reduce(ss, f_sqr.rearrange("p (h d) -> p h d", h=16), AX, ALU.add))
                    ts(ss, ss, 1e-24, None, ALU.max).then_inc(s.f_ss_in, 1)

                def rope_k(n):
                    j = n // 2
                    table = lambda i: wide(tabs[:, l, i, j * DF:(j + 1) * DF], [P, HF, DF], 1)
                    if n0 + n:
                        dve.wait_ge(s.f_rk, n0 + n)
                    tt(heads(f_t3), heads(ps[:, 1, :]), table(2), ALU.mult)
                    tt(heads(f_t4), heads(ps[:, 1, :]), table(3), ALU.mult).then_inc(s.f_rt, 1)

                def rope_q(n):
                    j = n // 2
                    table = lambda i: wide(tabs[:, l, i, j * DF:(j + 1) * DF], [P, HF, DF], 1)
                    if n0 + n:
                        dve.wait_ge(s.f_q_ps, n0 + n)
                    tt(heads(f_t1), heads(ps[:, 0, :]), table(0), ALU.mult)
                    after(tt(heads(f_t2), heads(ps[:, 0, :]), table(1), ALU.mult))
                    tt(heads(f_qr)[:, :, 0:32], heads(f_t1)[:, :, 0:32], heads(f_t2)[:, :, 32:64], ALU.add)
                    tt(heads(f_qr)[:, :, 32:64], heads(f_t1)[:, :, 32:64], heads(f_t2)[:, :, 0:32], ALU.add)\
                        .then_inc(s.f_rq, 1)

                def maxima(n, g):
                    N = n0 + n
                    dve.wait_ge(s.f_sc_ps, 2 * N + g + 1)
                    dve.wait_ge(s.f_root, N + 1)
                    if N:
                        dve.wait_ge(s.f_exp, 2 * N + g - 1)
                    lo = 0 if n // 2 else WIN
                    for i in range(4):
                        h = 4 * g + i
                        at = KW * (i // 2)
                        ins = dve.tensor_tensor_reduce(f_sc[:, h, lo:KW], ps[:, 4 + h % 2, at + lo:at + KW],
                                                       C("mask_f", lo, KW), f_ss[:, n % 2, h:h + 1], -3e38, ALU.add, ALU.max,
                                                       f_mx[:, h:h + 1])
                    after(ins)
                    ts(f_nm[:, 4 * g:4 * g + 4], f_mx[:, 4 * g:4 * g + 4], -1.0, None, ALU.mult).then_inc(s.f_max, 1)

                def add_out(n):
                    i = NT * (n % 2) + n // 2
                    dve.wait_ge(s.f_attn, n0 + n + 1)
                    tt(Y[:, i, :], Y[:, i, :], ps[:, 3, 0:D], ALU.add).then_inc(s.f_y, 1)

                def divide(n):
                    N = n0 + n
                    dve.wait_ge(s.f_exp, 2 * N + 2)
                    after(dve.reciprocal(f_ri, f_rs[:, n % 2, :]))
                    dve.wait_ge(s.f_o_ps, 4 * N + 4)
                    if N:
                        dve.wait_ge(s.f_oT_ps, N)
                    tt(heads(f_os), heads(ps[:, 3, :]), wide(f_ri, [P, HF, DF], 2), ALU.mult).then_inc(s.f_o_in, 1)

                for t in range(-1, PAIR + 2):
                    if live(t + 1):
                        sums(t + 1)
                        rope_k(t + 1)
                    if live(t - 2):
                        add_out(t - 2)
                    if live(t):
                        maxima(t, 0)
                    if live(t + 1):
                        rope_q(t + 1)
                    if live(t):
                        maxima(t, 1)
                    if live(t - 1):
                        divide(t - 1)
                for z in range(2):
                    dve.wait_ge(s.f_h_in, 2 * k + z + 1)
                    h = f_h[:, NT * z:NT * z + NT, :]
                    layer_norm(h, h, NT, EPS5).then_inc(s.ln_out, 1)
                for z in range(2):
                    for c, m in enumerate(HID_C):
                        dve.wait_ge(s.f_gelu, 6 * k + 3 * z + c + 1)
                        bias = W("f_cols", 8 * l + 5 + c, 8 * l + 6 + c)
                        stt(f_hm[0:m, z, c, :], ps[0:m, 3 + 2 * c, :], bias[0:m, :], f_gb[0:m, c, :],
                            ALU.add, ALU.mult).then_inc(s.f_mid, 1)
                for z in range(2):
                    y = Y[:, NT * z:NT * z + NT, :]
                    dve.wait_ge(s.f_down, 2 * k + z + 1)
                    after(tt(y, y, ps[:, z, :].rearrange("p (j d) -> p j d", j=NT), ALU.add))
                    tt(y, y, wide(R("b2", D * l, D * l + D), [P, NT, D], 1), ALU.add).then_inc(s.f_fin, 1)
                dve.wait_ge(s.f_fin, 2 * k + 2)

            def small_heads():
                flat = lambda a: a.rearrange("p j h d -> p (j h) d")
                stream = lambda k: Y[:, NT * (k % 2):NT * (k % 2) + NT, :]

                def keep_sums(k, r):
                    dve.wait_ge(s.b_pv, 8 * k + 2 * r + 2)
                    if k:
                        dve.wait_ge(s.b_rT, 4 * k - 3 + r)
                    dve.tensor_copy(b_oR[:, r, :], ps[:, 6 + r % 2, :]).then_inc(s.b_o_in, 1)

                def finish(t, i):
                    if 1 <= i <= 4:
                        r = i - 1
                        dve.wait_ge(s.b_rT, 4 * t + i)
                        if t and r == 0:
                            dve.wait_ge(s.b_oT_ps, t)
                        o = ps[:, 4 + r % 2, :].rearrange("p (j g n) -> p j g n", j=NT, g=NG)
                        after(dve.reciprocal(b_ri[:, r], o[:, :, :, HD]))
                        tt(b_os[:, :, :, r, :], o[:, :, :, 0:HD], wide(b_ri[:, r], [P, NT, NG, HD], 3), ALU.mult)\
                            .then_inc(s.b_div, 1)
                    elif i == 6:
                        dve.wait_ge(s.b_out, t + 1)
                        after(tt(stream(t), stream(t), ps[:, 5, :].rearrange("p (j d) -> p j d", j=NT), ALU.add))

                def prepare(k, i):
                    y = stream(k)
                    if i == 6:
                        if k:
                            dve.wait_ge(s.b_xT_ps, k)
                        after(tt(b_hn, y, y, ALU.mult))
                        after(dve.tensor_reduce(rstd[:, 0:NT], b_hn, AX, ALU.add))
                        ts(rstd[:, 0:NT], rstd[:, 0:NT], 1.0 / D, EPS6, ALU.mult, ALU.add).then_inc(s.b_ms, 1)
                    elif i == 7:
                        dve.wait_ge(s.b_rn, 2 * k + 1)
                        tt(b_hn, y, wide(rstd[:, 0:NT], [P, NT, D], 2), ALU.mult).then_inc(s.b_hn_in, 1)
                    elif i == 11:
                        dve.wait_ge(s.b_qk_in, k + 1)
                        nm = "g" if k < 2 else "l"
                        cos = wide(C("cos_" + nm).rearrange("p (j d) -> p j d", j=NT), [P, NT, 20, 4], 2)
                        sin = wide(C("sin_" + nm).rearrange("p (j d) -> p j d", j=NT), [P, NT, 20, 4], 2)
                        even, odd = b_qk[:, :, :, 0:HD:2], b_qk[:, :, :, 1:HD:2]
                        tt(b_t[0], even, cos, ALU.mult)
                        tt(b_t[1], odd, sin, ALU.mult)
                        tt(b_t[2], even, sin, ALU.mult)
                        after(tt(b_t[3], odd, cos, ALU.mult))
                        tt(b_qr[:, :, :, 0:HD:2], b_t[0], b_t[1], ALU.subtract)
                        after(tt(b_qr[:, :, :, 1:HD:2], b_t[2], b_t[3], ALU.add))
                        sq = b_sq.rearrange("p (n d) -> p n d", d=HD)
                        after(tt(sq, flat(b_qr), flat(b_qr), ALU.mult))
                        after(dve.tensor_reduce(rstd[:, 0:80], sq, AX, ALU.add))
                        ts(rstd[:, 0:80], rstd[:, 0:80], 1.0 / HD, EPS6, ALU.mult, ALU.add).then_inc(s.b_ms, 1)
                    elif i == 13:
                        dve.wait_ge(s.b_rn, 2 * k + 2)
                        after(tt(flat(b_qr), flat(b_qr), wide(rstd[:, 0:80], [P, 80, HD], 2), ALU.mult))
                        for r in range(NR):
                            ins = dve.tensor_copy(b_kr[:, :, :, r, :], b_qr[:, :, HB:20, :])
                        ins.then_inc(s.b_rope, 1)
                    elif i == 14:
                        dve.wait_ge(s.b_tps, k + 1)
                        for r in range(NR):
                            ins = ts(b_kT[:, k % 2, r, :], ps[:, 5, :], C("rows", r, r + 1), None, ALU.mult)
                        ins.then_inc(s.b_kT_in, 1)

                def mask(U, j):
                    dve.wait_ge(s.b_exp, 4 * U + j + 1)
                    glob = U < 16
                    n, at = small_masked(glob, j), small_at(glob, j)
                    v = b_p[:, U % 2, :, at:at + n]
                    m = C("causal" if glob else "local", 0, n)
                    tt(v, v, m.unsqueeze(1).broadcast_to([P, 2, n]), ALU.mult).then_inc(s.b_mask_v, 1)

                for i in range(16):
                    prepare(0, i)
                for U in range(32):
                    k, u = U // 8, U % 8
                    for half in range(2):
                        mask(U, 2 * half + 1)
                        if half and U and u % 2 == 0:
                            keep_sums((U - 1) // 8, (U - 1) % 8 // 2)
                        if k >= 1:
                            finish(k - 1, 2 * u + half)
                        if k < 3:
                            prepare(k + 1, 2 * u + half)
                keep_sums(3, 3)
                for i in range(16):
                    finish(3, i)

            def head_attention():
                part = lambda u, n: c_qkv[:, u, 128 * n:128 * n + 128].rearrange("p (h d) -> p h d", h=HB)
                full = [P, HB, HB, HD]

                def scores(u):
                    b = u % 2
                    dve.wait_ge(s.c_qkv_in, u // NT + 1)
                    prod = c_prod.rearrange("p (h t d) -> p h t d", h=HB, t=HB)
                    after(tt(prod, part(u, 0).unsqueeze(2).broadcast_to(full),
                             part(u, 1).unsqueeze(1).broadcast_to(full), ALU.mult))
                    if u >= 2:
                        dve.wait_ge(s.c_exp, u - 1)
                    after(dve.tensor_reduce(c_sc[:, b], prod, AX, ALU.add))
                    after(dve.tensor_reduce(mxa[:, :], c_sc[:, b], AX, ALU.max))
                    tt(c_sc[:, b], c_sc[:, b], wide(mxa[:, :], [P, HB, HB], 2), ALU.subtract).then_inc(s.c_shift, 1)

                def weights(u):
                    b = u % 2
                    dve.wait_ge(s.c_exp, u + 1)
                    after(dve.tensor_reduce(rsa[:, :], c_e[:, b], AX, ALU.add))
                    after(dve.reciprocal(ria[:, :], rsa[:, :]))
                    tt(c_e[:, b], c_e[:, b], wide(ria[:, :], [P, HB, HB], 2), ALU.mult).then_inc(s.c_wts, 1)

                def summed(u):
                    dve.wait_ge(s.c_prod, u + 1)
                    after(dve.tensor_reduce(c_os[:, u * P:(u + 1) * P],
                                            c_mix[:, u % 2].rearrange("p (n t) -> p n t", t=HB), AX, ALU.add))
                    dve.sem_inc(s.c_red, 1)
                    if u % NT == NT - 1:
                        dve.sem_inc(s.c_os_in, 1)

                for u in range(PAIR + 2):
                    if u < PAIR:
                        scores(u)
                    if u >= 2:
                        summed(u - 2)
                    if 1 <= u <= PAIR:
                        weights(u - 1)
                for z in range(2):
                    dve.wait_ge(s.c_out, z + 1)
                    xb = XB[:, NT * z:NT * z + NT, :]
                    tt(xb, xb, ps[:, 5 + z, :].rearrange("p (j d) -> p j d", j=NT), ALU.add).then_inc(s.c_sum, 1)
                dve.wait_ge(s.c_sum, 2)

            def full_attention():
                layer_norm(XB[:, 0:NT, :], Y[:, 0:NT, :], NT, EPS5).then_inc(s.ln_out, 1)
                dve.wait_ge(s.ln_out, 1)
                layer_norm(Y[:, 0:NT, :], Y[:, 0:NT, :], NT, EPS5).then_inc(s.ln_out, 1)
                dve.wait_ge(s.m_sq, 1)
                after(dve.tensor_reduce(rstd[:, 0:16], m_sq.rearrange("p (n d) -> p n d", d=DF), AX, ALU.add))
                root(16, ts(rstd[:, 0:16], rstd[:, 0:16], 1.0 / DF, 1e-16, ALU.mult, ALU.max))
                rooted()
                for c in range(2):
                    src = ps[:, 1 + c, :].rearrange("p (j h d) -> p j h d", j=NT, h=2)
                    rn = rstd[:, 8 * c:8 * c + 8].rearrange("p (j h) -> p j h", j=NT)
                    dst = m_qk[:, :, 128 * c:128 * c + 128].rearrange("p j (h d) -> p j h d", h=2)
                    ins = tt(dst, src, wide(rn, [P, NT, 2, DF], 3), ALU.mult)
                ins.then_inc(s.m_qk_in, 1)
                dve.wait_ge(s.m_tps, 1)
                ts(m_kT, ps[:, 5, :], W("d_cols", 3, 4), None, ALU.mult).then_inc(s.m_kT_in, 1)
                steps, heads, dv = full_steps(), 2, DF
                scale = float(DF) ** -0.5

                def maxima(st):
                    dve.wait_ge(s.m_s, st + 1)
                    if st >= 2:
                        dve.wait_ge(s.m_exp, st - 1)
                    b = 2 * (st % 2)
                    after(dve.tensor_reduce(mxa[:, b:b + 2], ps[:, b:b + 2, :], AX, ALU.max))
                    ts(nma[:, b:b + 2], mxa[:, b:b + 2], -scale, None, ALU.mult).then_inc(s.m_max, 1)

                maxima(0)
                maxima(1)
                for st in range(len(steps)):
                    dve.wait_ge(s.m_tp, st + 1)
                    if st:
                        dve.wait_ge(s.m_pv, st)
                    dve.tensor_copy(m_pT[:, 1], ps[:, 5, :].rearrange("p (j t) -> p j t", j=NT))\
                        .then_inc(s.m_pT_b, 1)
                    if st + 2 < len(steps):
                        maxima(st + 2)
                dve.wait_ge(s.m_pv, len(steps))
                n = NT * heads
                after(dve.reciprocal(m_rs[:, 0:n], m_rs[:, 0:n]))
                tt(m_os.rearrange("p (n d) -> p n d", n=n), ps[:, 6, :].rearrange("p (n d) -> p n d", n=n),
                   wide(m_rs[:, 0:n], [P, n, dv], 2), ALU.mult).then_inc(s.m_os_in, 1)
                dve.wait_ge(s.m_out, 1)
                xb = XB[:, 0:NT, :]
                after(tt(xb, xb, ps[:, 1, :].rearrange("p (j d) -> p j d", j=NT), ALU.add))
                after(tt(xb, xb, wide(R("bo"), [P, NT, D], 1), ALU.add))

            def experts(k):
                def step(ins):
                    after(ins)

                def three(ap):
                    return ap.unsqueeze(2).broadcast_to([P, TT, E])

                layer_norm(X, e_xl, TT, EPS5).then_inc(es.e_ln, 1)
                dve.wait_ge(es.e_lg_ps, k + 1)
                step(tt(e_lg, ps[:, 2, 0:128].rearrange("p (i e) -> p i e", i=TT), wide(R("bs"), [P, TT, E], 1), ALU.add))
                step(dve.tensor_reduce(e_m[:, 0], e_lg, AX, ALU.max))
                tt(e_lg, e_lg, three(e_m[:, 0]), ALU.subtract).then_inc(es.e_shift, 1)
                dve.wait_ge(es.e_expd, k + 1)
                step(dve.tensor_reduce(e_m[:, 1], e_ex, AX, ALU.add))
                step(dve.reciprocal(e_m[:, 2], e_m[:, 1]))
                step(tt(e_pr, e_ex, three(e_m[:, 2]), ALU.mult))
                step(dve.tensor_reduce(e_m[:, 3], e_pr, AX, ALU.max))
                step(tt(e_cand, e_pr, three(e_m[:, 3]), ALU.is_equal))
                step(tt(e_cand, e_cand, wide(C("iota8"), [P, TT, E], 1), ALU.mult))
                step(dve.tensor_reduce(e_m[:, 4], e_cand, AX, ALU.min))
                tt(e_oh, wide(C("iota8"), [P, TT, E], 1), three(e_m[:, 4]), ALU.is_equal)
                tt(e_xl, e_xl, e_m[:, 3].unsqueeze(2).broadcast_to([P, TT, D]), ALU.mult).then_inc(es.e_probs, 1)
                dve.wait_ge(es.e_rank_ps, k + 1)
                rank = ps[:, 3, 0:128].rearrange("p (i e) -> p i e", i=TT)
                dve.memset(e_pre[:, 0, :], 0.0)
                dve.memset(e_eo[:, 0:1], 0.0)
                step(dve.tensor_copy(e_tot, ps[:, 3, 128:256].rearrange("p (i e) -> p i e", i=TT)))
                for i in range(TT - 1):
                    step(tt(e_pre[:, i + 1, :], e_pre[:, i, :], e_tot[:, i, :], ALU.add))
                step(tt(e_tot[:, 0, :], e_pre[:, TT - 1, :], e_tot[:, TT - 1, :], ALU.add))
                for e in range(E - 1):
                    step(tt(e_eo[:, e + 1:e + 2], e_eo[:, e:e + 1], e_tot[:, 0, e:e + 1], ALU.add))
                step(tt(e_pos, rank, e_pre, ALU.add))
                step(tt(e_pos, e_pos, wide(e_eo, [P, TT, E], 1), ALU.add))
                step(tt(e_pos, e_pos, e_oh, ALU.mult))
                step(dve.tensor_reduce(e_m[:, 5], e_pos, AX, ALU.add))
                dve.tensor_copy(e_idx[:, :], e_m[:, 5]).then_inc(es.e_idx_in, 1)
                n = E * NB
                dve.wait_ge(es.e_b2_in, k + 1)
                for q in range(n):
                    e, c = q % E, q // E
                    dve.wait_ge(es.e_down, n * k + q + 1)
                    if e:
                        dve.wait_ge(es.e_acc_in, n * k + q)
                    for j in range(NT):
                        i = NT * c + j
                        ins = stt(e_acc[:, i, :], ps[:, 6 + q % 2, j * P:(j + 1) * P], e_oh[:, i, e:e + 1],
                                  e_acc[:, i, :], ALU.mult, ALU.add)
                    ins.then_inc(es.e_acc_in, 1)
                dve.wait_ge(es.e_back_in, 16 * (k + 1))
                tt(X[:, :, :], X[:, :, :], e_back, ALU.add).then_inc(es.e_out, 1)
                dve.wait_ge(es.e_out, k + 1)

            def stages(which):
                f = 0
                for i, st in enumerate(which):
                    if st == "a":
                        linear_attention()
                    elif st == "f":
                        layer_norm(XB, Y, 2 * NT, EPS5).then_inc(s.ln_out, 1)
                        for l in range(2):
                            window_layer(f, l)
                            f += 1
                        after(tt(XB[:, :, :], XB[:, :, :], Y[:, :, :], ALU.add))
                    elif st == "b":
                        after(layer_norm(XB, Y, 2 * NT, EPS5))
                        small_heads()
                        after(tt(XB[:, :, :], XB[:, :, :], Y[:, :, :], ALU.add))
                    elif st == "c":
                        layer_norm(XB, Y, 2 * NT, EPS5).then_inc(s.ln_out, 1)
                        head_attention()
                    else:
                        full_attention()
                    stage_done(dve, i + 1)

            dve.memset(f_hT[64:128, :, 0:1], 0.0)
            dve.drain()
            dve.wait_ge(s_loaded, 64)
            for l in range(2):
                for n, (tab, gain) in enumerate((("cos_q", "qs"), ("sin_q", "qs"), ("cos_k", "ks"), ("sin_k", "ks"))):
                    ins = tt(tabs[:, l, n, :].rearrange("p (j d) -> p j d", j=NT),
                             C(tab).rearrange("p (j d) -> p j d", j=NT),
                             wide(R(gain, DF * l, DF * l + DF), [P, NT, DF], 1), ALU.mult)
            ins.then_inc(s_tabs, 1)
            dve.wait_ge(s_tabs, 1)
            with dve.Fori(0, NB) as b:
                dve.wait_ge(batch_go, b + 1)
                dve.sem_inc(batch_seen, 1)
                steps_done.n = asked.n = 0
                after(ts(XB[:, 0:NT, :], X[:, bass.ds(b * NT, NT), :], 1.0, None, ALU.mult))
                stages(["a"])
                ts(X[:, bass.ds(b * NT, NT), :], XB[:, 0:NT, :], 1.0, None, ALU.mult).then_inc(batch_done, 1)
            if STAGES >= 2:
                dve.wait_ge(s_rest, 16)
                with dve.Fori(0, NP) as b:
                    dve.wait_ge(batch_go, b + NB + 1)
                    dve.sem_inc(batch_seen, 1)
                    steps_done.n = asked.n = 0
                    after(ts(XB[:, :, :], X[:, bass.ds(b * PAIR, PAIR), :], 1.0, None, ALU.mult))
                    stages(in_loop)
                    ts(X[:, bass.ds(b * PAIR, PAIR), :], XB[:, :, :], 1.0, None, ALU.mult).then_inc(batch_done, 1)
            steps_done.n = asked.n = 0
            if STAGES >= 6:
                dve.wait_ge(batch_go, NB + NP + 1)
                dve.sem_inc(batch_seen, 1)
                experts(0)
            if STAGES >= 7:
                dve.drain().then_inc(batch_done, 1)
                with dve.Fori(0, NB) as b:
                    dve.wait_ge(batch_go, b + NB + NP + 2)
                    dve.sem_inc(batch_seen, 1)
                    steps_done.n = asked.n = 0
                    after(ts(XB[:, 0:NT, :], X[:, bass.ds(b * NT, NT), :], 1.0, None, ALU.mult))
                    stages(["d"])
                    ts(X[:, bass.ds(b * NT, NT), :], XB[:, 0:NT, :], 1.0, None, ALU.mult).then_inc(batch_done, 1)
            if STAGES >= 8:
                steps_done.n = asked.n = 0
                dve.wait_ge(batch_go, 2 * NB + NP + 2)
                dve.sem_inc(batch_seen, 1)
                experts(1)
            dve.drain().then_inc(s_tabs, 1)

        @block.gpsimd
        def _(pool):
            asked, steps_done = Count(), Count()
            after = chain(pool, s.pool_step, steps_done)

            def root(n, at=0):
                pool.wait_ge(s.pow_in, asked.next())
                pool.tensor_tensor(rstd[:, at:at + n], rstd[:, at:at + n], C("neghalf", 0, n), ALU.pow)\
                    .then_inc(s.pow_out, 1)

            def window_layer(k):
                heads = lambda t: t.rearrange("p (h d) -> p h d", h=HF)
                for n in range(PAIR):
                    N = PAIR * k + n
                    pool.wait_ge(s.f_ss_in, N + 1)
                    ss = f_ss[:, n % 2, :]
                    after(pool.tensor_tensor(ss[:, 8:16], ss[:, 8:16], C("neghalf", 0, 8), ALU.pow))
                    pool.wait_ge(s.f_rt, N + 1)
                    pool.tensor_tensor(heads(f_kr)[:, :, 0:32], heads(f_t3)[:, :, 0:32],
                                       heads(f_t4)[:, :, 32:64], ALU.add)
                    after(pool.tensor_tensor(heads(f_kr)[:, :, 32:64], heads(f_t3)[:, :, 32:64],
                                             heads(f_t4)[:, :, 0:32], ALU.add))
                    pool.tensor_tensor(heads(f_kr), heads(f_kr),
                                       ss[:, 8:16].unsqueeze(2).broadcast_to([P, HF, DF]), ALU.mult)\
                        .then_inc(s.f_rk, 1)
                    pool.tensor_tensor(ss[:, 0:8], ss[:, 0:8], C("neghalf", 0, 8), ALU.pow).then_inc(s.f_root, 1)

            def stages(which):
                f = 0
                for i, st in enumerate(which):
                    if st == "a":
                        root(NT)
                        for j in range(NT):
                            root(8, 8)
                            root(8, 0)
                    elif st == "f":
                        pool.memset(f_p[:, :, :, 0:256 - KW], 0.0).then_inc(s.f_zero, 1)
                        root(2 * NT)
                        for l in range(2):
                            window_layer(f)
                            f += 1
                            root(NT)
                            root(NT)
                    elif st == "b":
                        root(2 * NT)
                        pool.memset(b_vx, 0.0)
                        pool.drain()
                        pool.memset(b_vx.rearrange("p k j (g n) -> p (k j g) n", g=NG)[:, :, HD:HD + 1], 1.0)\
                            .then_inc(s.b_zero, 1)
                        for U in range(32):
                            glob = U < 16
                            m = C("causal") if glob else C("local")
                            for j in (0, 2):
                                pool.wait_ge(s.b_exp, 4 * U + j + 1)
                                n, at = small_masked(glob, j), small_at(glob, j)
                                v = b_p[:, U % 2, :, at:at + n]
                                pool.tensor_tensor(v, v, m[:, 0:n].unsqueeze(1).broadcast_to([P, 2, n]), ALU.mult)\
                                    .then_inc(s.b_mask_p, 1)
                    elif st == "c":
                        root(2 * NT)
                        for u in range(PAIR):
                            pool.wait_ge(s.c_wts, u + 1)
                            if u >= 2:
                                pool.wait_ge(s.c_red, u - 1)
                            full = [P, HB, HD, HB]
                            vals = c_qkv[:, u, 256:384].rearrange("p (t d) -> p d t", t=HB)
                            pool.tensor_tensor(c_mix[:, u % 2].rearrange("p (h d t) -> p h d t", h=HB, t=HB),
                                               c_e[:, u % 2].unsqueeze(2).broadcast_to(full),
                                               vals.unsqueeze(1).broadcast_to(full), ALU.mult)\
                                .then_inc(s.c_prod, 1)
                    else:
                        root(NT)
                        root(NT)
                        root(16)
                    stage_done(pool, i + 1)

            def experts(k):
                root(TT)
                pool.wait_ge(es.e_idx_in, k + 1)
                for i in range(TT):
                    if i % NT == 0:
                        pool.wait_ge(es.e_acc_in, E * NB * k + E * (i // NT + 1))
                    pool.indirect_dma_start(scratch[:, :], bass.IndirectOffsetOnAxis(ap=e_idx[:, i:i + 1], axis=0),
                                            e_acc[:, i, :], None).then_inc(es.e_sent, 16)

            pool.wait_ge(s_loaded, 64)
            with pool.Fori(0, NB) as b:
                pool.wait_ge(batch_go, b + 1)
                pool.sem_inc(batch_seen, 1)
                asked.n = steps_done.n = 0
                stages(["a"])
                pool.drain().then_inc(batch_done, 1)
            if STAGES >= 2:
                with pool.Fori(0, NP) as b:
                    pool.wait_ge(batch_go, b + NB + 1)
                    pool.sem_inc(batch_seen, 1)
                    asked.n = steps_done.n = 0
                    stages(in_loop)
                    pool.drain().then_inc(batch_done, 1)
            asked.n = 0
            if STAGES >= 6:
                pool.wait_ge(batch_go, NB + NP + 1)
                pool.sem_inc(batch_seen, 1)
                experts(0)
            if STAGES >= 7:
                with pool.Fori(0, NB) as b:
                    pool.wait_ge(batch_go, b + NB + NP + 2)
                    pool.sem_inc(batch_seen, 1)
                    asked.n = 0
                    stages(["d"])
                    pool.drain().then_inc(batch_done, 1)
            if STAGES >= 8:
                asked.n = 0
                pool.wait_ge(batch_go, 2 * NB + NP + 2)
                pool.sem_inc(batch_seen, 1)
                experts(1)

        @block.sync
        def _(sp):
            sp.dma_start(X[:, :, :], x_in.rearrange("b (t p) d -> p (b t) d", p=P)).then_inc(s_loaded, 16)
            sp.dma_start(Ct[:, :], c_in).then_inc(s_loaded, 16)
            sp.dma_start(Rt[:, :], r_in.broadcast_to([P, r_cols])).then_inc(s_loaded, 16)
            first_cols = w_at["f_wqkv"][0]
            sp.dma_start(Wt[:, 0:first_cols], w_in[:, 0:first_cols]).then_inc(s_loaded, 16)
            sp.dma_start(Wt[:, first_cols:], w_in[:, first_cols:]).then_inc(s_rest, 16)

            def clear():
                sp.sem_clear(range(first, first + len(names)))
                sp.sem_clear(batch_done)
                sp.sem_inc(batch_go, 1)

            def back(k):
                sp.wait_ge(es.e_sent, 16 * TT * (k + 1))
                sp.dma_start(e_back, scratch.rearrange("(i p) d -> p i d", p=P)).then_inc(es.e_back_in, 16)

            numbers = sorted(sem_number(sems[n]) for n in names)
            first = numbers[0]
            assert numbers == list(range(first, first + len(names)))
            sp.sem_inc(batch_go, 1)
            with sp.Fori(0, NB) as b:
                sp.wait_ge(batch_done, 4)
                clear()
            if STAGES >= 2:
                with sp.Fori(0, NP) as b:
                    sp.wait_ge(batch_done, 4)
                    clear()
            if STAGES >= 6:
                back(0)
            if STAGES >= 7:
                sp.wait_ge(batch_done, 1)
                clear()
                with sp.Fori(0, NB) as b:
                    sp.wait_ge(batch_done, 4)
                    clear()
            if STAGES >= 8:
                back(1)
            sp.wait_ge(s_tabs, 2)
            sp.dma_start(out.rearrange("b (t p) d -> p (b t) d", p=P), X[:, :, :]).then_inc(s_store, 16)
            sp.wait_ge(s_store, 16)


def live(n):
    return 0 <= n < PAIR


def sem_number(sem):
    return int(sem.num)


def small_width(glob, j):
    return S - j * P if glob else min(P + LW, S - j * P)


def small_masked(glob, j):
    return min(small_width(glob, j), P if glob else P + LW)


def small_at(glob, j):
    return sum(small_width(glob, i) for i in range(j))


def full_steps():
    return [(i, [(h, slice(64 * h, 64 * h + 64)) for h in range(2)]) for i in range(NT)]


def kernel(**inputs):
    import numpy as _np
    import concourse.bacc as _bacc
    from concourse import mybir as _mybir
    from concourse.bass_utils import run_bass_kernel_spmd as _run

    g = {k: _np.asarray(v) for k, v in inputs.items()}
    a = {k[len("L0_attn_a_"):]: v for k, v in g.items() if k.startswith("L0_attn_a_")}
    b = {k[len("L0_attn_b_"):]: v for k, v in g.items() if k.startswith("L0_attn_b_")}
    f = {k[len("L0_ffn_"):]: v for k, v in g.items() if k.startswith("L0_ffn_")}
    c = {k[len("L1_attn_a_"):]: v for k, v in g.items() if k.startswith("L1_attn_a_")}
    d = {k[len("L1_attn_b_"):]: v for k, v in g.items() if k.startswith("L1_attn_b_")}
    e = {k[len("L1_ffn_"):]: v for k, v in g.items() if k.startswith("L1_ffn_")}

    def pad(m):
        out = _np.zeros((P, m.shape[1]), m.dtype)
        out[:m.shape[0]] = m
        return out

    def col(v):
        return pad(v[:, None])

    side = lambda xs: _np.concatenate(xs, 1)
    blocks = {
        "a_qkv": side([a["Wq"].T, a["Wk"].T, a["Wv"].T]),
        "a_wo": a["Wo"].reshape(D, HA, 128).transpose(2, 1, 0).reshape(128, -1),
        "a_wg": a["Wg"].T,
        "f_wqkv": side([f["wqkv"][l] for l in range(2)]),
        "f_wo": side([f["wo"][l][128 * i:128 * i + 128] for l in range(2) for i in range(4)]),
        "f_w1": side([f["w1"][l] for l in range(2)]),
        "f_w2": side([pad(f["w2"][l][128 * i:min(128 * i + 128, HID)]) for l in range(2) for i in range(3)]),
        "f_cols": side([side([col(f["ln_g"][l]), col(f["ln_b"][l])]
                             + [col(f["b1"][l][HID + 128 * i:min(HID + 128 * i + 128, 2 * HID)]) for i in range(3)]
                             + [col(f["b1"][l][128 * i:min(128 * i + 128, HID)]) for i in range(3)]) for l in range(2)]),
        "b_norm": side([col(b["norm1_w"]), col(b["norm2_w"])]),
        "b_gq": b["g_wq"], "b_lq": b["l_wq"], "b_down": b["g_kv_down"],
        "b_up": pad(side([b["g_k_up"], b["g_v_up"]])), "b_lkv": side([b["l_wk"], b["l_wv"]]),
        "b_gwo": b["g_wo"], "b_lwo": b["l_wo"],
        "c_qkv": side([c["Wq"].T, c["Wk"].T, c["Wv"].T]), "c_fc": c["Wfc"].T,
        "d_qkv": side([d["w_q"].T, d["w_k"].T, d["w_v"].T]), "d_wo": d["w_o"].T,
        "d_cols": side([col(d["ln_gamma"]), col(d["ln_beta"]), col(_np.tile(d["q_gamma"], 2)),
                        col(_np.tile(d["k_gamma"], 2))]),
        "e_ws": e["Ws"].T, "e_w1": side([e["W1"][i] for i in range(E)]), "e_w2": side([e["W2"][i] for i in range(E)]),
        "e_b1": e["b1"].T, "e_b2": pad(e["b2"]),
    }
    for name, w in WEIGHTS:
        assert blocks[name].shape == (P, w), (name, blocks[name].shape, w)
    rows = {"bg": a["bg"], "gain": a["qk_gain"].reshape(1), "qs": f["q_scale"].reshape(-1),
            "ks": f["k_scale"].reshape(-1), "b2": f["b2"].reshape(-1), "bo": d["b_o"], "bs": e["bs"]}
    tables = constants()
    c_at, _ = places([(k, v.shape[1]) for k, v in tables.items()])
    arrays = {
        "in_x": _np.ascontiguousarray(a["x"]),
        "in_w": _np.ascontiguousarray(side([blocks[n] for n, _ in WEIGHTS])),
        "in_c": _np.ascontiguousarray(side(list(tables.values()))),
        "in_r": _np.ascontiguousarray(_np.concatenate([rows[n] for n, _ in ROWS])[None, :]),
    }
    nc = _bacc.Bacc("TRN2", target_bir_lowering=False, num_devices=1)
    f32 = _mybir.dt.float32
    args = [nc.dram_tensor(n, v.shape, f32, kind="ExternalInput").ap() for n, v in arrays.items()]
    out = nc.dram_tensor("out_0", (NB, S, D), f32, kind="ExternalOutput").ap()
    scratch = nc.dram_tensor("sorted_rows", (NB * S, D), f32, kind="Internal").ap()
    program(nc, *args, out, scratch, c_at)
    r = _run(nc, [arrays], core_ids=[0])
    return r.results[0]["out_0"]
```
